# Optimizing a Trainium2 kernel written in Bass

```python
import numpy as np
import jax
import jax.numpy as jnp

def _softmax(x, axis=-1):
    return jax.nn.softmax(x, axis=axis)

def _gelu(x):
    return jax.nn.gelu(x, approximate=True)

def _silu(x):
    return jax.nn.silu(x)

def _sigmoid(x):
    return jax.nn.sigmoid(x)

def _layernorm(x, axis=-1, eps=1e-05):
    m = jnp.mean(x, axis=axis, keepdims=True)
    v = jnp.var(x, axis=axis, keepdims=True)
    return (x - m) / jnp.sqrt(v + eps)

def _scatter_add(tgt, idx, src, axis=0):
    return tgt.at[idx].add(src)

def _segment_sum(src, seg, n):
    return jax.ops.segment_sum(src, seg, n)
kernel_name = 'mk_recurrent_d2_jaxref_r8_c9b4d7'

def setup_inputs(seed: int=0):
    np.random.seed(seed)
    _w = jnp.asarray

    def _L0_attn_setup():
        import jax, jax.numpy as jnp
        import numpy as np
        B, N, D = (2, 256, 128)
        H, M = (8, 64)
        DK = D // H
        EPS = 1e-05

        def _gsa(q, k, v, s, g):
            b = q.shape[1]

            def step1(hk, t):
                q_t, k_t, s_t, g_t = t
                hk = hk * jnp.exp(g_t)[:, :, None, :] + k_t[..., :, None] * s_t[..., None, :]
                ok = jnp.einsum('bhk,bhkm->bhm', q_t, hk)
                return (hk, ok)
            hk0 = jnp.zeros((b, H, DK, M), q.dtype)
            _, ok = jax.lax.scan(step1, hk0, (q, k, s, g))
            qv = jax.nn.softmax(ok, axis=-1)

            def step2(hv, t):
                qv_t, s_t, v_t, g_t = t
                hv = hv * jnp.exp(g_t)[..., :, None] + s_t[..., :, None] * v_t[..., None, :]
                ov = jnp.einsum('bhm,bhmv->bhv', qv_t, hv)
                return (hv, ov)
            hv0 = jnp.zeros((b, H, M, DK), q.dtype)
            _, ov = jax.lax.scan(step2, hv0, (qv, s, v, g))
            return ov
        key = jax.random.key(seed)
        ks = jax.random.split(key, 9)
        std = 0.02
        return {'x': jax.random.normal(ks[0], (B, N, D), jnp.float32), 'Wq': jax.random.normal(ks[1], (D, D), jnp.float32) * std, 'Wk': jax.random.normal(ks[2], (D, D), jnp.float32) * std, 'Wv': jax.random.normal(ks[3], (D, D), jnp.float32) * std, 'Wf1': jax.random.normal(ks[4], (D, DK), jnp.float32) * std, 'Wf2': jax.random.normal(ks[5], (DK, H * M), jnp.float32) * std, 'Wg1': jax.random.normal(ks[6], (D, DK), jnp.float32) * std, 'Wg2': jax.random.normal(ks[7], (DK, D), jnp.float32) * std, 'Wo': jax.random.normal(ks[8], (D, D), jnp.float32) * std, 'norm_w': jnp.ones((D,), jnp.float32)}
    _L0_attn_in = _L0_attn_setup()

    def _L0_ffn_setup():
        import jax, jax.numpy as jnp
        import numpy as np
        B, S, D = (2, 64, 128)
        E, K, I = (16, 8, 128)
        I_SH = 128
        ROUTE_SCALE = 2.826
        key = jax.random.key(seed)
        ks = jax.random.split(key, 8)
        s = 0.02
        return {'x': jax.random.normal(ks[0], (B, S, D), dtype=jnp.float32), 'gate_w': jax.random.normal(ks[1], (E, D), dtype=jnp.float32) * s, 'expert_bias': jnp.zeros((E,), dtype=jnp.float32), 'w_gate': jax.random.normal(ks[2], (E, I, D), dtype=jnp.float32) * s, 'w_up': jax.random.normal(ks[3], (E, I, D), dtype=jnp.float32) * s, 'w_down': jax.random.normal(ks[4], (E, D, I), dtype=jnp.float32) * s, 'shared_gate_w': jax.random.normal(ks[5], (I_SH, D), dtype=jnp.float32) * s, 'shared_up_w': jax.random.normal(ks[6], (I_SH, D), dtype=jnp.float32) * s, 'shared_down_w': jax.random.normal(ks[7], (D, I_SH), dtype=jnp.float32) * s}
    _L0_ffn_in = _L0_ffn_setup()

    def _L1_attn_setup():
        import math
        import jax, jax.numpy as jnp
        import numpy as np
        B, T, D, H, L = (8, 256, 128, 16, 4)
        DK = D // H
        EPS_LN = 1e-05
        EPS_ATTN = 1e-06

        def _layernorm(x, scale, bias):
            mu = jnp.mean(x, axis=-1, keepdims=True)
            var = jnp.mean(jnp.square(x - mu), axis=-1, keepdims=True)
            return (x - mu) * jax.lax.rsqrt(var + EPS_LN) * scale + bias

        def _sinusoidal_pos_emb(t, d):
            half = d // 2
            freq = jnp.exp(jnp.arange(half, dtype=jnp.float32) * (-math.log(10000.0) / (half - 1)))
            pos = (jnp.arange(t, dtype=jnp.float32) + 1.0)[:, None] * freq[None, :]
            return jnp.concatenate([jnp.sin(pos), jnp.cos(pos)], axis=-1)

        def _linear_attention(q, k, v):
            qp = jax.nn.elu(q) + 1.0
            kp = jax.nn.elu(k) + 1.0
            kv = jnp.einsum('bshd,bshm->bhmd', kp, v)
            ksum = jnp.sum(kp, axis=1)
            z = 1.0 / (jnp.einsum('blhd,bhd->blh', qp, ksum) + EPS_ATTN)
            return jnp.einsum('blhd,bhmd,blh->blhm', qp, kv, z)

        def _encoder_layer(x, Wq, bq, Wk, bk, Wv, bv, Wo, bo, W1, b1, W2, b2, ln1_s, ln1_b, ln2_s, ln2_b):
            b, t, d = x.shape
            h = _layernorm(x, ln1_s, ln1_b)
            q = (h @ Wq + bq).reshape(b, t, H, DK)
            k = (h @ Wk + bk).reshape(b, t, H, DK)
            v = (h @ Wv + bv).reshape(b, t, H, DK)
            attn = _linear_attention(q, k, v).reshape(b, t, d)
            x = x + (attn @ Wo + bo)
            h = _layernorm(x, ln2_s, ln2_b)
            h = jax.nn.relu(h @ W1 + b1) @ W2 + b2
            return x + h
        key = jax.random.key(seed)
        ks = jax.random.split(key, 8)
        w = lambda k, shape: jax.random.normal(k, shape, dtype=jnp.float32) * 0.02
        return {'x_in': jax.random.normal(ks[0], (B, T, D), dtype=jnp.float32), 'Wq': w(ks[1], (L, D, D)), 'bq': jnp.zeros((L, D), jnp.float32), 'Wk': w(ks[2], (L, D, D)), 'bk': jnp.zeros((L, D), jnp.float32), 'Wv': w(ks[3], (L, D, D)), 'bv': jnp.zeros((L, D), jnp.float32), 'Wo': w(ks[4], (L, D, D)), 'bo': jnp.zeros((L, D), jnp.float32), 'W1': w(ks[5], (L, D, 4 * D)), 'b1': jnp.zeros((L, 4 * D), jnp.float32), 'W2': w(ks[6], (L, 4 * D, D)), 'b2': jnp.zeros((L, D), jnp.float32), 'ln1_s': jnp.ones((L, D), jnp.float32), 'ln1_b': jnp.zeros((L, D), jnp.float32), 'ln2_s': jnp.ones((L, D), jnp.float32), 'ln2_b': jnp.zeros((L, D), jnp.float32), 'lnf_s': jnp.ones((D,), jnp.float32), 'lnf_b': jnp.zeros((D,), jnp.float32)}
    _L1_attn_in = _L1_attn_setup()

    def _L1_ffn_setup():
        import jax, jax.numpy as jnp
        import numpy as np
        DIM = 128
        DEPTH = 2
        HEADS = 8
        DIM_HEAD = 64
        WINDOW = 64
        INNER = HEADS * DIM_HEAD
        HID = int(DIM * 4 * 2 / 3)
        B, N = (2, 1024)
        QK_SCALE = 8.0

        def shift_token(t):
            t1, t2 = jnp.split(t, 2, axis=-1)
            t2 = jnp.pad(t2, ((0, 0), (1, 0), (0, 0)))[:, :-1]
            return jnp.concatenate([t1, t2], axis=-1)

        def l2norm(t):
            return t / jnp.clip(jnp.linalg.norm(t, axis=-1, keepdims=True), 1e-12)

        def rotate_half(x):
            x1, x2 = jnp.split(x, 2, axis=-1)
            return jnp.concatenate([-x2, x1], axis=-1)

        def rotary_xpos(q, k):
            n = q.shape[-2]
            half_idx = jnp.arange(0, DIM_HEAD, 2, dtype=jnp.float32)
            inv_freq = 1.0 / 10000.0 ** (half_idx / DIM_HEAD)
            t = jnp.arange(n, dtype=jnp.float32)
            freqs = t[:, None] * inv_freq[None, :]
            freqs = jnp.concatenate([freqs, freqs], axis=-1)
            base = (half_idx + 0.4 * DIM_HEAD) / (1.4 * DIM_HEAD)
            power = (t - n // 2) / float(WINDOW // 2)
            scale = base[None, :] ** power[:, None]
            scale = jnp.concatenate([scale, scale], axis=-1)
            cos, sin = (jnp.cos(freqs), jnp.sin(freqs))
            q = q * cos * scale + rotate_half(q) * sin * scale
            k = k * cos / scale + rotate_half(k) * sin / scale
            return (q, k)

        def local_attention(q, k, v):
            b, h, n, d = q.shape
            w = n // WINDOW
            bq = q.reshape(b, h, w, WINDOW, d) * QK_SCALE
            bk = k.reshape(b, h, w, WINDOW, d)
            bv = v.reshape(b, h, w, WINDOW, d)

            def look_around(t):
                p = jnp.pad(t, ((0, 0), (0, 0), (1, 0), (0, 0), (0, 0)))
                return jnp.concatenate([p[:, :, :w], p[:, :, 1:]], axis=3)
            bk, bv = (look_around(bk), look_around(bv))
            bt = jnp.arange(n).reshape(w, WINDOW)
            btp = jnp.pad(bt, ((1, 0), (0, 0)), constant_values=-1)
            btk = jnp.concatenate([btp[:w], btp[1:]], axis=1)
            sim = jnp.einsum('bhwid,bhwjd->bhwij', bq, bk)
            i = bt[:, :, None]
            j = btk[:, None, :]
            mask = (i < j) | (i > j + WINDOW) | (j == -1)
            sim = jnp.where(mask, -jnp.finfo(sim.dtype).max, sim)
            attn = jax.nn.softmax(sim, axis=-1)
            out = jnp.einsum('bhwij,bhwjd->bhwid', attn, bv)
            return out.reshape(b, h, n, d)

        def _layer(x, wqkv, qs, ksc, wo, lg, lb, w1, b1, w2, b2):
            b, n, _ = x.shape
            h = shift_token(x)
            qkv = h @ wqkv
            q, k, v = jnp.split(qkv, 3, axis=-1)
            to_heads = lambda t: t.reshape(b, n, HEADS, DIM_HEAD).transpose(0, 2, 1, 3)
            q, k, v = (to_heads(q), to_heads(k), to_heads(v))
            q = l2norm(q) * qs
            k = l2norm(k) * ksc
            q, k = rotary_xpos(q, k)
            o = local_attention(q, k, v)
            o = o.transpose(0, 2, 1, 3).reshape(b, n, INNER)
            x = x + o @ wo
            h = shift_token(x)
            mu = h.mean(-1, keepdims=True)
            var = h.var(-1, keepdims=True)
            h = (h - mu) / jnp.sqrt(var + 1e-05) * lg + lb
            h = h @ w1 + b1
            a, g = jnp.split(h, 2, axis=-1)
            h = a * jax.nn.gelu(g, approximate=False)
            x = x + h @ w2 + b2
            return x
        key = jax.random.key(seed)
        ks = jax.random.split(key, 6)
        return {'x': jax.random.normal(ks[0], (B, N, DIM), jnp.float32), 'wqkv': jax.random.normal(ks[1], (DEPTH, DIM, 3 * INNER), jnp.float32) * 0.02, 'q_scale': jnp.ones((DEPTH, DIM_HEAD), jnp.float32), 'k_scale': jnp.ones((DEPTH, DIM_HEAD), jnp.float32), 'wo': jax.random.normal(ks[2], (DEPTH, INNER, DIM), jnp.float32) * 0.02, 'ln_g': jnp.ones((DEPTH, DIM), jnp.float32), 'ln_b': jnp.zeros((DEPTH, DIM), jnp.float32), 'w1': jax.random.normal(ks[3], (DEPTH, DIM, 2 * HID), jnp.float32) * 0.02, 'b1': jnp.zeros((DEPTH, 2 * HID), jnp.float32), 'w2': jax.random.normal(ks[4], (DEPTH, HID, DIM), jnp.float32) * 0.02, 'b2': jnp.zeros((DEPTH, DIM), jnp.float32)}
    _L1_ffn_in = _L1_ffn_setup()
    _d = {'L0_attn_x': _L0_attn_in['x'], 'L0_attn_Wq': _L0_attn_in['Wq'], 'L0_attn_Wk': _L0_attn_in['Wk'], 'L0_attn_Wv': _L0_attn_in['Wv'], 'L0_attn_Wf1': _L0_attn_in['Wf1'], 'L0_attn_Wf2': _L0_attn_in['Wf2'], 'L0_attn_Wg1': _L0_attn_in['Wg1'], 'L0_attn_Wg2': _L0_attn_in['Wg2'], 'L0_attn_Wo': _L0_attn_in['Wo'], 'L0_attn_norm_w': _L0_attn_in['norm_w'], 'L0_ffn_gate_w': _L0_ffn_in['gate_w'], 'L0_ffn_expert_bias': _L0_ffn_in['expert_bias'], 'L0_ffn_w_gate': _L0_ffn_in['w_gate'], 'L0_ffn_w_up': _L0_ffn_in['w_up'], 'L0_ffn_w_down': _L0_ffn_in['w_down'], 'L0_ffn_shared_gate_w': _L0_ffn_in['shared_gate_w'], 'L0_ffn_shared_up_w': _L0_ffn_in['shared_up_w'], 'L0_ffn_shared_down_w': _L0_ffn_in['shared_down_w'], 'L1_attn_Wq': _L1_attn_in['Wq'], 'L1_attn_bq': _L1_attn_in['bq'], 'L1_attn_Wk': _L1_attn_in['Wk'], 'L1_attn_bk': _L1_attn_in['bk'], 'L1_attn_Wv': _L1_attn_in['Wv'], 'L1_attn_bv': _L1_attn_in['bv'], 'L1_attn_Wo': _L1_attn_in['Wo'], 'L1_attn_bo': _L1_attn_in['bo'], 'L1_attn_W1': _L1_attn_in['W1'], 'L1_attn_b1': _L1_attn_in['b1'], 'L1_attn_W2': _L1_attn_in['W2'], 'L1_attn_b2': _L1_attn_in['b2'], 'L1_attn_ln1_s': _L1_attn_in['ln1_s'], 'L1_attn_ln1_b': _L1_attn_in['ln1_b'], 'L1_attn_ln2_s': _L1_attn_in['ln2_s'], 'L1_attn_ln2_b': _L1_attn_in['ln2_b'], 'L1_attn_lnf_s': _L1_attn_in['lnf_s'], 'L1_attn_lnf_b': _L1_attn_in['lnf_b'], 'L1_ffn_wqkv': _L1_ffn_in['wqkv'], 'L1_ffn_q_scale': _L1_ffn_in['q_scale'], 'L1_ffn_k_scale': _L1_ffn_in['k_scale'], 'L1_ffn_wo': _L1_ffn_in['wo'], 'L1_ffn_ln_g': _L1_ffn_in['ln_g'], 'L1_ffn_ln_b': _L1_ffn_in['ln_b'], 'L1_ffn_w1': _L1_ffn_in['w1'], 'L1_ffn_b1': _L1_ffn_in['b1'], 'L1_ffn_w2': _L1_ffn_in['w2'], 'L1_ffn_b2': _L1_ffn_in['b2']}
    _x0 = _d['L0_attn_x']
    _d['L0_attn_x'] = jax.random.normal(jax.random.fold_in(jax.random.key(seed), 1), (8, 256, 128), dtype=_x0.dtype)
    del _x0
    return _d

def reference(L0_attn_x, L0_attn_Wq, L0_attn_Wk, L0_attn_Wv, L0_attn_Wf1, L0_attn_Wf2, L0_attn_Wg1, L0_attn_Wg2, L0_attn_Wo, L0_attn_norm_w, L0_ffn_gate_w, L0_ffn_expert_bias, L0_ffn_w_gate, L0_ffn_w_up, L0_ffn_w_down, L0_ffn_shared_gate_w, L0_ffn_shared_up_w, L0_ffn_shared_down_w, L1_attn_Wq, L1_attn_bq, L1_attn_Wk, L1_attn_bk, L1_attn_Wv, L1_attn_bv, L1_attn_Wo, L1_attn_bo, L1_attn_W1, L1_attn_b1, L1_attn_W2, L1_attn_b2, L1_attn_ln1_s, L1_attn_ln1_b, L1_attn_ln2_s, L1_attn_ln2_b, L1_attn_lnf_s, L1_attn_lnf_b, L1_ffn_wqkv, L1_ffn_q_scale, L1_ffn_k_scale, L1_ffn_wo, L1_ffn_ln_g, L1_ffn_ln_b, L1_ffn_w1, L1_ffn_b1, L1_ffn_w2, L1_ffn_b2):

    def _L0_attn_ref(x, Wq, Wk, Wv, Wf1, Wf2, Wg1, Wg2, Wo, norm_w):
        import jax, jax.numpy as jnp
        import numpy as np
        B, N, D = (2, 256, 128)
        H, M = (8, 64)
        DK = D // H
        EPS = 1e-05

        def _gsa(q, k, v, s, g):
            b = q.shape[1]

            def step1(hk, t):
                q_t, k_t, s_t, g_t = t
                hk = hk * jnp.exp(g_t)[:, :, None, :] + k_t[..., :, None] * s_t[..., None, :]
                ok = jnp.einsum('bhk,bhkm->bhm', q_t, hk)
                return (hk, ok)
            hk0 = jnp.zeros((b, H, DK, M), q.dtype)
            _, ok = jax.lax.scan(step1, hk0, (q, k, s, g))
            qv = jax.nn.softmax(ok, axis=-1)

            def step2(hv, t):
                qv_t, s_t, v_t, g_t = t
                hv = hv * jnp.exp(g_t)[..., :, None] + s_t[..., :, None] * v_t[..., None, :]
                ov = jnp.einsum('bhm,bhmv->bhv', qv_t, hv)
                return (hv, ov)
            hv0 = jnp.zeros((b, H, M, DK), q.dtype)
            _, ov = jax.lax.scan(step2, hv0, (qv, s, v, g))
            return ov
        b, n, d = x.shape
        q = jax.nn.silu(x @ Wq).reshape(b, n, H, DK)
        k = jax.nn.silu(x @ Wk).reshape(b, n, H, DK)
        v = (x @ Wv).reshape(b, n, H, DK)
        f = x @ Wf1 @ Wf2
        log_f = jax.nn.log_sigmoid(f).reshape(b, n, H, M)
        s = 1.0 - jnp.exp(log_f)
        tm = lambda a: jnp.swapaxes(a, 0, 1)
        ov = _gsa(tm(q), tm(k), tm(v), tm(s), tm(log_f))
        out = tm(ov).reshape(b, n, d)
        gate = x @ Wg1 @ Wg2
        out = out * jax.nn.sigmoid(gate)
        og = out.reshape(b, n, H, DK)
        og = og * jax.lax.rsqrt(jnp.mean(og * og, axis=-1, keepdims=True) + EPS)
        out = og.reshape(b, n, d) * norm_w
        return out @ Wo

    def _L0_ffn_ref(x, gate_w, expert_bias, w_gate, w_up, w_down, shared_gate_w, shared_up_w, shared_down_w):
        import jax, jax.numpy as jnp
        import numpy as np
        B, S, D = (2, 64, 128)
        E, K, I = (16, 8, 128)
        I_SH = 128
        ROUTE_SCALE = 2.826
        gates = jnp.einsum('bsd,ed->bse', x, gate_w)
        scores = jax.nn.sigmoid(gates.astype(jnp.float32))
        sel_scores = scores + expert_bias
        _, inds = jax.lax.top_k(sel_scores, K)
        selected = jnp.take_along_axis(scores, inds, axis=-1)
        selected = selected / selected.sum(axis=-1, keepdims=True)
        selected = selected * ROUTE_SCALE
        onehot = jax.nn.one_hot(inds, E, dtype=selected.dtype)
        combine = jnp.einsum('bske,bsk->bse', onehot, selected)
        hg = jnp.einsum('bsd,eid->bsei', x, w_gate)
        hu = jnp.einsum('bsd,eid->bsei', x, w_up)
        h = jax.nn.silu(hg) * hu
        ye = jnp.einsum('bsei,edi->bsed', h, w_down)
        y = jnp.einsum('bsed,bse->bsd', ye, combine).astype(x.dtype)
        g = jnp.einsum('bsd,id->bsi', x, shared_gate_w)
        u = jnp.einsum('bsd,id->bsi', x, shared_up_w)
        y = y + jnp.einsum('bsi,di->bsd', jax.nn.silu(g) * u, shared_down_w)
        return y

    def _L1_attn_ref(x_in, Wq, bq, Wk, bk, Wv, bv, Wo, bo, W1, b1, W2, b2, ln1_s, ln1_b, ln2_s, ln2_b, lnf_s, lnf_b):
        import math
        import jax, jax.numpy as jnp
        import numpy as np
        B, T, D, H, L = (8, 256, 128, 16, 4)
        DK = D // H
        EPS_LN = 1e-05
        EPS_ATTN = 1e-06

        def _layernorm(x, scale, bias):
            mu = jnp.mean(x, axis=-1, keepdims=True)
            var = jnp.mean(jnp.square(x - mu), axis=-1, keepdims=True)
            return (x - mu) * jax.lax.rsqrt(var + EPS_LN) * scale + bias

        def _sinusoidal_pos_emb(t, d):
            half = d // 2
            freq = jnp.exp(jnp.arange(half, dtype=jnp.float32) * (-math.log(10000.0) / (half - 1)))
            pos = (jnp.arange(t, dtype=jnp.float32) + 1.0)[:, None] * freq[None, :]
            return jnp.concatenate([jnp.sin(pos), jnp.cos(pos)], axis=-1)

        def _linear_attention(q, k, v):
            qp = jax.nn.elu(q) + 1.0
            kp = jax.nn.elu(k) + 1.0
            kv = jnp.einsum('bshd,bshm->bhmd', kp, v)
            ksum = jnp.sum(kp, axis=1)
            z = 1.0 / (jnp.einsum('blhd,bhd->blh', qp, ksum) + EPS_ATTN)
            return jnp.einsum('blhd,bhmd,blh->blhm', qp, kv, z)

        def _encoder_layer(x, Wq, bq, Wk, bk, Wv, bv, Wo, bo, W1, b1, W2, b2, ln1_s, ln1_b, ln2_s, ln2_b):
            b, t, d = x.shape
            h = _layernorm(x, ln1_s, ln1_b)
            q = (h @ Wq + bq).reshape(b, t, H, DK)
            k = (h @ Wk + bk).reshape(b, t, H, DK)
            v = (h @ Wv + bv).reshape(b, t, H, DK)
            attn = _linear_attention(q, k, v).reshape(b, t, d)
            x = x + (attn @ Wo + bo)
            h = _layernorm(x, ln2_s, ln2_b)
            h = jax.nn.relu(h @ W1 + b1) @ W2 + b2
            return x + h
        b, t, d = x_in.shape
        x = math.sqrt(d) * x_in + _sinusoidal_pos_emb(t, d)[None, :, :]
        for i in range(L):
            x = _encoder_layer(x, Wq[i], bq[i], Wk[i], bk[i], Wv[i], bv[i], Wo[i], bo[i], W1[i], b1[i], W2[i], b2[i], ln1_s[i], ln1_b[i], ln2_s[i], ln2_b[i])
        return _layernorm(x, lnf_s, lnf_b)

    def _L1_ffn_ref(x, wqkv, q_scale, k_scale, wo, ln_g, ln_b, w1, b1, w2, b2):
        import jax, jax.numpy as jnp
        import numpy as np
        DIM = 128
        DEPTH = 2
        HEADS = 8
        DIM_HEAD = 64
        WINDOW = 64
        INNER = HEADS * DIM_HEAD
        HID = int(DIM * 4 * 2 / 3)
        B, N = (2, 1024)
        QK_SCALE = 8.0

        def shift_token(t):
            t1, t2 = jnp.split(t, 2, axis=-1)
            t2 = jnp.pad(t2, ((0, 0), (1, 0), (0, 0)))[:, :-1]
            return jnp.concatenate([t1, t2], axis=-1)

        def l2norm(t):
            return t / jnp.clip(jnp.linalg.norm(t, axis=-1, keepdims=True), 1e-12)

        def rotate_half(x):
            x1, x2 = jnp.split(x, 2, axis=-1)
            return jnp.concatenate([-x2, x1], axis=-1)

        def rotary_xpos(q, k):
            n = q.shape[-2]
            half_idx = jnp.arange(0, DIM_HEAD, 2, dtype=jnp.float32)
            inv_freq = 1.0 / 10000.0 ** (half_idx / DIM_HEAD)
            t = jnp.arange(n, dtype=jnp.float32)
            freqs = t[:, None] * inv_freq[None, :]
            freqs = jnp.concatenate([freqs, freqs], axis=-1)
            base = (half_idx + 0.4 * DIM_HEAD) / (1.4 * DIM_HEAD)
            power = (t - n // 2) / float(WINDOW // 2)
            scale = base[None, :] ** power[:, None]
            scale = jnp.concatenate([scale, scale], axis=-1)
            cos, sin = (jnp.cos(freqs), jnp.sin(freqs))
            q = q * cos * scale + rotate_half(q) * sin * scale
            k = k * cos / scale + rotate_half(k) * sin / scale
            return (q, k)

        def local_attention(q, k, v):
            b, h, n, d = q.shape
            w = n // WINDOW
            bq = q.reshape(b, h, w, WINDOW, d) * QK_SCALE
            bk = k.reshape(b, h, w, WINDOW, d)
            bv = v.reshape(b, h, w, WINDOW, d)

            def look_around(t):
                p = jnp.pad(t, ((0, 0), (0, 0), (1, 0), (0, 0), (0, 0)))
                return jnp.concatenate([p[:, :, :w], p[:, :, 1:]], axis=3)
            bk, bv = (look_around(bk), look_around(bv))
            bt = jnp.arange(n).reshape(w, WINDOW)
            btp = jnp.pad(bt, ((1, 0), (0, 0)), constant_values=-1)
            btk = jnp.concatenate([btp[:w], btp[1:]], axis=1)
            sim = jnp.einsum('bhwid,bhwjd->bhwij', bq, bk)
            i = bt[:, :, None]
            j = btk[:, None, :]
            mask = (i < j) | (i > j + WINDOW) | (j == -1)
            sim = jnp.where(mask, -jnp.finfo(sim.dtype).max, sim)
            attn = jax.nn.softmax(sim, axis=-1)
            out = jnp.einsum('bhwij,bhwjd->bhwid', attn, bv)
            return out.reshape(b, h, n, d)

        def _layer(x, wqkv, qs, ksc, wo, lg, lb, w1, b1, w2, b2):
            b, n, _ = x.shape
            h = shift_token(x)
            qkv = h @ wqkv
            q, k, v = jnp.split(qkv, 3, axis=-1)
            to_heads = lambda t: t.reshape(b, n, HEADS, DIM_HEAD).transpose(0, 2, 1, 3)
            q, k, v = (to_heads(q), to_heads(k), to_heads(v))
            q = l2norm(q) * qs
            k = l2norm(k) * ksc
            q, k = rotary_xpos(q, k)
            o = local_attention(q, k, v)
            o = o.transpose(0, 2, 1, 3).reshape(b, n, INNER)
            x = x + o @ wo
            h = shift_token(x)
            mu = h.mean(-1, keepdims=True)
            var = h.var(-1, keepdims=True)
            h = (h - mu) / jnp.sqrt(var + 1e-05) * lg + lb
            h = h @ w1 + b1
            a, g = jnp.split(h, 2, axis=-1)
            h = a * jax.nn.gelu(g, approximate=False)
            x = x + h @ w2 + b2
            return x
        for l in range(DEPTH):
            x = _layer(x, wqkv[l], q_scale[l], k_scale[l], wo[l], ln_g[l], ln_b[l], w1[l], b1[l], w2[l], b2[l])
        return x
    x = L0_attn_x
    xn = _layernorm(x, axis=-1)
    s = _L0_attn_ref(xn, L0_attn_Wq, L0_attn_Wk, L0_attn_Wv, L0_attn_Wf1, L0_attn_Wf2, L0_attn_Wg1, L0_attn_Wg2, L0_attn_Wo, L0_attn_norm_w)
    g = _silu(_L0_ffn_ref(xn, L0_ffn_gate_w, L0_ffn_expert_bias, L0_ffn_w_gate, L0_ffn_w_up, L0_ffn_w_down, L0_ffn_shared_gate_w, L0_ffn_shared_up_w, L0_ffn_shared_down_w))
    x = x + s * g
    xn = _layernorm(x, axis=-1)
    s = _L1_attn_ref(xn, L1_attn_Wq, L1_attn_bq, L1_attn_Wk, L1_attn_bk, L1_attn_Wv, L1_attn_bv, L1_attn_Wo, L1_attn_bo, L1_attn_W1, L1_attn_b1, L1_attn_W2, L1_attn_b2, L1_attn_ln1_s, L1_attn_ln1_b, L1_attn_ln2_s, L1_attn_ln2_b, L1_attn_lnf_s, L1_attn_lnf_b)
    g = _silu(_L1_ffn_ref(xn, L1_ffn_wqkv, L1_ffn_q_scale, L1_ffn_k_scale, L1_ffn_wo, L1_ffn_ln_g, L1_ffn_ln_b, L1_ffn_w1, L1_ffn_b1, L1_ffn_w2, L1_ffn_b2))
    x = x + s * g
    return x

_drawn_inputs = setup_inputs


def setup_inputs(seed=0):
    import zlib

    import numpy as np

    out = dict(_drawn_inputs(seed))
    spreads = {'L0_attn_norm_w': (1.0, 0.6),
     'L0_ffn_expert_bias': (0.0, 0.8),
     'L1_attn_bq': (0.0, 2.0),
     'L1_attn_bk': (0.0, 2.0),
     'L1_attn_bv': (0.0, 0.8),
     'L1_attn_bo': (0.0, 0.8),
     'L1_attn_b1': (0.0, 0.8),
     'L1_attn_b2': (0.0, 0.8),
     'L1_attn_ln1_s': (1.0, 0.6),
     'L1_attn_ln1_b': (0.0, 0.8),
     'L1_attn_ln2_s': (1.0, 0.6),
     'L1_attn_ln2_b': (0.0, 0.8),
     'L1_attn_lnf_s': (1.0, 0.2),
     'L1_attn_lnf_b': (0.0, 0.1),
     'L1_ffn_q_scale': (1.0, 0.6),
     'L1_ffn_k_scale': (1.0, 0.6),
     'L1_ffn_ln_g': (1.0, 0.6),
     'L1_ffn_ln_b': (0.0, 0.8),
     'L1_ffn_b1': (0.0, 0.8),
     'L1_ffn_b2': (0.0, 0.8)}
    factors = {'L0_attn_Wq': 8.0,
     'L0_attn_Wk': 8.0,
     'L0_attn_Wv': 8.0,
     'L0_attn_Wf1': 8.0,
     'L0_attn_Wf2': 8.0,
     'L0_attn_Wg1': 8.0,
     'L0_attn_Wg2': 8.0,
     'L0_attn_Wo': 8.0,
     'L0_ffn_gate_w': 8.0,
     'L0_ffn_w_gate': 8.0,
     'L0_ffn_w_up': 8.0,
     'L0_ffn_w_down': 8.0,
     'L0_ffn_shared_gate_w': 8.0,
     'L0_ffn_shared_up_w': 8.0,
     'L0_ffn_shared_down_w': 8.0,
     'L1_attn_Wq': 8.0,
     'L1_attn_Wk': 8.0,
     'L1_attn_Wv': 8.0,
     'L1_attn_Wo': 8.0,
     'L1_attn_W1': 8.0,
     'L1_attn_W2': 8.0,
     'L1_ffn_wqkv': 4.127,
     'L1_ffn_wo': 4.127,
     'L1_ffn_w1': 8.0,
     'L1_ffn_w2': 8.0}
    for name, (base, spread) in spreads.items():
        noise = np.random.default_rng([zlib.crc32(name.encode()), seed]).standard_normal(out[name].shape)
        drawn = base * np.exp(spread * noise) if base else spread * noise
        out[name] = jnp.asarray(drawn.astype(out[name].dtype))
    for name, factor in factors.items():
        out[name] = (out[name] * factor).astype(out[name].dtype)
    return out
```

```python
import numpy as np
import concourse.bass as bass
from concourse import mybir
from contextlib import ExitStack

F32 = mybir.dt.float32
ALU = mybir.AluOpType
ACT = mybir.ActivationFunctionType
AX_X = mybir.AxisListType.X

P = 128
D = 128
B = 8
T = 256
NT = T // P
EPS = 1e-5

GH, GDK, GM = 8, 16, 64
HM = GH * GM
CH = 8
CT = P // CH
NCH = T // CH
GRP = 64
GC = GRP // CH
NG = T // GRP
NB = HM // P
FLOOR = -19.0

E, TOPK = 16, 8
ROUTE_SCALE = 2.826

LA, LH, LDK = 4, 16, 8
FF = 4 * D

LF, FH, FDH, WIN = 2, 8, 64, 64
INNER = FH * FDH
KEYS = WIN + P
HID = int(D * 4 * 2 / 3)
HBLK = [(0, 128), (128, 128), (256, HID - 256)]
NEG = -1e30


def shape_constants():
    i = np.arange(P)
    pos, chunk = i % CH, i // CH
    c = {}
    c["ident"] = np.eye(P)
    same = chunk[:, None] == chunk[None, :]
    mid = CH // 2 - 1
    up = same & (pos[:, None] > mid) & (pos[:, None] <= pos[None, :])
    down = same & (pos[:, None] <= mid) & (pos[:, None] > pos[None, :])
    c["from_mid"] = -(up.astype(float) - down.astype(float))
    span = np.zeros((T, NCH))
    for n in range(NCH):
        span[n * CH + mid + 1:(n + 1) * CH + mid + 1, n] = -1.0
    span = span.reshape(GC, NT, 2, CH, NCH).transpose(1, 2, 0, 3, 4)
    c["mid_to_mid"] = span.reshape(NT, P, NCH).transpose(1, 0, 2).reshape(P, -1)
    c["chunk_causal"] = (same & (i[:, None] <= i[None, :])).astype(float)
    c["chunk_of_token"] = (2 * (chunk % GC) + chunk // GC == np.arange(CT)[:, None]).T.astype(float)
    kc = np.arange(GDK * GC)
    c["group_chunk"] = (kc[:, None] % GC == (np.arange(GRP) // CH)[None, :]).astype(float)
    c["sum_chunks"] = (kc[:, None] // GC == np.arange(GDK)[None, :]).astype(float)
    rep = np.zeros((P, GH, P))
    for h in range(GH):
        for k in range(GDK):
            rep[h * GDK + k, h, k * GC:(k + 1) * GC] = 1.0
    c["spread_key"] = rep.reshape(P, -1)
    c["head_rows"] = (i[:, None] // GDK == np.arange(GH)[None, :]).astype(float)
    return {k: np.ascontiguousarray(v, dtype=np.float32) for k, v in c.items()}


def layer1_constants():
    i = np.arange(P)
    c = {}
    c["ident"] = np.eye(P)
    c["head_block"] = (i[:, None] // LDK == i[None, :] // LDK).astype(float)
    c["next_token"] = (i[:, None] + 1 == i[None, :]).astype(float)
    c["next_tile"] = ((i[:, None] == P - 1) & (i[None, :] == 0)).astype(float)
    half = D // 2
    f32 = np.float32
    freq = np.exp(np.arange(half, dtype=f32) * f32(-np.log(10000.0) / (half - 1))).astype(f32)
    ang = ((np.arange(T, dtype=f32) + f32(1.0))[:, None] * freq[None, :]).astype(f32)
    emb = np.concatenate([np.sin(ang), np.cos(ang)], axis=-1)
    c["pos_emb"] = emb.reshape(NT, P, D).transpose(1, 0, 2).reshape(P, -1)
    hi = np.arange(0, FDH, 2, dtype=f32)
    inv = (f32(1.0) / f32(10000.0) ** (hi / f32(FDH))).astype(f32)
    t = np.arange(T, dtype=f32)
    ang = (t[:, None] * inv[None, :]).astype(f32)
    base = ((hi + f32(0.4 * FDH)) / f32(1.4 * FDH)).astype(f32)
    power = ((t - T // 2) / f32(WIN // 2)).astype(f32)
    sc = (base[None, :] ** power[:, None]).astype(f32)
    cos, sin = np.cos(ang), np.sin(ang)
    dbl = lambda a, s=1.0: np.concatenate([s * a, a], axis=-1)
    rot = np.stack([dbl(cos * sc), dbl(sin * sc, -1.0), dbl(cos / sc), dbl(sin / sc, -1.0)], axis=1)
    c["rotary"] = rot.reshape(NT, P, 4 * FDH).transpose(1, 0, 2).reshape(P, -1)
    j = np.arange(KEYS) - WIN
    m = []
    for tt in range(NT):
        qi, kj = i[:, None] + tt * P, j[None, :] + tt * P
        seen = (kj >= 0) & (qi >= kj) & (qi <= kj + WIN) & (kj // WIN >= qi // WIN - 1)
        m.append(np.where(seen, 0.0, NEG))
    c["window"] = np.stack(m, axis=1).reshape(P, -1)
    return {k: np.ascontiguousarray(v, dtype=np.float32) for k, v in c.items()}


class Banks:

    def __init__(self, ctx, nc, name, banks, jobs):
        self.banks, self.jobs = banks, {job: n for n, job in enumerate(jobs)}
        assert len(self.jobs) == len(jobs)
        self.filled = [ctx.enter_context(nc.semaphore(f"{name}_filled{i}")) for i in range(len(banks))]
        self.emptied = [ctx.enter_context(nc.semaphore(f"{name}_emptied{i}")) for i in range(len(banks))]

    def at(self, job):
        n = self.jobs[job]
        return n % len(self.banks), n // len(self.banks)

    def tile(self, job):
        return self.banks[self.at(job)[0]]

    def wait_free(self, pe, job):
        b, use = self.at(job)
        if use:
            pe.wait_ge(self.emptied[b], use)

    def is_filled(self, ins, job):
        ins.then_inc(self.filled[self.at(job)[0]], 1)

    def wait_filled(self, eng, job):
        b, use = self.at(job)
        eng.wait_ge(self.filled[b], use + 1)

    def is_emptied(self, ins, job):
        ins.then_inc(self.emptied[self.at(job)[0]], 1)

    def wait_emptied(self, eng, job):
        b, use = self.at(job)
        eng.wait_ge(self.emptied[b], use + 1)

    def sems(self):
        return self.filled + self.emptied


class Chain:

    def __init__(self, eng, sem):
        self.eng, self.sem, self.count = eng, sem, 0

    def __call__(self, ins):
        ins.then_inc(self.sem, 1)
        self.count += 1
        self.eng.wait_ge(self.sem, self.count)


def run_stages(*streams):
    live = list(streams)
    while live:
        for s in list(live):
            if next(s, "end") == "end":
                live.remove(s)


def layer0(nc, x, x1, w, const, psum):
    ctx = ExitStack()
    with ctx:
        def sb(name, *shape):
            return ctx.enter_context(nc.sbuf_tensor(name, list(shape), F32))

        def sem(name):
            return ctx.enter_context(nc.semaphore(name))

        widths = {k: v.shape[1] for k, v in const.items()}
        table = {k: sb(f"table_{k}", P, n) for k, n in widths.items()}
        ident = table["ident"]
        w_q, w_k, w_kv = sb("w_q", P, D), sb("w_k", P, D), sb("w_kv", P, 2 * D)
        w_fg = sb("w_fg", P, 2 * GDK)
        w_f2, w_g2 = sb("w_f2", GDK, HM), sb("w_g2", GDK, D)
        w_out, norm_w = sb("w_out", P, D), sb("norm_w", P, 1)
        gate_t = sb("gate_t", P, E)
        route_bias = sb("route_bias", P, E)
        w_in_t = sb("w_in_t", P, E + 1, 2, P)
        w_down_t = sb("w_down_t", P, E + 1, D)
        half_pow = sb("half_pow", P, 2 * GH)

        xin = sb("xin", P, NT, D)
        stats, moments = sb("stats", P, NT, 6), sb("moments", P, NT, 2)
        var_eps, rstd = sb("var_eps", P, NT), sb("rstd", P, NT)
        xn, xn_t = sb("xn", P, NT, D), sb("xn_t", P, T)
        tanh_qk, qk_t = sb("tanh_qk", P, 2, T), sb("qk_t", P, 2, T)
        tanh_k = sb("tanh_k", P, NT, D)
        kv = sb("kv", P, NT, 2, D)
        fg1 = sb("fg1", GDK, 2, T)
        sp = sb("softplus", P, NT, HM)
        slot_w = sb("slot_w", P, NT, HM)
        from_mid, to_mid = sb("from_mid", P, NT, HM), sb("to_mid", P, NT, HM)
        exp_gate = sb("exp_gate", P, NT, D)
        chunk_decay = sb("chunk_decay", P, NB, GDK, NCH)
        kv_chunks = sb("kv_chunks", P, NT, 2, D, CT)
        q_heads = sb("q_heads", P, GH, T)
        qk_near = sb("qk_near", P, NT, GH, P)
        q_spread = sb("q_spread", P, GH, T)
        state = sb("state", P, 2, NB, 1 + GDK * NCH)
        k_state_t = sb("k_state_t", P, NG, HM)
        slots = sb("slots", P, NT, HM)
        slot_max, slot_sum = sb("slot_max", P, NT, GH), sb("slot_sum", P, NT, GH)
        slot_q = sb("slot_q", P, NT, HM)
        slot_w_t, slot_q_t = sb("slot_w_t", P, NT, NB, P), sb("slot_q_t", P, NT, NB, P)
        far = sb("far", P, GH, P)
        den, og, og_sq = sb("den", P, NT, D), sb("og", P, NT, D), sb("og_sq", P, NT, D)
        og_ms, og_rms = sb("og_ms", P, NT * GH), sb("og_rms", P, NT * GH)
        og_t, attn = sb("og_t", P, T), sb("attn", P, NT, D)
        score, sel, sel_left = sb("score", P, NT, E), sb("sel", P, NT, E), sb("sel_left", P, NT, E)
        top8, mix_sum = sb("top8", P, NT, TOPK), sb("mix_sum", P, NT)
        mix = sb("mix", P, NT, E + 1)
        tanh_g, hid = sb("tanh_g", P, 2, T), sb("hid", P, 2, T)
        y, tanh_y = sb("y", P, NT, D), sb("tanh_y", P, NT, D)

        loads, scaled = sem("loads"), sem("out_scaled")
        pairs = ([(table[k][:], const[k]) for k in table]
                 + [(w_q[:], w["Wq"]), (w_k[:], w["Wk"]), (w_kv[:, 0:D], w["Wk"]), (w_kv[:, D:2 * D], w["Wv"]),
                    (w_fg[:, 0:GDK], w["Wf1"]), (w_fg[:, GDK:2 * GDK], w["Wg1"]), (w_f2[:], w["Wf2"]),
                    (w_g2[:], w["Wg2"]), (w_out[:], w["Wo"]), (norm_w[:], w["norm_w"].rearrange("(p a) -> p a", a=1)),
                    (gate_t[:], w["gate_w"]), (route_bias[:], w["expert_bias"].partition_broadcast(P)),
                    (w_in_t[:], w["w_in"]), (w_down_t[:], w["w_down"])])

        with nc.Block() as block:
            @block.sync
            def _(sync):
                for dst, src in pairs:
                    sync.dma_start(dst, src).then_inc(loads, 16)

            @block.vector
            def _(dve):
                dve.wait_ge(loads, 16 * len(pairs))
                dve.tensor_scalar(w_out[:], w_out[:], norm_w[:], None, ALU.mult).then_inc(scaled, 1)

            @block.gpsimd
            def _(pool):
                pool.memset(state[:, :, :, 0:1], 0.0)
                pool.memset(chunk_decay[:, :, :, NCH - 1:NCH], 0.0)
                pool.memset(mix[:, :, E:E + 1], 0.5)
                pool.memset(half_pow[:], -0.5)

        g_jobs = (["x_t", "qk", "kv", "fg1", "f0", "f1", "gate", "mid0", "mid1", "decay"]
                  + [f"near{t}{a}" for t in range(NT) for a in range(2)]
                  + [f"spread{a}" for a in range(4)]
                  + [f"state{j}{r}" for j in range(NB) for r in range(2)]
                  + [f"state_t{g}" for g in range(NG)]
                  + ["slots0", "slots1", "w_t0", "w_t1", "q_t0", "q_t1"]
                  + [f"near_v{t}{a}" for t in range(NT) for a in range(2)]
                  + ["far00", "far01", "read0", "far10", "far11", "read1", "og_t", "attn"])
        m_jobs = ["route"]
        for e in range(E + 1):
            m_jobs += [f"in{e}"] + ([f"out{e - 1}"] if e else [])
        m_jobs += [f"out{E}"]
        G = Banks(ctx, nc, "gsa", psum[0:4], g_jobs)
        M = Banks(ctx, nc, "moe", psum[4:8], m_jobs)
        names = ["x_loaded", "var_ready", "rstd_ready", "xn_ready", "qk_tanh", "k_tanh", "qk_ready", "softplus_ready",
                 "exp_ready", "slot_w_ready", "chunks_ready", "q_heads_ready", "sub0", "sub1", "slot_exp0", "slot_exp1",
                 "slot_q0", "slot_q1", "og_ms_ready", "og_rms_ready", "og_ready", "tanh_g_ready", "tanh_y_ready", "x1_ready", "x1_stored"]
        S = {n: sem(f"a_{n}") for n in names}
        steps = {n: sem(f"a_{n}_step") for n in ("dve", "act")}
        per_batch = G.sems() + M.sems() + list(S.values()) + list(steps.values())

        with nc.Fori(0, B) as b:
            with nc.Block() as block:
                @block.sync
                def _(sync):
                    src = x[bass.ds(b, 1)].rearrange("a (c t g u) d -> (a t g) c u d", t=NT, g=2, u=CH)
                    for t in range(NT):
                        for g in range(2):
                            sync.dma_start(xin[g * GRP:(g + 1) * GRP, t, :], src[2 * t + g]).then_inc(S["x_loaded"], 16)
                    dst = x1[bass.ds(b, 1)].rearrange("a (c t g u) d -> (a t g) c u d", t=NT, g=2, u=CH)
                    sync.wait_ge(S["x1_ready"], 1)
                    for t in range(NT):
                        for g in range(2):
                            sync.dma_start(dst[2 * t + g], y[g * GRP:(g + 1) * GRP, t, :]).then_inc(S["x1_stored"], 16)
                    sync.wait_ge(S["x1_stored"], 16 * NG)

                @block.tensor
                def _(pe):
                    def gsa():
                        G.wait_free(pe, "x_t")
                        pe.wait_ge(S["xn_ready"], 1)
                        for t in range(NT):
                            last = pe.transpose(G.tile("x_t")[:, t * P:(t + 1) * P], xn[:, t, :], ident[:])
                        G.is_filled(last, "x_t")
                        yield
                        G.wait_emptied(pe, "x_t")
                        G.wait_free(pe, "qk")
                        pe.matmul(G.tile("qk")[:, 0:T], w_q[:], xn_t[:], start=True, stop=True)
                        G.is_filled(pe.matmul(G.tile("qk")[:, T:2 * T], w_k[:], xn_t[:], start=True, stop=True), "qk")
                        G.wait_free(pe, "kv")
                        for t in range(NT):
                            last = pe.matmul(G.tile("kv")[:, t * 2 * D:(t + 1) * 2 * D], xn_t[:, t * P:(t + 1) * P], w_kv[:], start=True, stop=True)
                        G.is_filled(last, "kv")
                        G.wait_free(pe, "fg1")
                        pe.matmul(G.tile("fg1")[0:GDK, 0:T], w_fg[:, 0:GDK], xn_t[:], start=True, stop=True)
                        G.is_filled(pe.matmul(G.tile("fg1")[0:GDK, T:2 * T], w_fg[:, GDK:2 * GDK], xn_t[:], start=True, stop=True), "fg1")
                        yield
                        G.wait_emptied(pe, "fg1")
                        for t in range(NT):
                            G.wait_free(pe, f"f{t}")
                            G.is_filled(pe.matmul(G.tile(f"f{t}")[:], fg1[:, 0, t * P:(t + 1) * P], w_f2[:], start=True, stop=True), f"f{t}")
                        G.wait_free(pe, "gate")
                        for t in range(NT):
                            last = pe.matmul(G.tile("gate")[:, t * P:(t + 1) * P], fg1[:, 1, t * P:(t + 1) * P], w_g2[:], start=True, stop=True)
                        G.is_filled(last, "gate")
                        yield
                        pe.wait_ge(S["softplus_ready"], 1)
                        for t in range(NT):
                            G.wait_free(pe, f"mid{t}")
                            G.is_filled(pe.matmul(G.tile(f"mid{t}")[:], table["from_mid"][:], sp[:, t, :], start=True, stop=True), f"mid{t}")
                        G.wait_free(pe, "decay")
                        for j in range(NB):
                            for t in range(NT):
                                last = pe.matmul(G.tile("decay")[:, j * NCH:(j + 1) * NCH], sp[:, t, j * P:(j + 1) * P],
                                                 table["mid_to_mid"][:, t * NCH:(t + 1) * NCH], start=(t == 0), stop=(t == NT - 1))
                        G.is_filled(last, "decay")
                        yield
                        G.wait_emptied(pe, "qk")
                        pe.wait_ge(S["qk_ready"], 1)
                        pe.wait_ge(S["q_heads_ready"], GH)
                        for t in range(NT):
                            for a in range(2):
                                job = f"near{t}{a}"
                                G.wait_free(pe, job)
                                G.is_filled(pe.matmul(G.tile(job)[:], qk_t[:, 1, t * P:(t + 1) * P],
                                                      q_heads[:, 4 * a:4 * a + 4, t * P:(t + 1) * P], start=True, stop=True), job)
                        for a in range(4):
                            job = f"spread{a}"
                            G.wait_free(pe, job)
                            for i in range(2):
                                h = 2 * a + i
                                last = pe.matmul(G.tile(job)[:, i * T:(i + 1) * T], table["spread_key"][:, h * P:(h + 1) * P],
                                                 qk_t[:, 0, :], start=True, stop=True)
                            G.is_filled(last, job)
                        yield
                        pe.wait_ge(S["slot_w_ready"], 1)
                        pe.wait_ge(S["chunks_ready"], NT)
                        for j in range(NB):
                            for r in range(2):
                                job = f"state{j}{r}"
                                G.wait_free(pe, job)
                                out = G.tile(job)[:].rearrange("p (k g) -> p k g", g=NG)
                                for i in range(2):
                                    h = 2 * j + i
                                    for t in range(NT):
                                        last = pe.matmul(out[GM * i:GM * (i + 1), :, 2 * t:2 * t + 2],
                                                         to_mid[:, t, h * GM:(h + 1) * GM],
                                                         kv_chunks[:, t, r, h * GDK:(h + 1) * GDK, :], start=True, stop=True)
                                G.is_filled(last, job)
                        yield
                        for g in range(NG):
                            job = f"state_t{g}"
                            G.wait_free(pe, job)
                            if g == 0:
                                for j in range(NB):
                                    G.wait_emptied(pe, f"state{j}0")
                            for j in range(NB):
                                last = pe.transpose(G.tile(job)[:, j * P:(j + 1) * P], state[:, 0, j, g:GDK * NCH:NG], ident[:])
                            G.is_filled(last, job)
                        for t in range(NT):
                            job = f"slots{t}"
                            G.wait_free(pe, job)
                            for a in range(2):
                                G.wait_emptied(pe, f"near{t}{a}")
                            for a in range(4):
                                G.wait_emptied(pe, f"spread{a}")
                            for g in range(2):
                                G.wait_emptied(pe, f"state_t{2 * t + g}")
                            for h in range(GH):
                                cols = slice(h * GM, (h + 1) * GM)
                                for i in range(2):
                                    g = 2 * t + i
                                    pe.matmul(G.tile(job)[GRP * i:GRP * (i + 1), cols], q_spread[:, h, g * GRP:(g + 1) * GRP],
                                              k_state_t[:, g, cols], start=True, stop=False)
                                last = pe.matmul(G.tile(job)[:, cols], qk_near[:, t, h, :], to_mid[:, t, cols], start=False, stop=True)
                            G.is_filled(last, job)
                        yield
                        for t in range(NT):
                            job = f"w_t{t}"
                            G.wait_free(pe, job)
                            for j in range(NB):
                                last = pe.transpose(G.tile(job)[:, j * P:(j + 1) * P], to_mid[:, t, j * P:(j + 1) * P], ident[:])
                            G.is_filled(last, job)
                        yield
                        for t in range(NT):
                            job = f"q_t{t}"
                            G.wait_free(pe, job)
                            pe.wait_ge(S[f"slot_q{t}"], 1)
                            for j in range(NB):
                                last = pe.transpose(G.tile(job)[:, j * P:(j + 1) * P], slot_q[:, t, j * P:(j + 1) * P], ident[:])
                            G.is_filled(last, job)
                        yield
                        for t in range(NT):
                            G.wait_emptied(pe, f"w_t{t}")
                            G.wait_emptied(pe, f"q_t{t}")
                            for a in range(2):
                                job = f"near_v{t}{a}"
                                G.wait_free(pe, job)
                                for i in range(4):
                                    h = 2 * i + a
                                    rows = slice(GM * (h % 2), GM * (h % 2) + GM)
                                    last = pe.matmul(G.tile(job)[:, i * P:(i + 1) * P], slot_w_t[rows, t, h // 2, :],
                                                     slot_q_t[rows, t, h // 2, :], start=True, stop=True)
                                G.is_filled(last, job)
                        yield
                        for j in range(NB):
                            G.wait_emptied(pe, f"state{j}1")
                        for t in range(NT):
                            for a in range(2):
                                job = f"far{t}{a}"
                                G.wait_free(pe, job)
                                rows = slice(GM * a, GM * (a + 1))
                                for j in range(NB):
                                    for i in range(2):
                                        last = pe.matmul(G.tile(job)[:, j * P + i * GRP:j * P + (i + 1) * GRP],
                                                         state[rows, 1, j, 2 * t + i:GDK * NCH:NG],
                                                         slot_q_t[rows, t, j, i * GRP:(i + 1) * GRP], start=True, stop=True)
                                G.is_filled(last, job)
                            job = f"read{t}"
                            G.wait_free(pe, job)
                            for i in range(2):
                                G.wait_emptied(pe, f"far{t}{i}")
                                G.wait_emptied(pe, f"near_v{t}{i}")
                            for h in range(GH):
                                cols = slice(h * GDK, (h + 1) * GDK)
                                pe.matmul(G.tile(job)[:, cols], qk_near[:, t, h, :], kv[:, t, 1, cols], start=True, stop=False)
                                last = pe.matmul(G.tile(job)[:, cols], far[:, h, :], table["sum_chunks"][:], start=False, stop=True)
                            G.is_filled(last, job)
                        yield
                        G.wait_free(pe, "og_t")
                        pe.wait_ge(S["og_ready"], 1)
                        for t in range(NT):
                            last = pe.transpose(G.tile("og_t")[:, t * P:(t + 1) * P], og[:, t, :], ident[:])
                        G.is_filled(last, "og_t")
                        G.wait_free(pe, "attn")
                        G.wait_emptied(pe, "og_t")
                        for t in range(NT):
                            last = pe.matmul(G.tile("attn")[:, t * D:(t + 1) * D], og_t[:, t * P:(t + 1) * P], w_out[:], start=True, stop=True)
                        G.is_filled(last, "attn")

                    def experts_in(e):
                        job = f"in{e}"
                        M.wait_free(pe, job)
                        pe.matmul(M.tile(job)[:, 0:T], w_in_t[:, e, 0, :], xn_t[:], start=True, stop=True)
                        M.is_filled(pe.matmul(M.tile(job)[:, T:2 * T], w_in_t[:, e, 1, :], xn_t[:], start=True, stop=True), job)

                    def experts_out(e):
                        job = f"out{e}"
                        M.wait_free(pe, job)
                        M.wait_emptied(pe, f"in{e}")
                        for t in range(NT):
                            last = pe.matmul(M.tile(job)[:, t * D:(t + 1) * D], hid[:, e % 2, t * P:(t + 1) * P], w_down_t[:, e, :], start=True, stop=True)
                        M.is_filled(last, job)

                    def moe():
                        yield
                        G.wait_emptied(pe, "x_t")
                        M.wait_free(pe, "route")
                        for t in range(NT):
                            last = pe.matmul(M.tile("route")[:, t * E:(t + 1) * E], xn_t[:, t * P:(t + 1) * P], gate_t[:], start=True, stop=True)
                        M.is_filled(last, "route")
                        experts_in(0)
                        yield
                        for e in range(1, E + 1):
                            experts_in(e)
                            experts_out(e - 1)
                            if e % 2 == 0:
                                yield
                        experts_out(E)

                    run_stages(gsa(), moe())

                @block.scalar
                def _(act):
                    step = Chain(act, steps["act"])

                    def gsa():
                        G.wait_filled(act, "x_t")
                        G.is_emptied(act.activation(xn_t[:], G.tile("x_t")[:, 0:T], ACT.Copy), "x_t")
                        yield
                        G.wait_filled(act, "qk")
                        act.activation(tanh_qk[:].rearrange("p r t -> p (r t)"), G.tile("qk")[:], ACT.Tanh, scale=0.5).then_inc(S["qk_tanh"], 1)
                        G.wait_filled(act, "kv")
                        tok = G.tile("kv")[:].rearrange("p (t r d) -> p t r d", t=NT, r=2)
                        act.activation(tanh_k[:], tok[:, :, 0, :], ACT.Tanh, scale=0.5).then_inc(S["k_tanh"], 1)
                        G.wait_filled(act, "fg1")
                        G.is_emptied(act.activation(fg1[:].rearrange("p r t -> p (r t)"), G.tile("fg1")[0:GDK, :], ACT.Copy), "fg1")
                        yield
                        for t in range(NT):
                            G.wait_emptied(act, f"f{t}")
                        step(act.activation(sp[:], sp[:], ACT.Exp, scale=-1.0))
                        G.wait_filled(act, "gate")
                        G.is_emptied(act.activation(exp_gate[:].rearrange("p t d -> p (t d)"), G.tile("gate")[:, 0:T], ACT.Exp, scale=-1.0), "gate")
                        act.activation(sp[:], sp[:], ACT.Ln, bias=1.0).then_inc(S["softplus_ready"], 1)
                        act.wait_ge(S["softplus_ready"], 1)
                        act.activation(slot_w[:], sp[:], ACT.Exp, scale=-1.0).then_inc(S["exp_ready"], 1)
                        yield
                        for t in range(NT):
                            G.wait_filled(act, f"mid{t}")
                            act.activation(from_mid[:, t, :], G.tile(f"mid{t}")[:], ACT.Exp)
                            G.is_emptied(act.activation(to_mid[:, t, :], G.tile(f"mid{t}")[:], ACT.Exp, scale=-1.0), f"mid{t}")
                        G.wait_filled(act, "decay")
                        for j in range(NB):
                            src = G.tile("decay")[:, j * NCH:j * NCH + NCH - 1].unsqueeze(1).to_broadcast([P, GDK, NCH - 1])
                            last = act.activation(chunk_decay[:, j, :, 0:NCH - 1], src, ACT.Exp)
                        G.is_emptied(last, "decay")
                        yield
                        yield
                        yield
                        for g in range(NG):
                            job = f"state_t{g}"
                            G.wait_filled(act, job)
                            G.is_emptied(act.activation(k_state_t[:, g, :], G.tile(job)[:], ACT.Copy), job)
                        yield
                        for t in range(NT):
                            act.wait_ge(S[f"sub{t}"], 1)
                            act.activation(slots[:, t, :], slots[:, t, :], ACT.Exp).then_inc(S[f"slot_exp{t}"], 1)
                        for t in range(NT):
                            job = f"w_t{t}"
                            G.wait_filled(act, job)
                            G.is_emptied(act.activation(slot_w_t[:, t].rearrange("p j t -> p (j t)"), G.tile(job)[:], ACT.Copy), job)
                        yield
                        for t in range(NT):
                            job = f"q_t{t}"
                            G.wait_filled(act, job)
                            G.is_emptied(act.activation(slot_q_t[:, t].rearrange("p j t -> p (j t)"), G.tile(job)[:], ACT.Copy), job)
                        yield
                        yield
                        yield
                        G.wait_filled(act, "og_t")
                        G.is_emptied(act.activation(og_t[:], G.tile("og_t")[:, 0:T], ACT.Copy), "og_t")
                        G.wait_filled(act, "attn")
                        G.is_emptied(act.activation(attn[:].rearrange("p t d -> p (t d)"), G.tile("attn")[:, 0:T], ACT.Copy), "attn")

                    def tanh(e):
                        job = f"in{e}"
                        M.wait_filled(act, job)
                        if e >= 2:
                            M.wait_emptied(act, f"in{e - 2}")
                        act.activation(tanh_g[:, e % 2, :], M.tile(job)[:, 0:T], ACT.Tanh, scale=0.5).then_inc(S["tanh_g_ready"], 1)

                    def moe():
                        yield
                        M.wait_filled(act, "route")
                        M.is_emptied(act.activation(score[:].rearrange("p t e -> p (t e)"), M.tile("route")[:, 0:NT * E], ACT.Exp, scale=-1.0), "route")
                        tanh(0)
                        yield
                        for e in range(1, E + 1):
                            tanh(e)
                            if e % 2 == 0:
                                yield

                    run_stages(gsa(), moe())
                    M.wait_emptied(act, f"out{E}")
                    act.activation(tanh_y[:], y[:], ACT.Tanh, scale=0.5).then_inc(S["tanh_y_ready"], 1)

                @block.gpsimd
                def _(pool):
                    pool.wait_ge(S["var_ready"], 1)
                    pool.tensor_tensor(rstd[:], var_eps[:], half_pow[:, 0:NT], ALU.pow).then_inc(S["rstd_ready"], 1)
                    pool.wait_ge(S["qk_ready"], 1)
                    for h in range(GH):
                        pool.tensor_scalar(q_heads[:, h, :], qk_t[:, 0, :], table["head_rows"][:, h:h + 1], None, ALU.mult).then_inc(S["q_heads_ready"], 1)
                    pool.wait_ge(S["og_ms_ready"], 1)
                    pool.tensor_tensor(og_rms[:], og_ms[:], half_pow[:], ALU.pow).then_inc(S["og_rms_ready"], 1)

                @block.vector
                def _(dve):
                    step = Chain(dve, steps["dve"])

                    def gsa():
                        dve.wait_ge(S["x_loaded"], 16 * NG)
                        for t in range(NT):
                            last = dve.bn_stats(stats[:, t, :], xin[:, t, :])
                        step(last)
                        for t in range(NT):
                            last = dve.bn_aggr(moments[:, t, :], stats[:, t, :])
                        step(last)
                        dve.tensor_scalar(var_eps[:], moments[:, :, 1], EPS, None, ALU.add).then_inc(S["var_ready"], 1)
                        dve.wait_ge(S["rstd_ready"], 1)
                        for t in range(NT):
                            last = dve.tensor_scalar(xn[:, t, :], xin[:, t, :], moments[:, t, 0:1], rstd[:, t:t + 1], ALU.subtract, ALU.mult)
                        last.then_inc(S["xn_ready"], 1)
                        yield
                        dve.wait_ge(S["qk_tanh"], 1)
                        qk_flat = qk_t[:].rearrange("p r t -> p (r t)")
                        G.is_emptied(dve.scalar_tensor_tensor(qk_flat, tanh_qk[:].rearrange("p r t -> p (r t)"), 1.0,
                                                              G.tile("qk")[:], ALU.add, ALU.mult), "qk")
                        G.wait_emptied(dve, "qk")
                        dve.tensor_scalar(qk_flat, qk_flat, 0.5, None, ALU.mult).then_inc(S["qk_ready"], 1)
                        dve.wait_ge(S["k_tanh"], 1)
                        tok = G.tile("kv")[:].rearrange("p (t r d) -> p t r d", t=NT, r=2)
                        dve.scalar_tensor_tensor(kv[:, :, 0, :], tanh_k[:], 1.0, tok[:, :, 0, :], ALU.add, ALU.mult)
                        G.is_emptied(dve.tensor_copy(kv[:, :, 1, :], tok[:, :, 1, :]), "kv")
                        yield
                        for t in range(NT):
                            G.wait_filled(dve, f"f{t}")
                            G.is_emptied(dve.tensor_scalar(sp[:, t, :], G.tile(f"f{t}")[:], FLOOR, None, ALU.max), f"f{t}")
                        G.wait_emptied(dve, "kv")
                        for t in range(NT):
                            for r in range(2):
                                mask = table["chunk_of_token"][:].unsqueeze(1).to_broadcast([P, D, CT])
                                last = dve.scalar_tensor_tensor(kv_chunks[:, t, r], kv[:, t, r, :].unsqueeze(2).to_broadcast([P, D, CT]),
                                                                0.5 if r == 0 else 1.0, mask, ALU.mult, ALU.mult)
                            last.then_inc(S["chunks_ready"], 1)
                        yield
                        dve.wait_ge(S["exp_ready"], 1)
                        step(dve.tensor_scalar(slot_w[:], slot_w[:], -1.0, 1.0, ALU.mult, ALU.add))
                        for t in range(NT):
                            G.wait_emptied(dve, f"mid{t}")
                            last = dve.tensor_tensor(to_mid[:, t, :], to_mid[:, t, :], slot_w[:, t, :], ALU.mult)
                        last.then_inc(S["slot_w_ready"], 1)
                        yield
                        for t in range(NT):
                            for a in range(2):
                                job = f"near{t}{a}"
                                G.wait_filled(dve, job)
                                mask = table["chunk_causal"][:].unsqueeze(1).to_broadcast([P, 4, P])
                                G.is_emptied(dve.tensor_tensor(qk_near[:, t, 4 * a:4 * a + 4, :],
                                                               G.tile(job)[:].rearrange("p (h t) -> p h t", t=P), mask, ALU.mult), job)
                        for a in range(4):
                            job = f"spread{a}"
                            G.wait_filled(dve, job)
                            mask = table["group_chunk"][:].unsqueeze(1).to_broadcast([P, 2 * NG, GRP])
                            G.is_emptied(dve.tensor_tensor(q_spread[:, 2 * a:2 * a + 2, :].rearrange("p h (g t) -> p (h g) t", t=GRP),
                                                           G.tile(job)[:].rearrange("p (g t) -> p g t", t=GRP), mask, ALU.mult), job)
                        yield
                        G.wait_emptied(dve, "decay")
                        for j in range(NB):
                            for r in range(2):
                                job = f"state{j}{r}"
                                G.wait_filled(dve, job)
                                G.is_emptied(dve.tensor_tensor_scan(state[:, r, j, 1:1 + GDK * NCH], G.tile(job)[:],
                                                                    chunk_decay[:, j].rearrange("p k c -> p (k c)"), 0.0, ALU.add, ALU.mult), job)
                        yield
                        for t in range(NT):
                            job = f"slots{t}"
                            G.wait_filled(dve, job)
                            G.is_emptied(dve.tensor_tensor(slots[:, t, :], G.tile(job)[:], from_mid[:, t, :], ALU.mult), job)
                            G.wait_emptied(dve, job)
                            heads = slots[:, t, :].rearrange("p (h m) -> p h m", m=GM)
                            step(dve.tensor_reduce(slot_max[:, t, :], heads, AX_X, ALU.max))
                            dve.tensor_tensor(heads, heads, slot_max[:, t, :].unsqueeze(2).to_broadcast([P, GH, GM]), ALU.subtract).then_inc(S[f"sub{t}"], 1)
                        yield
                        for t in range(NT):
                            dve.wait_ge(S[f"slot_exp{t}"], 1)
                            dve.tensor_tensor(slot_q[:, t, :], slots[:, t, :], from_mid[:, t, :], ALU.mult).then_inc(S[f"slot_q{t}"], 1)
                            step(dve.tensor_reduce(slot_sum[:, t, :], slots[:, t, :].rearrange("p (h m) -> p h m", m=GM), AX_X, ALU.add))
                        yield
                        G.wait_emptied(dve, "gate")
                        step(dve.scalar_tensor_tensor(den[:].rearrange("p t (h v) -> p (t h) v", v=GDK), exp_gate[:].rearrange("p t (h v) -> p (t h) v", v=GDK), 1.0,
                                                      slot_sum[:].rearrange("p t h -> p (t h)").unsqueeze(2).to_broadcast([P, NT * GH, GDK]), ALU.add, ALU.mult))
                        step(dve.reciprocal(den[:], den[:]))
                        yield
                        for t in range(NT):
                            for a in range(2):
                                job = f"near_v{t}{a}"
                                G.wait_filled(dve, job)
                                mask = table["chunk_causal"][:].unsqueeze(1).to_broadcast([P, 4, P])
                                G.is_emptied(dve.tensor_tensor(qk_near[:, t, a:GH:2, :],
                                                               G.tile(job)[:].rearrange("p (h t) -> p h t", t=P), mask, ALU.mult), job)
                        yield
                        for t in range(NT):
                            if t:
                                G.wait_filled(dve, f"read{t - 1}")
                            for i in range(2):
                                job = f"far{t}{i}"
                                G.wait_filled(dve, job)
                                mask = table["group_chunk"][:].unsqueeze(1).unsqueeze(1).to_broadcast([P, NB, 2, GRP])
                                G.is_emptied(dve.tensor_tensor(far[:, i:GH:2, :].rearrange("p h (g t) -> p h g t", t=GRP),
                                                               G.tile(job)[:].rearrange("p (h g t) -> p h g t", g=2, t=GRP), mask, ALU.mult), job)
                            job = f"read{t}"
                            G.wait_filled(dve, job)
                            G.is_emptied(dve.tensor_tensor(og[:, t, :], G.tile(job)[:, 0:D], den[:, t, :], ALU.mult), job)
                        G.wait_emptied(dve, "read0")
                        G.wait_emptied(dve, "read1")
                        heads = og[:].rearrange("p t (h v) -> p (t h) v", v=GDK)
                        step(dve.tensor_tensor(og_sq[:], og[:], og[:], ALU.mult))
                        step(dve.tensor_reduce(og_ms[:], og_sq[:].rearrange("p t (h v) -> p (t h) v", v=GDK), AX_X, ALU.add))
                        dve.tensor_scalar(og_ms[:], og_ms[:], 1.0 / GDK, EPS, ALU.mult, ALU.add).then_inc(S["og_ms_ready"], 1)
                        dve.wait_ge(S["og_rms_ready"], 1)
                        dve.tensor_tensor(heads, heads, og_rms[:].unsqueeze(2).to_broadcast([P, NT * GH, GDK]), ALU.mult).then_inc(S["og_ready"], 1)
                        yield

                    def hidden(e):
                        job = f"in{e}"
                        dve.wait_ge(S["tanh_g_ready"], e + 1)
                        step(dve.scalar_tensor_tensor(hid[:, e % 2, :], tanh_g[:, e % 2, :], 1.0, M.tile(job)[:, 0:T], ALU.add, ALU.mult))
                        M.is_emptied(dve.tensor_tensor(hid[:, e % 2, :], hid[:, e % 2, :], M.tile(job)[:, T:2 * T], ALU.mult), job)

                    def add_up(e):
                        job = f"out{e}"
                        M.wait_filled(dve, job)
                        if e:
                            M.wait_emptied(dve, f"out{e - 1}")
                        for t in range(NT):
                            out = M.tile(job)[:, t * D:(t + 1) * D]
                            if e == 0:
                                last = dve.tensor_scalar(y[:, t, :], out, mix[:, t, e:e + 1], None, ALU.mult)
                            else:
                                last = dve.scalar_tensor_tensor(y[:, t, :], out, mix[:, t, e:e + 1], y[:, t, :], ALU.mult, ALU.add)
                        M.is_emptied(last, job)

                    def moe():
                        yield
                        M.wait_emptied(dve, "route")
                        step(dve.tensor_scalar(score[:], score[:], 1.0, None, ALU.add))
                        step(dve.reciprocal(score[:], score[:]))
                        step(dve.tensor_tensor(sel[:], score[:], route_bias[:].unsqueeze(1).to_broadcast([P, NT, E]), ALU.add))
                        for t in range(NT):
                            last = dve.max(top8[:, t, :], sel[:, t, :])
                        step(last)
                        for t in range(NT):
                            last = dve.match_replace(sel_left[:, t, :], top8[:, t, :], sel[:, t, :], -3e38)
                        step(last)
                        step(dve.tensor_tensor(sel_left[:], sel_left[:], sel[:], ALU.not_equal))
                        step(dve.tensor_tensor(sel_left[:], sel_left[:], score[:], ALU.mult))
                        step(dve.tensor_reduce(mix_sum[:], sel_left[:], AX_X, ALU.add))
                        step(dve.reciprocal(mix_sum[:], mix_sum[:]))
                        for t in range(NT):
                            last = dve.tensor_scalar(mix[:, t, 0:E], sel_left[:, t, :], mix_sum[:, t:t + 1], 0.5 * ROUTE_SCALE, ALU.mult, ALU.mult)
                        step(last)
                        hidden(0)
                        yield
                        for e in range(1, E + 1):
                            hidden(e)
                            add_up(e - 1)
                            if e % 2 == 0:
                                yield
                        add_up(E)

                    run_stages(gsa(), moe())
                    dve.wait_ge(S["tanh_y_ready"], 1)
                    G.wait_emptied(dve, "attn")
                    step(dve.scalar_tensor_tensor(y[:], tanh_y[:], 1.0, y[:], ALU.add, ALU.mult))
                    step(dve.tensor_tensor(y[:], y[:], attn[:], ALU.mult))
                    dve.scalar_tensor_tensor(y[:], y[:], 0.5, xin[:], ALU.mult, ALU.add).then_inc(S["x1_ready"], 1)

            with nc.Block() as block:
                @block.sync
                def _(sync):
                    for s in per_batch:
                        sync.sem_clear(s)


def layer1(nc, x1, out, wa, wf, const, psum):
    LSTEP = LA // LF
    ctx = ExitStack()
    with ctx:
        def sb(name, *shape):
            return ctx.enter_context(nc.sbuf_tensor(name, list(shape), F32))

        def sem(name):
            return ctx.enter_context(nc.semaphore(name))

        table = {k: sb(f"layer1_{k}", P, v.shape[1]) for k, v in const.items()}
        ident = table["ident"]
        x_enc, x_loc = sb("x_enc", P, B * NT, D), sb("x_loc", P, B * NT, D)
        x_in = sb("x_in", P, B * NT, D)
        half_pow = sb("half_pow1", P, 2 * B * NT)
        e_w, e_col, e_row = sb("e_w", P, LSTEP, ENC_W), sb("e_col", P, LSTEP, 5 + NB), sb("e_row", P, LSTEP, 4, D)
        l_w, l_col, l_row = sb("l_w", P, LOC_W), sb("l_col", P, 2 + 2 * len(HBLK)), sb("l_row", P, D + 4 * FDH)
        wq, wkv, wo = e_w[:, :, 0:D], e_w[:, :, D:3 * D], e_w[:, :, 3 * D:4 * D]
        w1, w2 = e_w[:, :, 4 * D:4 * D + FF], e_w[:, :, 4 * D + FF:ENC_W].rearrange("p l (a n) -> p l a n", n=D)
        bq, ln_s, ln_b = e_col[:, :, 0], e_col[:, :, 1:3], e_col[:, :, 3:5]
        b1 = e_col[:, :, 5:5 + NB]
        bkv, bo, b2 = e_row[:, :, 0:2, :], e_row[:, :, 2, :], e_row[:, :, 3, :]
        at_wo, at_w1 = 3 * INNER, 3 * INNER + NB * D
        at_w2 = at_w1 + 2 * HID
        l_wqkv, l_wo = l_w[:, 0:at_wo], l_w[:, at_wo:at_w1].rearrange("p (a n) -> p a n", n=D)
        l_w1, l_w2 = l_w[:, at_w1:at_w2], l_w[:, at_w2:LOC_W].rearrange("p (a n) -> p a n", n=D)
        l_g, l_bias = l_col[:, 0:1], l_col[:, 1:2]
        l_b1 = l_col[:, 2:2 + 2 * len(HBLK)].rearrange("p (a n) -> p a n", a=2)
        l_b2, qk_scale = l_row[:, 0:D], l_row[:, D:D + 4 * FDH]
        rot = sb("l_rot", P, NT, 4, FDH)
        lnf_s, lnf_b = sb("lnf_s", P, D), sb("lnf_b", P, D)

        stats, moments = sb("stats1", P, B * NT, 6), sb("moments1", P, B * NT, 2)
        var_eps, rstd = sb("var_eps1", P, B * NT), sb("rstd1", P, B * NT)
        loads, first, root = sem("b_loads"), sem("b_first_step"), sem("b_root")
        pairs = [(table[k][:], const[k]) for k in table] + [
            (x_in[:], x1.rearrange("b (t p) d -> p (b t) d", p=P)),
            (lnf_s[:], wa["lnf_s"].partition_broadcast(P)), (lnf_b[:], wa["lnf_b"].partition_broadcast(P))]
        with nc.Block() as block:
            @block.sync
            def _(sync):
                for dst, src in pairs:
                    sync.dma_start(dst, src).then_inc(loads, 16)

            @block.gpsimd
            def _(pool):
                pool.memset(half_pow[:], -0.5).then_inc(root, 1)
                pool.wait_ge(root, 2)
                pool.tensor_tensor(rstd[:], var_eps[:], half_pow[:, 0:B * NT], ALU.pow).then_inc(root, 1)

            @block.vector
            def _(dve):
                step = Chain(dve, first)
                dve.wait_ge(loads, 16 * len(pairs))
                for n in range(B * NT):
                    last = dve.bn_stats(stats[:, n, :], x_in[:, n, :])
                step(last)
                for n in range(B * NT):
                    last = dve.bn_aggr(moments[:, n, :], stats[:, n, :])
                step(last)
                dve.tensor_scalar(var_eps[:], moments[:, :, 1], EPS, None, ALU.add).then_inc(root, 1)
                dve.wait_ge(root, 3)
                for n in range(B * NT):
                    last = dve.tensor_scalar(x_loc[:, n, :], x_in[:, n, :], moments[:, n, 0:1], rstd[:, n:n + 1], ALU.subtract, ALU.mult)
                step(last)
                pos = table["pos_emb"][:]
                for n in range(B):
                    dve.scalar_tensor_tensor(x_enc[:, NT * n:NT * (n + 1), :].rearrange("p t d -> p (t d)"),
                                             x_loc[:, NT * n:NT * (n + 1), :].rearrange("p t d -> p (t d)"), float(np.sqrt(D)), pos, ALU.mult, ALU.add)

        e_x, e_xb = sb("e_x", P, NT, D), sb("e_xb", P, NT, D)
        e_stats, e_mom = sb("e_stats", P, NT, 6), sb("e_mom", P, NT, 2)
        e_var, e_rstd = sb("e_var", P, NT), sb("e_rstd", P, NT)
        e_n, e_h = sb("e_n", P, NT, D), sb("e_h", P, T)
        q_neg, q_pos = sb("q_neg", P, T), sb("q_pos", P, T)
        kv1 = sb("kv1", P, NT, 2 * D + 1)
        k_neg = sb("k_neg", P, NT, D)
        kv_mat, k_mat = sb("kv_mat", P, D), sb("k_mat", P, D)
        e_rec, e_attn = sb("e_rec", P, T), sb("e_attn", P, T)
        e_ff = sb("e_ff", P, NB, T)

        l_x, l_xb = sb("l_x", P, NT, D), sb("l_xb", P, NT, D)
        l_h = sb("l_h", P, T)
        qk, sq, turned = sb("l_qk", P, NT, 2 * FH, FDH), sb("l_sq", P, NT, 2 * FH, FDH), sb("l_turned", P, NT, 2 * FH, FDH)
        norm2, rnorm = sb("norm2", P, NT, 2 * FH), sb("rnorm", P, NT, 2 * FH)
        v, v_prev = sb("l_v", P, NT, INNER), sb("v_prev", WIN, INNER)
        q_t, k_t = sb("l_q_t", P, NB, T), sb("l_k_t", P, NB, T)
        sim = [sb("sim0", P, FH, P), sb("sim1", P, FH, KEYS)]
        neg_max, sim_sum = sb("neg_max", P, NT, FH), sb("sim_sum", P, NT, FH)
        own_t, prev_t = sb("own_t", P, NT, FH, P), sb("prev_t", WIN, FH, P)
        o, o_t = sb("l_o", P, NT, INNER), sb("l_o_t", P, NB, T)
        l_s, l_n, l_h2 = sb("l_s", P, NT, D), sb("l_n", P, NT, D), sb("l_h2", P, T)
        l_stats, l_mom = sb("l_stats", P, NT, 6), sb("l_mom", P, NT, 2)
        l_var, l_rstd = sb("l_var", P, NT), sb("l_rstd", P, NT)
        gelu, l_ff = sb("l_gelu", P, len(HBLK), T), sb("l_ff", P, len(HBLK), T)

        e_jobs = [f"{n}.{i}" for i in range(LSTEP) for n in ("h", "q", "kv", "mat", "read", "out", "h2", "ff0", "ff1", "out2")]
        l_jobs = (["x_t", "q0", "k0", "v0", "q1", "k1", "v1", "vp", "qt0", "kt0", "qt1", "kt1", "s00", "s01", "s10", "s11", "s12", "s13",
                   "own00", "own01", "o0", "own10", "own11", "prev0", "prev1", "o1", "ot0", "ot1", "wo", "shift", "h2_t", "ff0", "ff1", "ff2", "w2"])
        En = Banks(ctx, nc, "enc", psum[0:3], e_jobs)
        Lo = Banks(ctx, nc, "loc", psum[3:8], l_jobs)
        e_names = ["x_copied", "var", "rstd", "normed", "q_min", "q_exp", "q_ready", "k_min", "k_exp", "k_ready", "xb"]
        l_names = ["x_copied", "squared0", "squared1", "norm2_0", "norm2_1", "rnorm0", "rnorm1", "scaled0", "scaled1", "turned0", "turned1",
                   "rotated0", "rotated1", "neg_max0", "neg_max1", "exp0", "exp1", "xb", "h_half", "var", "rstd", "normed", "gelu"]
        SE = {n: sem(f"e_{n}") for n in e_names}
        SL = {n: sem(f"l_{n}") for n in l_names}
        steps = {n: sem(f"b_{n}_step") for n in ("dve",)}
        per_batch = En.sems() + Lo.sems() + list(SE.values()) + list(SL.values()) + list(steps.values())

        w_loaded, w_step = sem("w_loaded"), sem("w_step")
        HALF = FDH // 2

        with nc.Block() as block:
            @block.gpsimd
            def _(pool):
                pool.memset(kv1[:, :, 2 * D:2 * D + 1], 1.0)

            @block.vector
            def _(dve):
                dve.memset(l_h[D // 2:D, 0:1], 0.0)

        with nc.Fori(0, LF) as lay:
            wpairs = [(e_w[:], wa["w"][bass.ds(lay, 1)]), (l_w[:], wf["w"][bass.ds(lay, 1)]),
                      (e_col[:], wa["col"][bass.ds(lay, 1)]), (l_col[:], wf["col"][bass.ds(lay, 1)]),
                      (e_row[:], wa["row"][bass.ds(lay, 1)][0].partition_broadcast(P)),
                      (l_row[:], wf["row"][bass.ds(lay, 1)][0].partition_broadcast(P))]
            wpairs = [(dst, src if len(src.shape) == len(dst.shape) else src[0]) for dst, src in wpairs]

            with nc.Block() as block:
                @block.sync
                def _(sync):
                    for dst, src in wpairs[0::2]:
                        sync.dma_start(dst, src).then_inc(w_loaded, 16)

                @block.scalar
                def _(act):
                    for dst, src in wpairs[1::2]:
                        act.dma_start(dst, src).then_inc(w_loaded, 16)

                @block.vector
                def _(dve):
                    dve.wait_ge(w_loaded, 16 * len(wpairs))
                    src = table["rotary"][:].rearrange("p (t a) -> p t a", t=NT)
                    sc = qk_scale
                    dst = rot[:].rearrange("p t a d -> p t (a d)")
                    for n, by in ((0, 8.0), (1, 1.0)):
                        cols = slice(n * 2 * FDH, (n + 1) * 2 * FDH)
                        for t in range(NT):
                            dve.scalar_tensor_tensor(dst[:, t, cols], src[:, t, cols], by, sc[:, cols], ALU.mult, ALU.mult).then_inc(w_step, 1)
                    dve.wait_ge(w_step, 2 * NT)

            with nc.Fori(0, B) as b:
                with nc.Block() as block:
                    @block.tensor
                    def _(pe):
                        def enc():
                            def turn(job, src):
                                En.wait_free(pe, job)
                                for t in range(NT):
                                    last = pe.transpose(En.tile(job)[:, t * P:(t + 1) * P], src[:, t, :], ident[:])
                                En.is_filled(last, job)

                            for i in range(LSTEP):
                                pe.wait_ge(SE["normed"], 2 * i + 1)
                                turn(f"h.{i}", e_n)
                                yield
                                En.wait_emptied(pe, f"h.{i}")
                                job = f"q.{i}"
                                En.wait_free(pe, job)
                                En.is_filled(pe.matmul(En.tile(job)[:, 0:T], wq[:, i, :], e_h[:], start=True, stop=True), job)
                                job = f"kv.{i}"
                                En.wait_free(pe, job)
                                for t in range(NT):
                                    last = pe.matmul(En.tile(job)[:, t * 2 * D:(t + 1) * 2 * D], e_h[:, t * P:(t + 1) * P],
                                                     wkv[:, i, :], start=True, stop=True)
                                En.is_filled(last, job)
                                yield
                                job = f"mat.{i}"
                                En.wait_free(pe, job)
                                pe.wait_ge(SE["k_ready"], i + 1)
                                for t in range(NT):
                                    last = pe.matmul(En.tile(job)[:, 0:D + 1], kv1[:, t, 0:D], kv1[:, t, D:2 * D + 1], start=(t == 0), stop=(t == NT - 1))
                                En.is_filled(last, job)
                                yield
                                job = f"read.{i}"
                                En.wait_free(pe, job)
                                En.wait_emptied(pe, f"mat.{i}")
                                pe.wait_ge(SE["q_ready"], i + 1)
                                pe.matmul(En.tile(job)[:, 0:T], kv_mat[:], q_pos[:], start=True, stop=True)
                                En.is_filled(pe.matmul(En.tile(job)[:, T:2 * T], k_mat[:], q_pos[:], start=True, stop=True), job)
                                yield
                                job = f"out.{i}"
                                En.wait_free(pe, job)
                                En.wait_emptied(pe, f"read.{i}")
                                for t in range(NT):
                                    last = pe.matmul(En.tile(job)[:, t * D:(t + 1) * D], e_attn[:, t * P:(t + 1) * P], wo[:, i, :], start=True, stop=True)
                                En.is_filled(last, job)
                                yield
                                pe.wait_ge(SE["normed"], 2 * i + 2)
                                turn(f"h2.{i}", e_n)
                                yield
                                En.wait_emptied(pe, f"h2.{i}")
                                for a in range(2):
                                    job = f"ff{a}.{i}"
                                    En.wait_free(pe, job)
                                    for n in range(2):
                                        blk = 2 * a + n
                                        last = pe.matmul(En.tile(job)[:, n * T:(n + 1) * T], w1[:, i, blk * P:(blk + 1) * P], e_h[:], start=True, stop=True)
                                    En.is_filled(last, job)
                                yield
                                job = f"out2.{i}"
                                En.wait_free(pe, job)
                                for a in range(2):
                                    En.wait_emptied(pe, f"ff{a}.{i}")
                                for t in range(NT):
                                    for n in range(NB):
                                        last = pe.matmul(En.tile(job)[:, t * D:(t + 1) * D], e_ff[:, n, t * P:(t + 1) * P], w2[:, i, n, :],
                                                         start=(n == 0), stop=(n == NB - 1))
                                En.is_filled(last, job)
                                yield

                        def loc():
                            Lo.wait_free(pe, "x_t")
                            pe.wait_ge(SL["x_copied"], 1)
                            for t in range(NT):
                                last = pe.transpose(Lo.tile("x_t")[:, t * P:(t + 1) * P], l_x[:, t, :], ident[:])
                            Lo.is_filled(last, "x_t")
                            yield
                            Lo.wait_emptied(pe, "x_t")
                            for t in range(NT):
                                for n, name in enumerate("qkv"):
                                    job = f"{name}{t}"
                                    Lo.wait_free(pe, job)
                                    Lo.is_filled(pe.matmul(Lo.tile(job)[:], l_h[:, t * P:(t + 1) * P], l_wqkv[:, n * INNER:(n + 1) * INNER],
                                                           start=True, stop=True), job)
                                if t:
                                    Lo.wait_free(pe, "vp")
                                    Lo.is_filled(pe.matmul(Lo.tile("vp")[0:WIN, :], l_h[:, WIN:P], l_wqkv[:, 2 * INNER:3 * INNER], start=True, stop=True), "vp")
                                yield
                            for t in range(NT):
                                pe.wait_ge(SL[f"rotated{t}"], 1)
                                for a, name in enumerate(("qt", "kt")):
                                    job = f"{name}{t}"
                                    Lo.wait_free(pe, job)
                                    for j in range(NB):
                                        src = qk[:, t, FH * a + 2 * j:FH * a + 2 * j + 2, :].rearrange("p h d -> p (h d)")
                                        last = pe.transpose(Lo.tile(job)[:, j * P:(j + 1) * P], src, ident[:])
                                    Lo.is_filled(last, job)
                                yield
                            for t in range(NT):
                                Lo.wait_emptied(pe, f"qt{t}")
                                Lo.wait_emptied(pe, f"kt{t}")
                                per = 4 if t == 0 else 2
                                keys = P if t == 0 else KEYS
                                for n in range(FH // per):
                                    job = f"s{t}{n}"
                                    Lo.wait_free(pe, job)
                                    rows = slice(FDH * (n % 2), FDH * (n % 2) + FDH)
                                    for i in range(per):
                                        j = (n // 2) * per + i
                                        last = pe.matmul(Lo.tile(job)[:, i * keys:(i + 1) * keys], q_t[rows, j, t * P:(t + 1) * P],
                                                         k_t[rows, j, (t + 1) * P - keys:(t + 1) * P], start=True, stop=True)
                                    Lo.is_filled(last, job)
                                yield
                            for t in range(NT):
                                pe.wait_ge(SL[f"exp{t}"], FH)
                                for a in range(2):
                                    job = f"own{t}{a}"
                                    Lo.wait_free(pe, job)
                                    for i in range(4):
                                        last = pe.transpose(Lo.tile(job)[:, i * P:(i + 1) * P], sim[t][:, 4 * a + i, t * WIN:t * WIN + P], ident[:])
                                    Lo.is_filled(last, job)
                                if t:
                                    for a in range(2):
                                        job = f"prev{a}"
                                        Lo.wait_free(pe, job)
                                        for i in range(4):
                                            last = pe.transpose(Lo.tile(job)[0:WIN, i * P:(i + 1) * P], sim[t][:, 4 * a + i, 0:WIN], ident[:])
                                        Lo.is_filled(last, job)
                                job = f"o{t}"
                                Lo.wait_free(pe, job)
                                Lo.wait_emptied(pe, f"v{t}")
                                if t:
                                    Lo.wait_emptied(pe, "vp")
                                for h in range(FH):
                                    if h % 4 == 0:
                                        Lo.wait_emptied(pe, f"own{t}{h // 4}")
                                        if t:
                                            Lo.wait_emptied(pe, f"prev{h // 4}")
                                    cols = slice(h * FDH, (h + 1) * FDH)
                                    last = pe.matmul(Lo.tile(job)[:, cols], own_t[:, t, h, :], v[:, t, cols], start=True, stop=(t == 0))
                                    if t:
                                        last = pe.matmul(Lo.tile(job)[:, cols], prev_t[:, h, :], v_prev[:, cols], start=False, stop=True)
                                Lo.is_filled(last, job)
                                yield
                            for t in range(NT):
                                job = f"ot{t}"
                                Lo.wait_free(pe, job)
                                Lo.wait_emptied(pe, f"o{t}")
                                for j in range(NB):
                                    last = pe.transpose(Lo.tile(job)[:, j * P:(j + 1) * P], o[:, t, j * P:(j + 1) * P], ident[:])
                                Lo.is_filled(last, job)
                            yield
                            Lo.wait_free(pe, "wo")
                            for t in range(NT):
                                Lo.wait_emptied(pe, f"ot{t}")
                                for j in range(NB):
                                    last = pe.matmul(Lo.tile("wo")[:, t * D:(t + 1) * D], o_t[:, j, t * P:(t + 1) * P], l_wo[:, j, :],
                                                     start=(j == 0), stop=(j == NB - 1))
                            Lo.is_filled(last, "wo")
                            yield
                            Lo.wait_free(pe, "shift")
                            Lo.wait_emptied(pe, "wo")
                            late = l_x[:, :, D // 2:D]
                            pe.matmul(Lo.tile("shift")[:, 0:D // 2], table["next_token"][:], late[:, 0, :], start=True, stop=True)
                            pe.matmul(Lo.tile("shift")[:, D // 2:D], table["next_token"][:], late[:, 1, :], start=True, stop=False)
                            Lo.is_filled(pe.matmul(Lo.tile("shift")[:, D // 2:D], table["next_tile"][:], late[:, 0, :], start=False, stop=True), "shift")
                            yield
                            Lo.wait_free(pe, "h2_t")
                            pe.wait_ge(SL["normed"], 1)
                            for t in range(NT):
                                last = pe.transpose(Lo.tile("h2_t")[:, t * P:(t + 1) * P], l_n[:, t, :], ident[:])
                            Lo.is_filled(last, "h2_t")
                            yield
                            Lo.wait_emptied(pe, "h2_t")
                            for n, (at, size) in enumerate(HBLK):
                                job = f"ff{n}"
                                Lo.wait_free(pe, job)
                                for a in range(2):
                                    last = pe.matmul(Lo.tile(job)[0:size, a * T:(a + 1) * T], l_w1[:, a * HID + at:a * HID + at + size], l_h2[:], start=True, stop=True)
                                Lo.is_filled(last, job)
                            yield
                            Lo.wait_free(pe, "w2")
                            for n in range(len(HBLK)):
                                Lo.wait_emptied(pe, f"ff{n}")
                            for t in range(NT):
                                for n, (at, size) in enumerate(HBLK):
                                    last = pe.matmul(Lo.tile("w2")[:, t * D:(t + 1) * D], l_ff[0:size, n, t * P:(t + 1) * P], l_w2[0:size, n, :],
                                                     start=(n == 0), stop=(n == len(HBLK) - 1))
                            Lo.is_filled(last, "w2")

                        run_stages(enc(), loc())

                    @block.scalar
                    def _(act):
                        def enc():
                            for i in range(LSTEP):
                                job = f"h.{i}"
                                En.wait_filled(act, job)
                                En.is_emptied(act.activation(e_h[:], En.tile(job)[:, 0:T], ACT.Identity, scale=ln_s[:, i, 0:1], bias=ln_b[:, i, 0:1]), job)
                                yield
                                job = f"q.{i}"
                                act.wait_ge(SE["q_min"], i + 1)
                                En.is_emptied(act.activation(q_pos[:], En.tile(job)[:, 0:T], ACT.Relu, bias=bq[:, i:i + 1]), job)
                                act.activation(q_neg[:], q_neg[:], ACT.Exp).then_inc(SE["q_exp"], 1)
                                act.wait_ge(SE["k_min"], i + 1)
                                act.activation(k_neg[:], k_neg[:], ACT.Exp).then_inc(SE["k_exp"], 1)
                                yield
                                yield
                                yield
                                yield
                                job = f"h2.{i}"
                                En.wait_filled(act, job)
                                En.is_emptied(act.activation(e_h[:], En.tile(job)[:, 0:T], ACT.Identity, scale=ln_s[:, i, 1:2], bias=ln_b[:, i, 1:2]), job)
                                yield
                                for a in range(2):
                                    job = f"ff{a}.{i}"
                                    En.wait_filled(act, job)
                                    for n in range(2):
                                        blk = 2 * a + n
                                        last = act.activation(e_ff[:, blk, :], En.tile(job)[:, n * T:(n + 1) * T], ACT.Relu, bias=b1[:, i, blk:blk + 1])
                                    En.is_emptied(last, job)
                                yield
                                yield

                        def loc():
                            Lo.wait_filled(act, "x_t")
                            act.activation(l_h[0:D // 2, :], Lo.tile("x_t")[0:D // 2, 0:T], ACT.Copy)
                            Lo.is_emptied(act.activation(l_h[D // 2:D, 1:T], Lo.tile("x_t")[D // 2:D, 0:T - 1], ACT.Copy), "x_t")
                            yield
                            for t in range(NT):
                                for a, name in enumerate("qk"):
                                    job = f"{name}{t}"
                                    Lo.wait_filled(act, job)
                                    Lo.is_emptied(act.activation(qk[:, t, FH * a:FH * (a + 1), :].rearrange("p h d -> p (h d)"), Lo.tile(job)[:], ACT.Copy), job)
                                for name in "qk":
                                    Lo.wait_emptied(act, f"{name}{t}")
                                act.activation(sq[:, t], qk[:, t], ACT.Square).then_inc(SL[f"squared{t}"], 1)
                                job = f"v{t}"
                                Lo.wait_filled(act, job)
                                Lo.is_emptied(act.activation(v[:, t, :], Lo.tile(job)[:], ACT.Copy), job)
                                if t:
                                    Lo.wait_filled(act, "vp")
                                    Lo.is_emptied(act.activation(v_prev[:], Lo.tile("vp")[0:WIN, :], ACT.Copy), "vp")
                                yield
                            for t in range(NT):
                                for name, dst in (("qt", q_t), ("kt", k_t)):
                                    job = f"{name}{t}"
                                    Lo.wait_filled(act, job)
                                    Lo.is_emptied(act.activation(dst[:, :, t * P:(t + 1) * P], Lo.tile(job)[:].rearrange("p (j t) -> p j t", t=P), ACT.Copy), job)
                                yield
                            for t in range(NT):
                                act.wait_ge(SL[f"neg_max{t}"], 1)
                                for h in range(FH):
                                    act.activation(sim[t][:, h, :], sim[t][:, h, :], ACT.Exp, bias=neg_max[:, t, h:h + 1],
                                                   accum_out=sim_sum[:, t, h:h + 1]).then_inc(SL[f"exp{t}"], 1)
                                yield
                            for t in range(NT):
                                job = f"own{t}0"
                                Lo.wait_filled(act, job)
                                Lo.is_emptied(act.activation(own_t[:, t, 0:4, :].rearrange("p h t -> p (h t)"), Lo.tile(job)[:], ACT.Copy), job)
                                if t:
                                    Lo.wait_filled(act, "prev0")
                                    Lo.is_emptied(act.activation(prev_t[:, 0:4, :].rearrange("p h t -> p (h t)"), Lo.tile("prev0")[0:WIN, :], ACT.Copy), "prev0")
                                yield
                            for t in range(NT):
                                job = f"ot{t}"
                                Lo.wait_filled(act, job)
                                Lo.is_emptied(act.activation(o_t[:, :, t * P:(t + 1) * P], Lo.tile(job)[:].rearrange("p (j t) -> p j t", t=P), ACT.Copy), job)
                            yield
                            yield
                            Lo.wait_filled(act, "shift")
                            Lo.is_emptied(act.activation(l_s[:, :, D // 2:D], Lo.tile("shift")[:, 0:D].rearrange("p (t d) -> p t d", t=NT), ACT.Copy), "shift")
                            yield
                            Lo.wait_filled(act, "h2_t")
                            Lo.is_emptied(act.activation(l_h2[:], Lo.tile("h2_t")[:, 0:T], ACT.Identity, scale=l_g, bias=l_bias), "h2_t")
                            yield
                            for n, (at, size) in enumerate(HBLK):
                                job = f"ff{n}"
                                Lo.wait_filled(act, job)
                                act.activation(gelu[0:size, n, :], Lo.tile(job)[0:size, T:2 * T], ACT.Gelu, bias=l_b1[0:size, 1, n:n + 1]).then_inc(SL["gelu"], 1)
                            yield

                        run_stages(enc(), loc())

                    @block.gpsimd
                    def _(pool):
                        def bias_first(dst, src, bias, done):
                            pool.tensor_tensor(dst[:], src[:], bias.unsqueeze(1).to_broadcast([P, NT, D]), ALU.add).then_inc(done, 1)

                        def enc():
                            pool.tensor_copy(e_x[:], x_enc[:, bass.ds(b * NT, NT), :]).then_inc(SE["x_copied"], 1)
                            pool.wait_ge(SE["x_copied"], 1)
                            for i in range(LSTEP):
                                for n, (bias, jobs) in enumerate(((bo, "out"), (b2, "out2"))):
                                    m = 2 * i + n
                                    pool.wait_ge(SE["var"], m + 1)
                                    pool.tensor_tensor(e_rstd[:], e_var[:], half_pow[:, 0:NT], ALU.pow).then_inc(SE["rstd"], 1)
                                    bias_first(e_xb, e_x, bias[:, i, :], SE["xb"])
                                    for _ in range(4):
                                        yield

                        def loc():
                            pool.tensor_copy(l_x[:], x_loc[:, bass.ds(b * NT, NT), :]).then_inc(SL["x_copied"], 1)
                            yield
                            for t in range(NT):
                                pool.wait_ge(SL[f"norm2_{t}"], 1)
                                pool.tensor_tensor(rnorm[:, t, :], norm2[:, t, :], half_pow[:, 0:2 * FH], ALU.pow).then_inc(SL[f"rnorm{t}"], 1)
                                pool.wait_ge(SL[f"scaled{t}"], 1)
                                for half in range(2):
                                    to, src = slice(half * HALF, (half + 1) * HALF), slice((1 - half) * HALF, (2 - half) * HALF)
                                    for a in range(2):
                                        hs = slice(FH * a, FH * (a + 1))
                                        by = rot[:, t, 2 * a + 1, to].unsqueeze(1).to_broadcast([P, FH, HALF])
                                        pool.tensor_tensor(turned[:, t, hs, to], qk[:, t, hs, src], by, ALU.mult).then_inc(SL[f"turned{t}"], 1)
                                yield
                            for _ in range(8):
                                yield

                            Lo.wait_emptied(pool, "wo")
                            pool.tensor_copy(l_s[:, :, 0:D // 2], l_x[:, :, 0:D // 2]).then_inc(SL["h_half"], 1)
                            yield
                            pool.wait_ge(SL["var"], 1)
                            pool.tensor_tensor(l_rstd[:], l_var[:], half_pow[:, 0:NT], ALU.pow).then_inc(SL["rstd"], 1)
                            bias_first(l_xb, l_x, l_b2, SL["xb"])

                        run_stages(enc(), loc())

                    @block.vector
                    def _(dve):
                        step = Chain(dve, steps["dve"])

                        def norm(x, stats, mom, var, rstd, out, S, n):
                            for t in range(NT):
                                last = dve.bn_stats(stats[:, t, :], x[:, t, :])
                            step(last)
                            for t in range(NT):
                                last = dve.bn_aggr(mom[:, t, :], stats[:, t, :])
                            step(last)
                            dve.tensor_scalar(var[:], mom[:, :, 1], EPS, None, ALU.add).then_inc(S["var"], 1)
                            dve.wait_ge(S["rstd"], n + 1)
                            for t in range(NT):
                                last = dve.tensor_scalar(out[:, t, :], x[:, t, :], mom[:, t, 0:1], rstd[:, t:t + 1], ALU.subtract, ALU.mult)
                            last.then_inc(S["normed"], 1)

                        def enc():
                            two = lambda a: a.rearrange("p (t d) -> p t d", t=NT)
                            for i in range(LSTEP):
                                if i == 0:
                                    dve.wait_ge(SE["x_copied"], 1)
                                else:
                                    En.wait_emptied(dve, f"out2.{i - 1}")
                                norm(e_x, e_stats, e_mom, e_var, e_rstd, e_n, SE, 2 * i)
                                yield
                                job = f"q.{i}"
                                En.wait_filled(dve, job)
                                dve.tensor_scalar(q_neg[:], En.tile(job)[:, 0:T], bq[:, i:i + 1], 0.0, ALU.add, ALU.min).then_inc(SE["q_min"], 1)
                                job = f"kv.{i}"
                                En.wait_filled(dve, job)
                                En.is_emptied(dve.tensor_tensor(kv1[:, :, 0:2 * D], En.tile(job)[:].rearrange("p (t n) -> p t n", t=NT),
                                                                bkv[:, i].rearrange("p a n -> p (a n)").unsqueeze(1).to_broadcast([P, NT, 2 * D]), ALU.add), job)
                                En.wait_emptied(dve, job)
                                dve.tensor_scalar(k_neg[:], kv1[:, :, 0:D], 0.0, None, ALU.min).then_inc(SE["k_min"], 1)
                                dve.wait_ge(SE["q_exp"], i + 1)
                                dve.tensor_tensor(q_pos[:], q_pos[:], q_neg[:], ALU.add).then_inc(SE["q_ready"], 1)
                                dve.wait_ge(SE["k_exp"], i + 1)
                                dve.scalar_tensor_tensor(kv1[:, :, 0:D], kv1[:, :, 0:D], 0.0, k_neg[:], ALU.max, ALU.add).then_inc(SE["k_ready"], 1)
                                yield
                                job = f"mat.{i}"
                                En.wait_filled(dve, job)
                                dve.tensor_tensor(kv_mat[:], En.tile(job)[:, 0:D], table["head_block"][:], ALU.mult)
                                En.is_emptied(dve.tensor_scalar(k_mat[:], table["head_block"][:], En.tile(job)[:, D:D + 1], None, ALU.mult), job)
                                yield
                                job = f"read.{i}"
                                En.wait_filled(dve, job)
                                step(dve.tensor_scalar(e_rec[:], En.tile(job)[:, T:2 * T], 1e-6, None, ALU.add))
                                step(dve.reciprocal(e_rec[:], e_rec[:]))
                                En.is_emptied(dve.tensor_tensor(e_attn[:], En.tile(job)[:, 0:T], e_rec[:], ALU.mult), job)
                                yield
                                job = f"out.{i}"
                                En.wait_filled(dve, job)
                                dve.wait_ge(SE["xb"], 2 * i + 1)
                                En.is_emptied(dve.tensor_tensor(e_x[:], two(En.tile(job)[:, 0:T]), e_xb[:], ALU.add), job)
                                En.wait_emptied(dve, job)
                                norm(e_x, e_stats, e_mom, e_var, e_rstd, e_n, SE, 2 * i + 1)
                                yield
                                yield
                                yield
                                job = f"out2.{i}"
                                En.wait_filled(dve, job)
                                dve.wait_ge(SE["xb"], 2 * i + 2)
                                dst = e_x[:] if i < LSTEP - 1 else x_enc[:, bass.ds(b * NT, NT), :]
                                En.is_emptied(dve.tensor_tensor(dst, two(En.tile(job)[:, 0:T]), e_xb[:], ALU.add), job)
                                yield

                        def loc():
                            yield
                            for t in range(NT):
                                dve.wait_ge(SL[f"squared{t}"], 1)
                                step(dve.tensor_reduce(norm2[:, t, :], sq[:, t], AX_X, ALU.add))
                                dve.tensor_scalar(norm2[:, t, :], norm2[:, t, :], 1e-24, None, ALU.max).then_inc(SL[f"norm2_{t}"], 1)
                                dve.wait_ge(SL[f"rnorm{t}"], 1)
                                dve.tensor_tensor(qk[:, t], qk[:, t], rnorm[:, t, :].unsqueeze(2).to_broadcast([P, 2 * FH, FDH]), ALU.mult).then_inc(SL[f"scaled{t}"], 1)
                                dve.wait_ge(SL[f"scaled{t}"], 1)
                                for a in range(2):
                                    hs = slice(FH * a, FH * (a + 1))
                                    last = dve.tensor_tensor(sq[:, t, hs, :], qk[:, t, hs, :], rot[:, t, 2 * a, :].unsqueeze(1).to_broadcast([P, FH, FDH]), ALU.mult)
                                step(last)
                                dve.wait_ge(SL[f"turned{t}"], 4)
                                dve.tensor_tensor(qk[:, t], sq[:, t], turned[:, t], ALU.add).then_inc(SL[f"rotated{t}"], 1)
                                yield
                            yield
                            yield
                            for t in range(NT):
                                per = 4 if t == 0 else 2
                                keys = P if t == 0 else KEYS
                                mask = table["window"][:, t * KEYS + KEYS - keys:(t + 1) * KEYS].unsqueeze(1).to_broadcast([P, per, keys])
                                for n in range(FH // per):
                                    job = f"s{t}{n}"
                                    Lo.wait_filled(dve, job)
                                    h0 = n % 2 + 2 * (n // 2) * per
                                    Lo.is_emptied(dve.tensor_tensor(sim[t][:, h0:h0 + 2 * per - 1:2, :],
                                                                    Lo.tile(job)[:, 0:per * keys].rearrange("p (h k) -> p h k", k=keys), mask, ALU.add), job)
                                for n in range(FH // per):
                                    Lo.wait_emptied(dve, f"s{t}{n}")
                                dve.tensor_reduce(neg_max[:, t, :], sim[t][:], AX_X, ALU.max, negate=True).then_inc(SL[f"neg_max{t}"], 1)
                                yield
                            for t in range(NT):
                                job = f"own{t}1"
                                Lo.wait_filled(dve, job)
                                Lo.is_emptied(dve.tensor_copy(own_t[:, t, 4:8, :].rearrange("p h t -> p (h t)"), Lo.tile(job)[:]), job)
                                if t:
                                    Lo.wait_filled(dve, "prev1")
                                    Lo.is_emptied(dve.tensor_copy(prev_t[:, 4:8, :].rearrange("p h t -> p (h t)"), Lo.tile("prev1")[0:WIN, :]), "prev1")
                                dve.wait_ge(SL[f"exp{t}"], FH)
                                step(dve.reciprocal(sim_sum[:, t, :], sim_sum[:, t, :]))
                                job = f"o{t}"
                                Lo.wait_filled(dve, job)
                                Lo.is_emptied(dve.tensor_tensor(o[:, t, :].rearrange("p (h d) -> p h d", d=FDH), Lo.tile(job)[:].rearrange("p (h d) -> p h d", d=FDH),
                                                                sim_sum[:, t, :].unsqueeze(2).to_broadcast([P, FH, FDH]), ALU.mult), job)
                                yield
                            yield
                            two = lambda a: a.rearrange("p (t d) -> p t d", t=NT)
                            Lo.wait_filled(dve, "wo")
                            Lo.is_emptied(dve.tensor_tensor(l_x[:], l_x[:], two(Lo.tile("wo")[:, 0:T]), ALU.add), "wo")
                            yield
                            yield
                            Lo.wait_emptied(dve, "shift")
                            dve.wait_ge(SL["h_half"], 1)
                            norm(l_s, l_stats, l_mom, l_var, l_rstd, l_n, SL, 0)
                            yield
                            for n, (at, size) in enumerate(HBLK):
                                job = f"ff{n}"
                                dve.wait_ge(SL["gelu"], n + 1)
                                Lo.is_emptied(dve.scalar_tensor_tensor(l_ff[0:size, n, :], Lo.tile(job)[0:size, 0:T], l_b1[0:size, 0, n:n + 1],
                                                                       gelu[0:size, n, :], ALU.add, ALU.mult), job)
                            yield
                            Lo.wait_filled(dve, "w2")
                            dve.wait_ge(SL["xb"], 1)
                            Lo.is_emptied(dve.tensor_tensor(x_loc[:, bass.ds(b * NT, NT), :], two(Lo.tile("w2")[:, 0:T]), l_xb[:], ALU.add), "w2")
                            Lo.wait_emptied(dve, "w2")

                        run_stages(enc(), loc())
                        En.wait_emptied(dve, f"out2.{LSTEP - 1}")

                with nc.Block() as block:
                    @block.sync
                    def _(sync):
                        for s in per_batch:
                            sync.sem_clear(s)

            with nc.Block() as block:
                @block.sync
                def _(sync):
                    for s in (w_loaded, w_step):
                        sync.sem_clear(s)

        fin = ctx.enter_context(nc.semaphore("final_step"))
        root2, tanh_done, stored = sem("final_root"), sem("final_tanh"), sem("stored")
        silu = sq[:].rearrange("p t h d -> p (t h d)").rearrange("p (n d) -> p n d", d=D)
        with nc.Block() as block:
            @block.scalar
            def _(act):
                act.activation(silu, x_loc[:], ACT.Tanh, scale=0.5).then_inc(tanh_done, 1)

            @block.gpsimd
            def _(pool):
                pool.wait_ge(root2, 1)
                pool.tensor_tensor(rstd[:], var_eps[:], half_pow[:, 0:B * NT], ALU.pow).then_inc(root2, 1)

            @block.vector
            def _(dve):
                step = Chain(dve, fin)
                for n in range(B * NT):
                    last = dve.bn_stats(stats[:, n, :], x_enc[:, n, :])
                step(last)
                for n in range(B * NT):
                    last = dve.bn_aggr(moments[:, n, :], stats[:, n, :])
                step(last)
                dve.tensor_scalar(var_eps[:], moments[:, :, 1], EPS, None, ALU.add).then_inc(root2, 1)
                dve.wait_ge(root2, 2)
                for n in range(B * NT):
                    last = dve.tensor_scalar(x_enc[:, n, :], x_enc[:, n, :], moments[:, n, 0:1], rstd[:, n:n + 1], ALU.subtract, ALU.mult)
                step(last)
                wide = [P, B * NT, D]
                step(dve.tensor_tensor(x_enc[:], x_enc[:], lnf_s[:].unsqueeze(1).to_broadcast(wide), ALU.mult))
                step(dve.tensor_tensor(x_enc[:], x_enc[:], lnf_b[:].unsqueeze(1).to_broadcast(wide), ALU.add))
                dve.wait_ge(tanh_done, 1)
                step(dve.scalar_tensor_tensor(x_loc[:], silu, 1.0, x_loc[:], ALU.add, ALU.mult))
                step(dve.tensor_tensor(x_loc[:], x_loc[:], x_enc[:], ALU.mult))
                step(dve.scalar_tensor_tensor(x_in[:], x_loc[:], 0.5, x_in[:], ALU.mult, ALU.add))

            @block.sync
            def _(sync):
                sync.wait_ge(fin, 8)
                sync.dma_start(out.rearrange("b (t p) d -> p (b t) d", p=P), x_in[:]).then_inc(stored, 16)
                sync.wait_ge(stored, 16)


ENC_W, LOC_W = 4 * D + 2 * FF, 3 * INNER + NB * D + 2 * HID + len(HBLK) * D
ATTN0 = ("Wq", "Wk", "Wv", "Wf1", "Wf2", "Wg1", "Wg2", "Wo", "norm_w")
ATTN1 = ("Wq", "bq", "Wk", "bk", "Wv", "bv", "Wo", "bo", "W1", "b1", "W2", "b2", "ln1_s", "ln1_b", "ln2_s", "ln2_b", "lnf_s", "lnf_b")
FFN1 = ("wqkv", "q_scale", "k_scale", "wo", "ln_g", "ln_b", "w1", "b1", "w2", "b2")


def build(nc, x, w0, attn1, ffn1, tables0, tables1, x1, out):
    with ExitStack() as ctx:
        psum = [ctx.enter_context(nc.psum_tensor(f"bank{i}", [P, 512], F32)) for i in range(8)]
        layer0(nc, x, x1, w0, tables0, psum)
        layer1(nc, x1, out, attn1, ffn1, tables1, psum)


def lay_out_experts(a):
    gate = np.concatenate([a["L0_ffn_w_gate"], a["L0_ffn_shared_gate_w"][None]])
    up = np.concatenate([a["L0_ffn_w_up"], a["L0_ffn_shared_up_w"][None]])
    down = np.concatenate([a["L0_ffn_w_down"], a["L0_ffn_shared_down_w"][None]])
    return {"w_in": np.stack([gate, up], axis=1).transpose(3, 0, 1, 2),
            "w_down": down.transpose(2, 0, 1),
            "gate_w": a["L0_ffn_gate_w"].T, "expert_bias": a["L0_ffn_expert_bias"]}


def lay_out_layer1(a):
    e = {k: a[f"L1_attn_{k}"] for k in ATTN1}
    f = {k: a[f"L1_ffn_{k}"] for k in FFN1}
    step = LA // LF
    rows = lambda m: m.reshape(LA, -1, P, m.shape[-1]).transpose(0, 2, 1, 3).reshape(LA, P, -1)
    w = np.concatenate([e["Wq"], e["Wk"], e["Wv"], e["Wo"], e["W1"], rows(e["W2"])], axis=-1)
    col = np.concatenate([np.stack([e[k] for k in ("bq", "ln1_s", "ln2_s", "ln1_b", "ln2_b")], axis=-1),
                          e["b1"].reshape(LA, NB, P).transpose(0, 2, 1)], axis=-1)
    row = np.stack([e[k] for k in ("bk", "bv", "bo", "b2")], axis=1)
    enc = {"w": w.reshape(LF, step, P, -1).transpose(0, 2, 1, 3), "col": col.reshape(LF, step, P, -1).transpose(0, 2, 1, 3),
           "row": row.reshape(LF, step, 4, D), "lnf_s": e["lnf_s"], "lnf_b": e["lnf_b"]}
    pad = len(HBLK) * P - HID
    filled = lambda m, axis: np.concatenate([m, np.zeros([pad if n == axis else s for n, s in enumerate(m.shape)], m.dtype)], axis=axis)
    w = np.concatenate([f["wqkv"], f["wo"].reshape(LF, NB, P, D).transpose(0, 2, 1, 3).reshape(LF, P, -1), f["w1"],
                        filled(f["w2"], 1).reshape(LF, len(HBLK), P, D).transpose(0, 2, 1, 3).reshape(LF, P, -1)], axis=-1)
    b1 = filled(f["b1"].reshape(LF, 2, HID), 2).reshape(LF, 2 * len(HBLK), P).transpose(0, 2, 1)
    swap = lambda m: np.concatenate([m[:, FDH // 2:], m[:, :FDH // 2]], axis=-1)
    loc = {"w": w, "col": np.concatenate([f["ln_g"][..., None], f["ln_b"][..., None], b1], axis=-1),
           "row": np.concatenate([f["b2"], f["q_scale"], swap(f["q_scale"]), f["k_scale"], swap(f["k_scale"])], axis=-1)}
    return enc, loc


def kernel(**inputs):
    import concourse.bacc as bacc
    from concourse.bass_utils import run_bass_kernel_spmd
    nc = bacc.Bacc("TRN2", target_bir_lowering=False, num_devices=1)
    arrays = {}

    def dram(name, a):
        arrays[name] = np.ascontiguousarray(a)
        return nc.dram_tensor(name, arrays[name].shape, F32, kind="ExternalInput").ap()

    x = dram("L0_attn_x", inputs["L0_attn_x"])
    w0 = {k: dram(f"L0_attn_{k}", inputs[f"L0_attn_{k}"]) for k in ATTN0}
    w0.update({k: dram(f"L0_ffn_{k}", v) for k, v in lay_out_experts({k: np.asarray(v) for k, v in inputs.items()}).items()})
    enc, loc = lay_out_layer1({k: np.asarray(v) for k, v in inputs.items()})
    attn1 = {k: dram(f"L1_attn_{k}", v) for k, v in enc.items()}
    ffn1 = {k: dram(f"L1_ffn_{k}", v) for k, v in loc.items()}
    tables0 = {k: dram(f"table0_{k}", v) for k, v in shape_constants().items()}
    tables1 = {k: dram(f"table1_{k}", v) for k, v in layer1_constants().items()}
    x1 = nc.dram_tensor("x1", (B, T, D), F32, kind="Internal").ap()
    out = nc.dram_tensor("out", (B, T, D), F32, kind="ExternalOutput").ap()
    build(nc, x, w0, attn1, ffn1, tables0, tables1, x1, out)
    r = run_bass_kernel_spmd(nc, [arrays], core_ids=[0])
    return r.results[0]["out"]
```

```python
import numpy as np
import concourse.bass as bass
from concourse import mybir
from contextlib import ExitStack

F32 = mybir.dt.float32
ALU = mybir.AluOpType
ACT = mybir.ActivationFunctionType
AX_X = mybir.AxisListType.X

P = 128
D = 128
B = 8
T = 256
NT = T // P
EPS = 1e-5

GH, GDK, GM = 8, 16, 64
HM = GH * GM
CH = 8
CT = P // CH
NCH = T // CH
GRP = 64
GC = GRP // CH
NG = T // GRP
NB = HM // P
FLOOR = -19.0

E, TOPK = 16, 8
ROUTE_SCALE = 2.826

LA, LH, LDK = 4, 16, 8
FF = 4 * D

LF, FH, FDH, WIN = 2, 8, 64, 64
INNER = FH * FDH
KEYS = WIN + P
HID = int(D * 4 * 2 / 3)
HBLK = [(0, 128), (128, 128), (256, HID - 256)]
NEG = -1e30


def shape_constants():
    i = np.arange(P)
    pos, chunk = i % CH, i // CH
    c = {}
    c["ident"] = np.eye(P)
    same = chunk[:, None] == chunk[None, :]
    mid = CH // 2 - 1
    up = same & (pos[:, None] > mid) & (pos[:, None] <= pos[None, :])
    down = same & (pos[:, None] <= mid) & (pos[:, None] > pos[None, :])
    c["from_mid"] = -(up.astype(float) - down.astype(float))
    span = np.zeros((T, NCH))
    for n in range(NCH):
        span[n * CH + mid + 1:(n + 1) * CH + mid + 1, n] = -1.0
    span = span.reshape(GC, NT, 2, CH, NCH).transpose(1, 2, 0, 3, 4)
    c["mid_to_mid"] = span.reshape(NT, P, NCH).transpose(1, 0, 2).reshape(P, -1)
    c["chunk_causal"] = (same & (i[:, None] <= i[None, :])).astype(float)
    c["chunk_of_token"] = (2 * (chunk % GC) + chunk // GC == np.arange(CT)[:, None]).T.astype(float)
    kc = np.arange(GDK * GC)
    c["group_chunk"] = (kc[:, None] % GC == (np.arange(GRP) // CH)[None, :]).astype(float)
    c["sum_chunks"] = (kc[:, None] // GC == np.arange(GDK)[None, :]).astype(float)
    rep = np.zeros((P, GH, P))
    for h in range(GH):
        for k in range(GDK):
            rep[h * GDK + k, h, k * GC:(k + 1) * GC] = 1.0
    c["spread_key"] = rep.reshape(P, -1)
    c["head_rows"] = (i[:, None] // GDK == np.arange(GH)[None, :]).astype(float)
    return {k: np.ascontiguousarray(v, dtype=np.float32) for k, v in c.items()}


def layer1_constants():
    i = np.arange(P)
    c = {}
    c["ident"] = np.eye(P)
    c["head_block"] = (i[:, None] // LDK == i[None, :] // LDK).astype(float)
    c["next_token"] = (i[:, None] + 1 == i[None, :]).astype(float)
    c["next_tile"] = ((i[:, None] == P - 1) & (i[None, :] == 0)).astype(float)
    half = D // 2
    f32 = np.float32
    freq = np.exp(np.arange(half, dtype=f32) * f32(-np.log(10000.0) / (half - 1))).astype(f32)
    ang = ((np.arange(T, dtype=f32) + f32(1.0))[:, None] * freq[None, :]).astype(f32)
    emb = np.concatenate([np.sin(ang), np.cos(ang)], axis=-1)
    c["pos_emb"] = emb.reshape(NT, P, D).transpose(1, 0, 2).reshape(P, -1)
    hi = np.arange(0, FDH, 2, dtype=f32)
    inv = (f32(1.0) / f32(10000.0) ** (hi / f32(FDH))).astype(f32)
    t = np.arange(T, dtype=f32)
    ang = (t[:, None] * inv[None, :]).astype(f32)
    base = ((hi + f32(0.4 * FDH)) / f32(1.4 * FDH)).astype(f32)
    power = ((t - T // 2) / f32(WIN // 2)).astype(f32)
    sc = (base[None, :] ** power[:, None]).astype(f32)
    cos, sin = np.cos(ang), np.sin(ang)
    dbl = lambda a, s=1.0: np.concatenate([s * a, a], axis=-1)
    rot = np.stack([dbl(cos * sc), dbl(sin * sc, -1.0), dbl(cos / sc), dbl(sin / sc, -1.0)], axis=1)
    c["rotary"] = rot.reshape(NT, P, 4 * FDH).transpose(1, 0, 2).reshape(P, -1)
    j = np.arange(KEYS) - WIN
    m = []
    for tt in range(NT):
        qi, kj = i[:, None] + tt * P, j[None, :] + tt * P
        seen = (kj >= 0) & (qi >= kj) & (qi <= kj + WIN) & (kj // WIN >= qi // WIN - 1)
        m.append(np.where(seen, 0.0, NEG))
    c["window"] = np.stack(m, axis=1).reshape(P, -1)
    return {k: np.ascontiguousarray(v, dtype=np.float32) for k, v in c.items()}


class Banks:

    def __init__(self, ctx, nc, name, banks, jobs):
        self.banks, self.jobs = banks, {job: n for n, job in enumerate(jobs)}
        assert len(self.jobs) == len(jobs)
        self.filled = [ctx.enter_context(nc.semaphore(f"{name}_filled{i}")) for i in range(len(banks))]
        self.emptied = [ctx.enter_context(nc.semaphore(f"{name}_emptied{i}")) for i in range(len(banks))]

    def at(self, job):
        n = self.jobs[job]
        return n % len(self.banks), n // len(self.banks)

    def tile(self, job):
        return self.banks[self.at(job)[0]]

    def wait_free(self, pe, job):
        b, use = self.at(job)
        if use:
            pe.wait_ge(self.emptied[b], use)

    def is_filled(self, ins, job):
        ins.then_inc(self.filled[self.at(job)[0]], 1)

    def wait_filled(self, eng, job):
        b, use = self.at(job)
        eng.wait_ge(self.filled[b], use + 1)

    def is_emptied(self, ins, job):
        ins.then_inc(self.emptied[self.at(job)[0]], 1)

    def wait_emptied(self, eng, job):
        b, use = self.at(job)
        eng.wait_ge(self.emptied[b], use + 1)

    def sems(self):
        return self.filled + self.emptied


class Chain:

    def __init__(self, eng, sem):
        self.eng, self.sem, self.count = eng, sem, 0

    def __call__(self, ins):
        ins.then_inc(self.sem, 1)
        self.count += 1
        self.eng.wait_ge(self.sem, self.count)


def run_stages(*streams):
    live = list(streams)
    while live:
        for s in list(live):
            if next(s, "end") == "end":
                live.remove(s)


def layer0(nc, x, x1, w, const, psum):
    ctx = ExitStack()
    with ctx:
        def sb(name, *shape):
            return ctx.enter_context(nc.sbuf_tensor(name, list(shape), F32))

        def sem(name):
            return ctx.enter_context(nc.semaphore(name))

        widths = {k: v.shape[1] for k, v in const.items()}
        table = {k: sb(f"table_{k}", P, n) for k, n in widths.items()}
        ident = table["ident"]
        w_q, w_k, w_kv = sb("w_q", P, D), sb("w_k", P, D), sb("w_kv", P, 2 * D)
        w_fg = sb("w_fg", P, 2 * GDK)
        w_f2, w_g2 = sb("w_f2", GDK, HM), sb("w_g2", GDK, D)
        w_out, norm_w = sb("w_out", P, D), sb("norm_w", P, 1)
        gate_t = sb("gate_t", P, E)
        route_bias = sb("route_bias", P, E)
        w_in_t = sb("w_in_t", P, E + 1, 2, P)
        w_down_t = sb("w_down_t", P, E + 1, D)
        half_pow = sb("half_pow", P, 2 * GH)

        xin = sb("xin", P, NT, D)
        stats, moments = sb("stats", P, NT, 6), sb("moments", P, NT, 2)
        var_eps, rstd = sb("var_eps", P, NT), sb("rstd", P, NT)
        xn, xn_t = sb("xn", P, NT, D), sb("xn_t", P, T)
        tanh_qk, qk_t = sb("tanh_qk", P, 2, T), sb("qk_t", P, 2, T)
        tanh_k = sb("tanh_k", P, NT, D)
        kv = sb("kv", P, NT, 2, D)
        fg1 = sb("fg1", GDK, 2, T)
        sp = sb("softplus", P, NT, HM)
        slot_w = sb("slot_w", P, NT, HM)
        from_mid, to_mid = sb("from_mid", P, NT, HM), sb("to_mid", P, NT, HM)
        exp_gate = sb("exp_gate", P, NT, D)
        chunk_decay = sb("chunk_decay", P, NB, GDK, NCH)
        kv_chunks = sb("kv_chunks", P, NT, 2, D, CT)
        q_heads = sb("q_heads", P, GH, T)
        qk_near = sb("qk_near", P, NT, GH, P)
        q_spread = sb("q_spread", P, GH, T)
        state = sb("state", P, 2, NB, 1 + GDK * NCH)
        k_state_t = sb("k_state_t", P, NG, HM)
        slots = sb("slots", P, NT, HM)
        slot_max, slot_sum = sb("slot_max", P, NT, GH), sb("slot_sum", P, NT, GH)
        slot_q = sb("slot_q", P, NT, HM)
        slot_w_t, slot_q_t = sb("slot_w_t", P, NT, NB, P), sb("slot_q_t", P, NT, NB, P)
        far = sb("far", P, GH, P)
        den, og, og_sq = sb("den", P, NT, D), sb("og", P, NT, D), sb("og_sq", P, NT, D)
        og_ms, og_rms = sb("og_ms", P, NT * GH), sb("og_rms", P, NT * GH)
        og_t, attn = sb("og_t", P, T), sb("attn", P, NT, D)
        score, sel, sel_left = sb("score", P, NT, E), sb("sel", P, NT, E), sb("sel_left", P, NT, E)
        top8, mix_sum = sb("top8", P, NT, TOPK), sb("mix_sum", P, NT)
        mix = sb("mix", P, NT, E + 1)
        tanh_g, hid = sb("tanh_g", P, 2, T), sb("hid", P, 2, T)
        y, tanh_y = sb("y", P, NT, D), sb("tanh_y", P, NT, D)

        loads, scaled = sem("loads"), sem("out_scaled")
        pairs = ([(table[k][:], const[k]) for k in table]
                 + [(w_q[:], w["Wq"]), (w_k[:], w["Wk"]), (w_kv[:, 0:D], w["Wk"]), (w_kv[:, D:2 * D], w["Wv"]),
                    (w_fg[:, 0:GDK], w["Wf1"]), (w_fg[:, GDK:2 * GDK], w["Wg1"]), (w_f2[:], w["Wf2"]),
                    (w_g2[:], w["Wg2"]), (w_out[:], w["Wo"]), (norm_w[:], w["norm_w"].rearrange("(p a) -> p a", a=1)),
                    (gate_t[:], w["gate_w"]), (route_bias[:], w["expert_bias"].partition_broadcast(P)),
                    (w_in_t[:], w["w_in"]), (w_down_t[:], w["w_down"])])

        with nc.Block() as block:
            @block.sync
            def _(sync):
                for dst, src in pairs:
                    sync.dma_start(dst, src).then_inc(loads, 16)

            @block.vector
            def _(dve):
                dve.wait_ge(loads, 16 * len(pairs))
                dve.tensor_scalar(w_out[:], w_out[:], norm_w[:], None, ALU.mult).then_inc(scaled, 1)

            @block.gpsimd
            def _(pool):
                pool.memset(state[:, :, :, 0:1], 0.0)
                pool.memset(chunk_decay[:, :, :, NCH - 1:NCH], 0.0)
                pool.memset(mix[:, :, E:E + 1], 0.5)
                pool.memset(half_pow[:], -0.5)

        g_jobs = (["x_t", "qk", "kv", "fg1", "f0", "f1", "gate", "mid0", "mid1", "decay"]
                  + [f"near{t}{a}" for t in range(NT) for a in range(2)]
                  + [f"spread{a}" for a in range(4)]
                  + [f"state{j}{r}" for j in range(NB) for r in range(2)]
                  + [f"state_t{g}" for g in range(NG)]
                  + ["slots0", "slots1", "w_t0", "w_t1", "q_t0", "q_t1"]
                  + [f"near_v{t}{a}" for t in range(NT) for a in range(2)]
                  + ["far00", "far01", "read0", "far10", "far11", "read1", "og_t", "attn"])
        m_jobs = ["route"]
        for e in range(E + 1):
            m_jobs += [f"in{e}"] + ([f"out{e - 1}"] if e else [])
        m_jobs += [f"out{E}"]
        G = Banks(ctx, nc, "gsa", psum[0:4], g_jobs)
        M = Banks(ctx, nc, "moe", psum[4:8], m_jobs)
        names = ["x_loaded", "var_ready", "rstd_ready", "xn_ready", "qk_tanh", "k_tanh", "qk_ready", "softplus_ready",
                 "exp_ready", "slot_w_ready", "chunks_ready", "q_heads_ready", "sub0", "sub1", "slot_exp0", "slot_exp1",
                 "slot_q0", "slot_q1", "og_ms_ready", "og_rms_ready", "og_ready", "tanh_g_ready", "tanh_y_ready", "x1_ready", "x1_stored"]
        S = {n: sem(f"a_{n}") for n in names}
        steps = {n: sem(f"a_{n}_step") for n in ("dve", "act")}
        per_batch = G.sems() + M.sems() + list(S.values()) + list(steps.values())

        with nc.Fori(0, B) as b:
            with nc.Block() as block:
                @block.sync
                def _(sync):
                    src = x[bass.ds(b, 1)].rearrange("a (c t g u) d -> (a t g) c u d", t=NT, g=2, u=CH)
                    for t in range(NT):
                        for g in range(2):
                            sync.dma_start(xin[g * GRP:(g + 1) * GRP, t, :], src[2 * t + g]).then_inc(S["x_loaded"], 16)
                    dst = x1[bass.ds(b, 1)].rearrange("a (c t g u) d -> (a t g) c u d", t=NT, g=2, u=CH)
                    sync.wait_ge(S["x1_ready"], 1)
                    for t in range(NT):
                        for g in range(2):
                            sync.dma_start(dst[2 * t + g], y[g * GRP:(g + 1) * GRP, t, :]).then_inc(S["x1_stored"], 16)
                    sync.wait_ge(S["x1_stored"], 16 * NG)

                @block.tensor
                def _(pe):
                    def gsa():
                        G.wait_free(pe, "x_t")
                        pe.wait_ge(S["xn_ready"], 1)
                        for t in range(NT):
                            last = pe.transpose(G.tile("x_t")[:, t * P:(t + 1) * P], xn[:, t, :], ident[:])
                        G.is_filled(last, "x_t")
                        yield
                        G.wait_emptied(pe, "x_t")
                        G.wait_free(pe, "qk")
                        pe.matmul(G.tile("qk")[:, 0:T], w_q[:], xn_t[:], start=True, stop=True)
                        G.is_filled(pe.matmul(G.tile("qk")[:, T:2 * T], w_k[:], xn_t[:], start=True, stop=True), "qk")
                        G.wait_free(pe, "kv")
                        for t in range(NT):
                            last = pe.matmul(G.tile("kv")[:, t * 2 * D:(t + 1) * 2 * D], xn_t[:, t * P:(t + 1) * P], w_kv[:], start=True, stop=True)
                        G.is_filled(last, "kv")
                        G.wait_free(pe, "fg1")
                        pe.matmul(G.tile("fg1")[0:GDK, 0:T], w_fg[:, 0:GDK], xn_t[:], start=True, stop=True)
                        G.is_filled(pe.matmul(G.tile("fg1")[0:GDK, T:2 * T], w_fg[:, GDK:2 * GDK], xn_t[:], start=True, stop=True), "fg1")
                        yield
                        G.wait_emptied(pe, "fg1")
                        for t in range(NT):
                            G.wait_free(pe, f"f{t}")
                            G.is_filled(pe.matmul(G.tile(f"f{t}")[:], fg1[:, 0, t * P:(t + 1) * P], w_f2[:], start=True, stop=True), f"f{t}")
                        G.wait_free(pe, "gate")
                        for t in range(NT):
                            last = pe.matmul(G.tile("gate")[:, t * P:(t + 1) * P], fg1[:, 1, t * P:(t + 1) * P], w_g2[:], start=True, stop=True)
                        G.is_filled(last, "gate")
                        yield
                        pe.wait_ge(S["softplus_ready"], 1)
                        for t in range(NT):
                            G.wait_free(pe, f"mid{t}")
                            G.is_filled(pe.matmul(G.tile(f"mid{t}")[:], table["from_mid"][:], sp[:, t, :], start=True, stop=True), f"mid{t}")
                        G.wait_free(pe, "decay")
                        for j in range(NB):
                            for t in range(NT):
                                last = pe.matmul(G.tile("decay")[:, j * NCH:(j + 1) * NCH], sp[:, t, j * P:(j + 1) * P],
                                                 table["mid_to_mid"][:, t * NCH:(t + 1) * NCH], start=(t == 0), stop=(t == NT - 1))
                        G.is_filled(last, "decay")
                        yield
                        G.wait_emptied(pe, "qk")
                        pe.wait_ge(S["qk_ready"], 1)
                        pe.wait_ge(S["q_heads_ready"], GH)
                        for t in range(NT):
                            for a in range(2):
                                job = f"near{t}{a}"
                                G.wait_free(pe, job)
                                G.is_filled(pe.matmul(G.tile(job)[:], qk_t[:, 1, t * P:(t + 1) * P],
                                                      q_heads[:, 4 * a:4 * a + 4, t * P:(t + 1) * P], start=True, stop=True), job)
                        for a in range(4):
                            job = f"spread{a}"
                            G.wait_free(pe, job)
                            for i in range(2):
                                h = 2 * a + i
                                last = pe.matmul(G.tile(job)[:, i * T:(i + 1) * T], table["spread_key"][:, h * P:(h + 1) * P],
                                                 qk_t[:, 0, :], start=True, stop=True)
                            G.is_filled(last, job)
                        yield
                        pe.wait_ge(S["slot_w_ready"], 1)
                        pe.wait_ge(S["chunks_ready"], NT)
                        for j in range(NB):
                            for r in range(2):
                                job = f"state{j}{r}"
                                G.wait_free(pe, job)
                                out = G.tile(job)[:].rearrange("p (k g) -> p k g", g=NG)
                                for i in range(2):
                                    h = 2 * j + i
                                    for t in range(NT):
                                        last = pe.matmul(out[GM * i:GM * (i + 1), :, 2 * t:2 * t + 2],
                                                         to_mid[:, t, h * GM:(h + 1) * GM],
                                                         kv_chunks[:, t, r, h * GDK:(h + 1) * GDK, :], start=True, stop=True)
                                G.is_filled(last, job)
                        yield
                        for g in range(NG):
                            job = f"state_t{g}"
                            G.wait_free(pe, job)
                            if g == 0:
                                for j in range(NB):
                                    G.wait_emptied(pe, f"state{j}0")
                            for j in range(NB):
                                last = pe.transpose(G.tile(job)[:, j * P:(j + 1) * P], state[:, 0, j, g:GDK * NCH:NG], ident[:])
                            G.is_filled(last, job)
                        for t in range(NT):
                            job = f"slots{t}"
                            G.wait_free(pe, job)
                            for a in range(2):
                                G.wait_emptied(pe, f"near{t}{a}")
                            for a in range(4):
                                G.wait_emptied(pe, f"spread{a}")
                            for g in range(2):
                                G.wait_emptied(pe, f"state_t{2 * t + g}")
                            for h in range(GH):
                                cols = slice(h * GM, (h + 1) * GM)
                                for i in range(2):
                                    g = 2 * t + i
                                    pe.matmul(G.tile(job)[GRP * i:GRP * (i + 1), cols], q_spread[:, h, g * GRP:(g + 1) * GRP],
                                              k_state_t[:, g, cols], start=True, stop=False)
                                last = pe.matmul(G.tile(job)[:, cols], qk_near[:, t, h, :], to_mid[:, t, cols], start=False, stop=True)
                            G.is_filled(last, job)
                        yield
                        for t in range(NT):
                            job = f"w_t{t}"
                            G.wait_free(pe, job)
                            for j in range(NB):
                                last = pe.transpose(G.tile(job)[:, j * P:(j + 1) * P], to_mid[:, t, j * P:(j + 1) * P], ident[:])
                            G.is_filled(last, job)
                        yield
                        for t in range(NT):
                            job = f"q_t{t}"
                            G.wait_free(pe, job)
                            pe.wait_ge(S[f"slot_q{t}"], 1)
                            for j in range(NB):
                                last = pe.transpose(G.tile(job)[:, j * P:(j + 1) * P], slot_q[:, t, j * P:(j + 1) * P], ident[:])
                            G.is_filled(last, job)
                        yield
                        for t in range(NT):
                            G.wait_emptied(pe, f"w_t{t}")
                            G.wait_emptied(pe, f"q_t{t}")
                            for a in range(2):
                                job = f"near_v{t}{a}"
                                G.wait_free(pe, job)
                                for i in range(4):
                                    h = 2 * i + a
                                    rows = slice(GM * (h % 2), GM * (h % 2) + GM)
                                    last = pe.matmul(G.tile(job)[:, i * P:(i + 1) * P], slot_w_t[rows, t, h // 2, :],
                                                     slot_q_t[rows, t, h // 2, :], start=True, stop=True)
                                G.is_filled(last, job)
                        yield
                        for j in range(NB):
                            G.wait_emptied(pe, f"state{j}1")
                        for t in range(NT):
                            for a in range(2):
                                job = f"far{t}{a}"
                                G.wait_free(pe, job)
                                rows = slice(GM * a, GM * (a + 1))
                                for j in range(NB):
                                    for i in range(2):
                                        last = pe.matmul(G.tile(job)[:, j * P + i * GRP:j * P + (i + 1) * GRP],
                                                         state[rows, 1, j, 2 * t + i:GDK * NCH:NG],
                                                         slot_q_t[rows, t, j, i * GRP:(i + 1) * GRP], start=True, stop=True)
                                G.is_filled(last, job)
                            job = f"read{t}"
                            G.wait_free(pe, job)
                            for i in range(2):
                                G.wait_emptied(pe, f"far{t}{i}")
                                G.wait_emptied(pe, f"near_v{t}{i}")
                            for h in range(GH):
                                cols = slice(h * GDK, (h + 1) * GDK)
                                pe.matmul(G.tile(job)[:, cols], qk_near[:, t, h, :], kv[:, t, 1, cols], start=True, stop=False)
                                last = pe.matmul(G.tile(job)[:, cols], far[:, h, :], table["sum_chunks"][:], start=False, stop=True)
                            G.is_filled(last, job)
                        yield
                        G.wait_free(pe, "og_t")
                        pe.wait_ge(S["og_ready"], 1)
                        for t in range(NT):
                            last = pe.transpose(G.tile("og_t")[:, t * P:(t + 1) * P], og[:, t, :], ident[:])
                        G.is_filled(last, "og_t")
                        G.wait_free(pe, "attn")
                        G.wait_emptied(pe, "og_t")
                        for t in range(NT):
                            last = pe.matmul(G.tile("attn")[:, t * D:(t + 1) * D], og_t[:, t * P:(t + 1) * P], w_out[:], start=True, stop=True)
                        G.is_filled(last, "attn")

                    def experts_in(e):
                        job = f"in{e}"
                        M.wait_free(pe, job)
                        pe.matmul(M.tile(job)[:, 0:T], w_in_t[:, e, 0, :], xn_t[:], start=True, stop=True)
                        M.is_filled(pe.matmul(M.tile(job)[:, T:2 * T], w_in_t[:, e, 1, :], xn_t[:], start=True, stop=True), job)

                    def experts_out(e):
                        job = f"out{e}"
                        M.wait_free(pe, job)
                        M.wait_emptied(pe, f"in{e}")
                        for t in range(NT):
                            last = pe.matmul(M.tile(job)[:, t * D:(t + 1) * D], hid[:, e % 2, t * P:(t + 1) * P], w_down_t[:, e, :], start=True, stop=True)
                        M.is_filled(last, job)

                    def moe():
                        yield
                        G.wait_emptied(pe, "x_t")
                        M.wait_free(pe, "route")
                        for t in range(NT):
                            last = pe.matmul(M.tile("route")[:, t * E:(t + 1) * E], xn_t[:, t * P:(t + 1) * P], gate_t[:], start=True, stop=True)
                        M.is_filled(last, "route")
                        experts_in(0)
                        yield
                        for e in range(1, E + 1):
                            experts_in(e)
                            experts_out(e - 1)
                            if e % 2 == 0:
                                yield
                        experts_out(E)

                    run_stages(gsa(), moe())

                @block.scalar
                def _(act):
                    step = Chain(act, steps["act"])

                    def gsa():
                        G.wait_filled(act, "x_t")
                        G.is_emptied(act.activation(xn_t[:], G.tile("x_t")[:, 0:T], ACT.Copy), "x_t")
                        yield
                        G.wait_filled(act, "qk")
                        act.activation(tanh_qk[:].rearrange("p r t -> p (r t)"), G.tile("qk")[:], ACT.Tanh, scale=0.5).then_inc(S["qk_tanh"], 1)
                        G.wait_filled(act, "kv")
                        tok = G.tile("kv")[:].rearrange("p (t r d) -> p t r d", t=NT, r=2)
                        act.activation(tanh_k[:], tok[:, :, 0, :], ACT.Tanh, scale=0.5).then_inc(S["k_tanh"], 1)
                        G.wait_filled(act, "fg1")
                        G.is_emptied(act.activation(fg1[:].rearrange("p r t -> p (r t)"), G.tile("fg1")[0:GDK, :], ACT.Copy), "fg1")
                        yield
                        for t in range(NT):
                            G.wait_emptied(act, f"f{t}")
                        step(act.activation(sp[:], sp[:], ACT.Exp, scale=-1.0))
                        G.wait_filled(act, "gate")
                        G.is_emptied(act.activation(exp_gate[:].rearrange("p t d -> p (t d)"), G.tile("gate")[:, 0:T], ACT.Exp, scale=-1.0), "gate")
                        act.activation(sp[:], sp[:], ACT.Ln, bias=1.0).then_inc(S["softplus_ready"], 1)
                        act.wait_ge(S["softplus_ready"], 1)
                        act.activation(slot_w[:], sp[:], ACT.Exp, scale=-1.0).then_inc(S["exp_ready"], 1)
                        yield
                        for t in range(NT):
                            G.wait_filled(act, f"mid{t}")
                            act.activation(from_mid[:, t, :], G.tile(f"mid{t}")[:], ACT.Exp)
                            G.is_emptied(act.activation(to_mid[:, t, :], G.tile(f"mid{t}")[:], ACT.Exp, scale=-1.0), f"mid{t}")
                        G.wait_filled(act, "decay")
                        for j in range(NB):
                            src = G.tile("decay")[:, j * NCH:j * NCH + NCH - 1].unsqueeze(1).to_broadcast([P, GDK, NCH - 1])
                            last = act.activation(chunk_decay[:, j, :, 0:NCH - 1], src, ACT.Exp)
                        G.is_emptied(last, "decay")
                        yield
                        yield
                        yield
                        for g in range(NG):
                            job = f"state_t{g}"
                            G.wait_filled(act, job)
                            G.is_emptied(act.activation(k_state_t[:, g, :], G.tile(job)[:], ACT.Copy), job)
                        yield
                        for t in range(NT):
                            act.wait_ge(S[f"sub{t}"], 1)
                            act.activation(slots[:, t, :], slots[:, t, :], ACT.Exp).then_inc(S[f"slot_exp{t}"], 1)
                        for t in range(NT):
                            job = f"w_t{t}"
                            G.wait_filled(act, job)
                            G.is_emptied(act.activation(slot_w_t[:, t].rearrange("p j t -> p (j t)"), G.tile(job)[:], ACT.Copy), job)
                        yield
                        for t in range(NT):
                            job = f"q_t{t}"
                            G.wait_filled(act, job)
                            G.is_emptied(act.activation(slot_q_t[:, t].rearrange("p j t -> p (j t)"), G.tile(job)[:], ACT.Copy), job)
                        yield
                        yield
                        yield
                        G.wait_filled(act, "og_t")
                        G.is_emptied(act.activation(og_t[:], G.tile("og_t")[:, 0:T], ACT.Copy), "og_t")
                        G.wait_filled(act, "attn")
                        G.is_emptied(act.activation(attn[:].rearrange("p t d -> p (t d)"), G.tile("attn")[:, 0:T], ACT.Copy), "attn")

                    def tanh(e):
                        job = f"in{e}"
                        M.wait_filled(act, job)
                        if e >= 2:
                            M.wait_emptied(act, f"in{e - 2}")
                        act.activation(tanh_g[:, e % 2, :], M.tile(job)[:, 0:T], ACT.Tanh, scale=0.5).then_inc(S["tanh_g_ready"], 1)

                    def moe():
                        yield
                        M.wait_filled(act, "route")
                        M.is_emptied(act.activation(score[:].rearrange("p t e -> p (t e)"), M.tile("route")[:, 0:NT * E], ACT.Exp, scale=-1.0), "route")
                        tanh(0)
                        yield
                        for e in range(1, E + 1):
                            tanh(e)
                            if e % 2 == 0:
                                yield

                    run_stages(gsa(), moe())
                    M.wait_emptied(act, f"out{E}")
                    act.activation(tanh_y[:], y[:], ACT.Tanh, scale=0.5).then_inc(S["tanh_y_ready"], 1)

                @block.gpsimd
                def _(pool):
                    pool.wait_ge(S["var_ready"], 1)
                    pool.tensor_tensor(rstd[:], var_eps[:], half_pow[:, 0:NT], ALU.pow).then_inc(S["rstd_ready"], 1)
                    pool.wait_ge(S["qk_ready"], 1)
                    for h in range(GH):
                        pool.tensor_scalar(q_heads[:, h, :], qk_t[:, 0, :], table["head_rows"][:, h:h + 1], None, ALU.mult).then_inc(S["q_heads_ready"], 1)
                    pool.wait_ge(S["og_ms_ready"], 1)
                    pool.tensor_tensor(og_rms[:], og_ms[:], half_pow[:], ALU.pow).then_inc(S["og_rms_ready"], 1)

                @block.vector
                def _(dve):
                    step = Chain(dve, steps["dve"])

                    def gsa():
                        dve.wait_ge(S["x_loaded"], 16 * NG)
                        for t in range(NT):
                            last = dve.bn_stats(stats[:, t, :], xin[:, t, :])
                        step(last)
                        for t in range(NT):
                            last = dve.bn_aggr(moments[:, t, :], stats[:, t, :])
                        step(last)
                        dve.tensor_scalar(var_eps[:], moments[:, :, 1], EPS, None, ALU.add).then_inc(S["var_ready"], 1)
                        dve.wait_ge(S["rstd_ready"], 1)
                        for t in range(NT):
                            last = dve.tensor_scalar(xn[:, t, :], xin[:, t, :], moments[:, t, 0:1], rstd[:, t:t + 1], ALU.subtract, ALU.mult)
                        last.then_inc(S["xn_ready"], 1)
                        yield
                        dve.wait_ge(S["qk_tanh"], 1)
                        qk_flat = qk_t[:].rearrange("p r t -> p (r t)")
                        G.is_emptied(dve.scalar_tensor_tensor(qk_flat, tanh_qk[:].rearrange("p r t -> p (r t)"), 1.0,
                                                              G.tile("qk")[:], ALU.add, ALU.mult), "qk")
                        G.wait_emptied(dve, "qk")
                        dve.tensor_scalar(qk_flat, qk_flat, 0.5, None, ALU.mult).then_inc(S["qk_ready"], 1)
                        dve.wait_ge(S["k_tanh"], 1)
                        tok = G.tile("kv")[:].rearrange("p (t r d) -> p t r d", t=NT, r=2)
                        dve.scalar_tensor_tensor(kv[:, :, 0, :], tanh_k[:], 1.0, tok[:, :, 0, :], ALU.add, ALU.mult)
                        G.is_emptied(dve.tensor_copy(kv[:, :, 1, :], tok[:, :, 1, :]), "kv")
                        yield
                        for t in range(NT):
                            G.wait_filled(dve, f"f{t}")
                            G.is_emptied(dve.tensor_scalar(sp[:, t, :], G.tile(f"f{t}")[:], FLOOR, None, ALU.max), f"f{t}")
                        G.wait_emptied(dve, "kv")
                        for t in range(NT):
                            for r in range(2):
                                mask = table["chunk_of_token"][:].unsqueeze(1).to_broadcast([P, D, CT])
                                last = dve.scalar_tensor_tensor(kv_chunks[:, t, r], kv[:, t, r, :].unsqueeze(2).to_broadcast([P, D, CT]),
                                                                0.5 if r == 0 else 1.0, mask, ALU.mult, ALU.mult)
                            last.then_inc(S["chunks_ready"], 1)
                        yield
                        dve.wait_ge(S["exp_ready"], 1)
                        step(dve.tensor_scalar(slot_w[:], slot_w[:], -1.0, 1.0, ALU.mult, ALU.add))
                        for t in range(NT):
                            G.wait_emptied(dve, f"mid{t}")
                            last = dve.tensor_tensor(to_mid[:, t, :], to_mid[:, t, :], slot_w[:, t, :], ALU.mult)
                        last.then_inc(S["slot_w_ready"], 1)
                        yield
                        for t in range(NT):
                            for a in range(2):
                                job = f"near{t}{a}"
                                G.wait_filled(dve, job)
                                mask = table["chunk_causal"][:].unsqueeze(1).to_broadcast([P, 4, P])
                                G.is_emptied(dve.tensor_tensor(qk_near[:, t, 4 * a:4 * a + 4, :],
                                                               G.tile(job)[:].rearrange("p (h t) -> p h t", t=P), mask, ALU.mult), job)
                        for a in range(4):
                            job = f"spread{a}"
                            G.wait_filled(dve, job)
                            mask = table["group_chunk"][:].unsqueeze(1).to_broadcast([P, 2 * NG, GRP])
                            G.is_emptied(dve.tensor_tensor(q_spread[:, 2 * a:2 * a + 2, :].rearrange("p h (g t) -> p (h g) t", t=GRP),
                                                           G.tile(job)[:].rearrange("p (g t) -> p g t", t=GRP), mask, ALU.mult), job)
                        yield
                        G.wait_emptied(dve, "decay")
                        for j in range(NB):
                            for r in range(2):
                                job = f"state{j}{r}"
                                G.wait_filled(dve, job)
                                G.is_emptied(dve.tensor_tensor_scan(state[:, r, j, 1:1 + GDK * NCH], G.tile(job)[:],
                                                                    chunk_decay[:, j].rearrange("p k c -> p (k c)"), 0.0, ALU.add, ALU.mult), job)
                        yield
                        for t in range(NT):
                            job = f"slots{t}"
                            G.wait_filled(dve, job)
                            G.is_emptied(dve.tensor_tensor(slots[:, t, :], G.tile(job)[:], from_mid[:, t, :], ALU.mult), job)
                            G.wait_emptied(dve, job)
                            heads = slots[:, t, :].rearrange("p (h m) -> p h m", m=GM)
                            step(dve.tensor_reduce(slot_max[:, t, :], heads, AX_X, ALU.max))
                            dve.tensor_tensor(heads, heads, slot_max[:, t, :].unsqueeze(2).to_broadcast([P, GH, GM]), ALU.subtract).then_inc(S[f"sub{t}"], 1)
                        yield
                        for t in range(NT):
                            dve.wait_ge(S[f"slot_exp{t}"], 1)
                            dve.tensor_tensor(slot_q[:, t, :], slots[:, t, :], from_mid[:, t, :], ALU.mult).then_inc(S[f"slot_q{t}"], 1)
                            step(dve.tensor_reduce(slot_sum[:, t, :], slots[:, t, :].rearrange("p (h m) -> p h m", m=GM), AX_X, ALU.add))
                        yield
                        G.wait_emptied(dve, "gate")
                        step(dve.scalar_tensor_tensor(den[:].rearrange("p t (h v) -> p (t h) v", v=GDK), exp_gate[:].rearrange("p t (h v) -> p (t h) v", v=GDK), 1.0,
                                                      slot_sum[:].rearrange("p t h -> p (t h)").unsqueeze(2).to_broadcast([P, NT * GH, GDK]), ALU.add, ALU.mult))
                        step(dve.reciprocal(den[:], den[:]))
                        yield
                        for t in range(NT):
                            for a in range(2):
                                job = f"near_v{t}{a}"
                                G.wait_filled(dve, job)
                                mask = table["chunk_causal"][:].unsqueeze(1).to_broadcast([P, 4, P])
                                G.is_emptied(dve.tensor_tensor(qk_near[:, t, a:GH:2, :],
                                                               G.tile(job)[:].rearrange("p (h t) -> p h t", t=P), mask, ALU.mult), job)
                        yield
                        for t in range(NT):
                            if t:
                                G.wait_filled(dve, f"read{t - 1}")
                            for i in range(2):
                                job = f"far{t}{i}"
                                G.wait_filled(dve, job)
                                mask = table["group_chunk"][:].unsqueeze(1).unsqueeze(1).to_broadcast([P, NB, 2, GRP])
                                G.is_emptied(dve.tensor_tensor(far[:, i:GH:2, :].rearrange("p h (g t) -> p h g t", t=GRP),
                                                               G.tile(job)[:].rearrange("p (h g t) -> p h g t", g=2, t=GRP), mask, ALU.mult), job)
                            job = f"read{t}"
                            G.wait_filled(dve, job)
                            G.is_emptied(dve.tensor_tensor(og[:, t, :], G.tile(job)[:, 0:D], den[:, t, :], ALU.mult), job)
                        G.wait_emptied(dve, "read0")
                        G.wait_emptied(dve, "read1")
                        heads = og[:].rearrange("p t (h v) -> p (t h) v", v=GDK)
                        step(dve.tensor_tensor(og_sq[:], og[:], og[:], ALU.mult))
                        step(dve.tensor_reduce(og_ms[:], og_sq[:].rearrange("p t (h v) -> p (t h) v", v=GDK), AX_X, ALU.add))
                        dve.tensor_scalar(og_ms[:], og_ms[:], 1.0 / GDK, EPS, ALU.mult, ALU.add).then_inc(S["og_ms_ready"], 1)
                        dve.wait_ge(S["og_rms_ready"], 1)
                        dve.tensor_tensor(heads, heads, og_rms[:].unsqueeze(2).to_broadcast([P, NT * GH, GDK]), ALU.mult).then_inc(S["og_ready"], 1)
                        yield

                    def hidden(e):
                        job = f"in{e}"
                        dve.wait_ge(S["tanh_g_ready"], e + 1)
                        step(dve.scalar_tensor_tensor(hid[:, e % 2, :], tanh_g[:, e % 2, :], 1.0, M.tile(job)[:, 0:T], ALU.add, ALU.mult))
                        M.is_emptied(dve.tensor_tensor(hid[:, e % 2, :], hid[:, e % 2, :], M.tile(job)[:, T:2 * T], ALU.mult), job)

                    def add_up(e):
                        job = f"out{e}"
                        M.wait_filled(dve, job)
                        if e:
                            M.wait_emptied(dve, f"out{e - 1}")
                        for t in range(NT):
                            out = M.tile(job)[:, t * D:(t + 1) * D]
                            if e == 0:
                                last = dve.tensor_scalar(y[:, t, :], out, mix[:, t, e:e + 1], None, ALU.mult)
                            else:
                                last = dve.scalar_tensor_tensor(y[:, t, :], out, mix[:, t, e:e + 1], y[:, t, :], ALU.mult, ALU.add)
                        M.is_emptied(last, job)

                    def moe():
                        yield
                        M.wait_emptied(dve, "route")
                        step(dve.tensor_scalar(score[:], score[:], 1.0, None, ALU.add))
                        step(dve.reciprocal(score[:], score[:]))
                        step(dve.tensor_tensor(sel[:], score[:], route_bias[:].unsqueeze(1).to_broadcast([P, NT, E]), ALU.add))
                        for t in range(NT):
                            last = dve.max(top8[:, t, :], sel[:, t, :])
                        step(last)
                        for t in range(NT):
                            last = dve.match_replace(sel_left[:, t, :], top8[:, t, :], sel[:, t, :], -3e38)
                        step(last)
                        step(dve.tensor_tensor(sel_left[:], sel_left[:], sel[:], ALU.not_equal))
                        step(dve.tensor_tensor(sel_left[:], sel_left[:], score[:], ALU.mult))
                        step(dve.tensor_reduce(mix_sum[:], sel_left[:], AX_X, ALU.add))
                        step(dve.reciprocal(mix_sum[:], mix_sum[:]))
                        for t in range(NT):
                            last = dve.tensor_scalar(mix[:, t, 0:E], sel_left[:, t, :], mix_sum[:, t:t + 1], 0.5 * ROUTE_SCALE, ALU.mult, ALU.mult)
                        step(last)
                        hidden(0)
                        yield
                        for e in range(1, E + 1):
                            hidden(e)
                            add_up(e - 1)
                            if e % 2 == 0:
                                yield
                        add_up(E)

                    run_stages(gsa(), moe())
                    dve.wait_ge(S["tanh_y_ready"], 1)
                    G.wait_emptied(dve, "attn")
                    step(dve.scalar_tensor_tensor(y[:], tanh_y[:], 1.0, y[:], ALU.add, ALU.mult))
                    step(dve.tensor_tensor(y[:], y[:], attn[:], ALU.mult))
                    dve.scalar_tensor_tensor(y[:], y[:], 0.5, xin[:], ALU.mult, ALU.add).then_inc(S["x1_ready"], 1)

            with nc.Block() as block:
                @block.sync
                def _(sync):
                    for s in per_batch:
                        sync.sem_clear(s)


def layer1(nc, x1, out, wa, wf, const, psum):
    LSTEP = LA // LF
    ctx = ExitStack()
    with ctx:
        def sb(name, *shape):
            return ctx.enter_context(nc.sbuf_tensor(name, list(shape), F32))

        def sem(name):
            return ctx.enter_context(nc.semaphore(name))

        table = {k: sb(f"layer1_{k}", P, v.shape[1]) for k, v in const.items()}
        ident = table["ident"]
        x_enc, x_loc = sb("x_enc", P, B * NT, D), sb("x_loc", P, B * NT, D)
        x_in = sb("x_in", P, B * NT, D)
        half_pow = sb("half_pow1", P, 2 * B * NT)
        e_w, e_col, e_row = sb("e_w", P, LSTEP, ENC_W), sb("e_col", P, LSTEP, 5 + NB), sb("e_row", P, LSTEP, 4, D)
        l_w, l_col, l_row = sb("l_w", P, LOC_W), sb("l_col", P, 2 + 2 * len(HBLK)), sb("l_row", P, D + 4 * FDH)
        wq, wkv, wo = e_w[:, :, 0:D], e_w[:, :, D:3 * D], e_w[:, :, 3 * D:4 * D]
        w1, w2 = e_w[:, :, 4 * D:4 * D + FF], e_w[:, :, 4 * D + FF:ENC_W].rearrange("p l (a n) -> p l a n", n=D)
        bq, ln_s, ln_b = e_col[:, :, 0], e_col[:, :, 1:3], e_col[:, :, 3:5]
        b1 = e_col[:, :, 5:5 + NB]
        bkv, bo, b2 = e_row[:, :, 0:2, :], e_row[:, :, 2, :], e_row[:, :, 3, :]
        at_wo, at_w1 = 3 * INNER, 3 * INNER + NB * D
        at_w2 = at_w1 + 2 * HID
        l_wqkv, l_wo = l_w[:, 0:at_wo], l_w[:, at_wo:at_w1].rearrange("p (a n) -> p a n", n=D)
        l_w1, l_w2 = l_w[:, at_w1:at_w2], l_w[:, at_w2:LOC_W].rearrange("p (a n) -> p a n", n=D)
        l_g, l_bias = l_col[:, 0:1], l_col[:, 1:2]
        l_b1 = l_col[:, 2:2 + 2 * len(HBLK)].rearrange("p (a n) -> p a n", a=2)
        l_b2, qk_scale = l_row[:, 0:D], l_row[:, D:D + 4 * FDH]
        rot = sb("l_rot", P, NT, 4, FDH)
        lnf_s, lnf_b = sb("lnf_s", P, D), sb("lnf_b", P, D)

        stats, moments = sb("stats1", P, B * NT, 6), sb("moments1", P, B * NT, 2)
        var_eps, rstd = sb("var_eps1", P, B * NT), sb("rstd1", P, B * NT)
        loads, first, root = sem("b_loads"), sem("b_first_step"), sem("b_root")
        pairs = [(table[k][:], const[k]) for k in table] + [
            (x_in[:], x1.rearrange("b (t p) d -> p (b t) d", p=P)),
            (lnf_s[:], wa["lnf_s"].partition_broadcast(P)), (lnf_b[:], wa["lnf_b"].partition_broadcast(P))]
        with nc.Block() as block:
            @block.sync
            def _(sync):
                for dst, src in pairs:
                    sync.dma_start(dst, src).then_inc(loads, 16)

            @block.gpsimd
            def _(pool):
                pool.memset(half_pow[:], -0.5).then_inc(root, 1)
                pool.wait_ge(root, 2)
                pool.tensor_tensor(rstd[:], var_eps[:], half_pow[:, 0:B * NT], ALU.pow).then_inc(root, 1)

            @block.vector
            def _(dve):
                step = Chain(dve, first)
                dve.wait_ge(loads, 16 * len(pairs))
                for n in range(B * NT):
                    last = dve.bn_stats(stats[:, n, :], x_in[:, n, :])
                step(last)
                for n in range(B * NT):
                    last = dve.bn_aggr(moments[:, n, :], stats[:, n, :])
                step(last)
                dve.tensor_scalar(var_eps[:], moments[:, :, 1], EPS, None, ALU.add).then_inc(root, 1)
                dve.wait_ge(root, 3)
                for n in range(B * NT):
                    last = dve.tensor_scalar(x_loc[:, n, :], x_in[:, n, :], moments[:, n, 0:1], rstd[:, n:n + 1], ALU.subtract, ALU.mult)
                step(last)
                pos = table["pos_emb"][:]
                for n in range(B):
                    dve.scalar_tensor_tensor(x_enc[:, NT * n:NT * (n + 1), :].rearrange("p t d -> p (t d)"),
                                             x_loc[:, NT * n:NT * (n + 1), :].rearrange("p t d -> p (t d)"), float(np.sqrt(D)), pos, ALU.mult, ALU.add)

        def encoder_buffers(i):
            n = lambda name, *shape: sb(f"e{i}_{name}", *shape)
            return dict(
                x=n("x", P, NT, D), xb=n("xb", P, NT, D), stats=n("stats", P, NT, 6), mom=n("mom", P, NT, 2),
                var=n("var", P, NT), rstd=n("rstd", P, NT), n=n("n", P, NT, D), h=n("h", P, T),
                q_neg=n("q_neg", P, T), q_pos=n("q_pos", P, T),
                kv1=n("kv1", P, NT, 2 * D + 1),
                k_neg=n("k_neg", P, NT, D), kv_mat=n("kv_mat", P, D), k_mat=n("k_mat", P, D),
                rec=n("rec", P, T), attn=n("attn", P, T), ff=n("ff", P, NB, T))

        EB = [encoder_buffers(i) for i in range(LSTEP)]

        l_x, l_x2, l_xb = sb("l_x", P, NT, D), sb("l_x2", P, NT, D), sb("l_xb", P, NT, D)
        l_h = sb("l_h", P, T)
        qk, sq, turned = sb("l_qk", P, NT, 2 * FH, FDH), sb("l_sq", P, NT, 2 * FH, FDH), sb("l_turned", P, NT, 2 * FH, FDH)
        norm2, rnorm = sb("norm2", P, NT, 2 * FH), sb("rnorm", P, NT, 2 * FH)
        v, v_prev = sb("l_v", P, NT, INNER), sb("v_prev", WIN, INNER)
        q_t, k_t = sb("l_q_t", P, NB, T), sb("l_k_t", P, NB, T)
        sim = [sb("sim0", P, FH, P), sb("sim1", P, FH, KEYS)]
        neg_max, sim_sum, sim_rec = sb("neg_max", P, NT, FH), sb("sim_sum", P, NT, FH), sb("sim_rec", P, NT, FH)
        own_t, prev_t = sb("own_t", P, NT, FH, P), sb("prev_t", WIN, FH, P)
        o_t = sb("l_o_t", P, NB, T)
        l_s, l_n, l_h2 = sb("l_s", P, NT, D), sb("l_n", P, NT, D), sb("l_h2", P, T)
        l_stats, l_mom = sb("l_stats", P, NT, 6), sb("l_mom", P, NT, 2)
        l_var, l_rstd = sb("l_var", P, NT), sb("l_rstd", P, NT)
        gelu, l_ff = sb("l_gelu", P, len(HBLK), T), sb("l_ff", P, len(HBLK), T)

        e_jobs = ["h", "q", "kv", "mat", "read", "out", "h2", "ff0", "ff1", "out2"]
        a_jobs = ["x_t", "q0", "k0", "v0", "q1", "k1", "v1", "vp", "qt0", "kt0", "qt1", "kt1", "s00", "s01", "s10", "s11", "s12", "s13"]
        f_jobs = ["own00", "own01", "o0", "own10", "own11", "prev0", "prev1", "o1", "wo", "shift", "h2_t", "ff0", "ff1", "ff2", "w2"]
        En = [Banks(ctx, nc, f"enc{i}", psum[2 * i:2 * i + 2], e_jobs) for i in range(LSTEP)]
        Lo = Banks(ctx, nc, "scores", psum[4:6], a_jobs)
        Ff = Banks(ctx, nc, "mix", psum[6:8], f_jobs)
        e_names = ["x_copied", "var", "rstd", "normed", "q_min", "q_exp", "q_ready", "k_min", "k_exp", "k_ready", "xb"]
        l_names = ["x_copied", "squared0", "squared1", "norm2_0", "norm2_1", "rnorm0", "rnorm1", "scaled0", "scaled1", "turned0", "turned1",
                   "rotated0", "rotated1", "neg_max0", "neg_max1", "exp0", "exp1", "divided"]
        f_names = ["x_copied", "x_mixed", "xb", "h_half", "var", "rstd", "normed", "gelu"]
        SE = [{n: sem(f"e{i}_{n}") for n in e_names} for i in range(LSTEP)]
        SL = {n: sem(f"l_{n}") for n in l_names}
        SF = {n: sem(f"f_{n}") for n in f_names}
        dve_step = sem("b_dve_step")
        per_batch = range(En[0].filled[0].num, dve_step.num + 1)

        w_loaded, w_step = sem("w_loaded"), sem("w_step")
        HALF = FDH // 2

        with nc.Block() as block:
            @block.gpsimd
            def _(pool):
                for e in EB:
                    pool.memset(e["kv1"][:, :, 2 * D:2 * D + 1], 1.0)

            @block.vector
            def _(dve):
                dve.memset(l_h[D // 2:D, 0:1], 0.0)

        with nc.Fori(0, LF) as lay:
            wpairs = [(e_w[:], wa["w"][bass.ds(lay, 1)]), (l_w[:], wf["w"][bass.ds(lay, 1)]),
                      (e_col[:], wa["col"][bass.ds(lay, 1)]), (l_col[:], wf["col"][bass.ds(lay, 1)]),
                      (e_row[:], wa["row"][bass.ds(lay, 1)][0].partition_broadcast(P)),
                      (l_row[:], wf["row"][bass.ds(lay, 1)][0].partition_broadcast(P))]
            wpairs = [(dst, src if len(src.shape) == len(dst.shape) else src[0]) for dst, src in wpairs]

            with nc.Block() as block:
                @block.sync
                def _(sync):
                    for dst, src in wpairs[0::2]:
                        sync.dma_start(dst, src).then_inc(w_loaded, 16)

                @block.scalar
                def _(act):
                    for dst, src in wpairs[1::2]:
                        act.dma_start(dst, src).then_inc(w_loaded, 16)

                @block.vector
                def _(dve):
                    dve.wait_ge(w_loaded, 16 * len(wpairs))
                    src = table["rotary"][:].rearrange("p (t a) -> p t a", t=NT)
                    sc = qk_scale
                    dst = rot[:].rearrange("p t a d -> p t (a d)")
                    for n, by in ((0, 8.0), (1, 1.0)):
                        cols = slice(n * 2 * FDH, (n + 1) * 2 * FDH)
                        for t in range(NT):
                            dve.scalar_tensor_tensor(dst[:, t, cols], src[:, t, cols], by, sc[:, cols], ALU.mult, ALU.mult).then_inc(w_step, 1)
                    dve.wait_ge(w_step, 2 * NT)

            def step_of(early, late):
                def streams(enc, scores, mix):
                    first = [] if early is None else [enc(0, early), scores(early)]
                    second = [] if late is None else [mix(late), enc(1, late)]
                    return second + first

                with nc.Block() as block:
                    @block.tensor
                    def _(pe):
                        def enc(i, b):
                            e = EB[i]
                            def turn(job, src):
                                En[i].wait_free(pe, job)
                                for t in range(NT):
                                    last = pe.transpose(En[i].tile(job)[:, t * P:(t + 1) * P], src[:, t, :], ident[:])
                                En[i].is_filled(last, job)

                            pe.wait_ge(SE[i]["normed"], 1)
                            turn("h", e["n"])
                            yield
                            En[i].wait_emptied(pe, "h")
                            job = "q"
                            En[i].wait_free(pe, job)
                            En[i].is_filled(pe.matmul(En[i].tile(job)[:, 0:T], wq[:, i, :], e["h"][:], start=True, stop=True), job)
                            job = "kv"
                            En[i].wait_free(pe, job)
                            for t in range(NT):
                                last = pe.matmul(En[i].tile(job)[:, t * 2 * D:(t + 1) * 2 * D], e["h"][:, t * P:(t + 1) * P],
                                                 wkv[:, i, :], start=True, stop=True)
                            En[i].is_filled(last, job)
                            yield
                            job = "mat"
                            En[i].wait_free(pe, job)
                            pe.wait_ge(SE[i]["k_ready"], 1)
                            for t in range(NT):
                                last = pe.matmul(En[i].tile(job)[:, 0:D + 1], e["kv1"][:, t, 0:D], e["kv1"][:, t, D:2 * D + 1], start=(t == 0), stop=(t == NT - 1))
                            En[i].is_filled(last, job)
                            yield
                            job = "read"
                            En[i].wait_free(pe, job)
                            En[i].wait_emptied(pe, "mat")
                            pe.wait_ge(SE[i]["q_ready"], 1)
                            pe.matmul(En[i].tile(job)[:, 0:T], e["kv_mat"][:], e["q_pos"][:], start=True, stop=True)
                            En[i].is_filled(pe.matmul(En[i].tile(job)[:, T:2 * T], e["k_mat"][:], e["q_pos"][:], start=True, stop=True), job)
                            yield
                            job = "out"
                            En[i].wait_free(pe, job)
                            En[i].wait_emptied(pe, "read")
                            for t in range(NT):
                                last = pe.matmul(En[i].tile(job)[:, t * D:(t + 1) * D], e["attn"][:, t * P:(t + 1) * P], wo[:, i, :], start=True, stop=True)
                            En[i].is_filled(last, job)
                            yield
                            pe.wait_ge(SE[i]["normed"], 2)
                            turn("h2", e["n"])
                            yield
                            En[i].wait_emptied(pe, "h2")
                            for a in range(2):
                                job = f"ff{a}"
                                En[i].wait_free(pe, job)
                                for n in range(2):
                                    blk = 2 * a + n
                                    last = pe.matmul(En[i].tile(job)[:, n * T:(n + 1) * T], w1[:, i, blk * P:(blk + 1) * P], e["h"][:], start=True, stop=True)
                                En[i].is_filled(last, job)
                            yield
                            job = "out2"
                            En[i].wait_free(pe, job)
                            for a in range(2):
                                En[i].wait_emptied(pe, f"ff{a}")
                            for t in range(NT):
                                for n in range(NB):
                                    last = pe.matmul(En[i].tile(job)[:, t * D:(t + 1) * D], e["ff"][:, n, t * P:(t + 1) * P], w2[:, i, n, :],
                                                     start=(n == 0), stop=(n == NB - 1))
                            En[i].is_filled(last, job)
                            yield

                        def scores(b):
                            Lo.wait_free(pe, "x_t")
                            pe.wait_ge(SL["x_copied"], 1)
                            for t in range(NT):
                                last = pe.transpose(Lo.tile("x_t")[:, t * P:(t + 1) * P], l_x[:, t, :], ident[:])
                            Lo.is_filled(last, "x_t")
                            yield
                            Lo.wait_emptied(pe, "x_t")
                            for t in range(NT):
                                for n, name in enumerate("qkv"):
                                    job = f"{name}{t}"
                                    Lo.wait_free(pe, job)
                                    Lo.is_filled(pe.matmul(Lo.tile(job)[:], l_h[:, t * P:(t + 1) * P], l_wqkv[:, n * INNER:(n + 1) * INNER],
                                                           start=True, stop=True), job)
                                if t:
                                    Lo.wait_free(pe, "vp")
                                    Lo.is_filled(pe.matmul(Lo.tile("vp")[0:WIN, :], l_h[:, WIN:P], l_wqkv[:, 2 * INNER:3 * INNER], start=True, stop=True), "vp")
                                yield
                            for t in range(NT):
                                pe.wait_ge(SL[f"rotated{t}"], 1)
                                for a, name in enumerate(("qt", "kt")):
                                    job = f"{name}{t}"
                                    Lo.wait_free(pe, job)
                                    for j in range(NB):
                                        src = qk[:, t, FH * a + 2 * j:FH * a + 2 * j + 2, :].rearrange("p h d -> p (h d)")
                                        last = pe.transpose(Lo.tile(job)[:, j * P:(j + 1) * P], src, ident[:])
                                    Lo.is_filled(last, job)
                                yield
                            for t in range(NT):
                                Lo.wait_emptied(pe, f"qt{t}")
                                Lo.wait_emptied(pe, f"kt{t}")
                                per = 4 if t == 0 else 2
                                keys = P if t == 0 else KEYS
                                for n in range(FH // per):
                                    job = f"s{t}{n}"
                                    Lo.wait_free(pe, job)
                                    rows = slice(FDH * (n % 2), FDH * (n % 2) + FDH)
                                    for i in range(per):
                                        j = (n // 2) * per + i
                                        last = pe.matmul(Lo.tile(job)[:, i * keys:(i + 1) * keys], q_t[rows, j, t * P:(t + 1) * P],
                                                         k_t[rows, j, (t + 1) * P - keys:(t + 1) * P], start=True, stop=True)
                                    Lo.is_filled(last, job)
                                yield

                        def mix(b):
                            def turn_scores(job, t, a, rows, keys):
                                Ff.wait_free(pe, job)
                                for n in range(4):
                                    last = pe.transpose(Ff.tile(job)[0:rows, n * P:(n + 1) * P], sim[t][:, 4 * a + n, keys], ident[:])
                                Ff.is_filled(last, job)

                            def attend(t):
                                job = f"o{t}"
                                Ff.wait_free(pe, job)
                                for h in range(FH):
                                    if h % 4 == 0:
                                        Ff.wait_emptied(pe, f"own{t}{h // 4}")
                                        if t:
                                            Ff.wait_emptied(pe, f"prev{h // 4}")
                                    cols, at = slice(h * FDH, (h + 1) * FDH), FDH * (h % 2)
                                    dst = Ff.tile(job)[at:at + FDH, (h // 2) * P:(h // 2 + 1) * P]
                                    last = pe.matmul(dst, v[:, t, cols], own_t[:, t, h, :], start=True, stop=(t == 0))
                                    if t:
                                        last = pe.matmul(dst, v_prev[:, cols], prev_t[:, h, :], start=False, stop=True)
                                Ff.is_filled(last, job)

                            turn_scores("own00", 0, 0, P, slice(0, P))
                            turn_scores("own01", 0, 1, P, slice(0, P))
                            yield
                            attend(0)
                            turn_scores("own10", 1, 0, P, slice(WIN, WIN + P))
                            turn_scores("own11", 1, 1, P, slice(WIN, WIN + P))
                            yield
                            turn_scores("prev0", 1, 0, WIN, slice(0, WIN))
                            turn_scores("prev1", 1, 1, WIN, slice(0, WIN))
                            yield
                            attend(1)
                            yield
                            Ff.wait_free(pe, "wo")
                            for t in range(NT):
                                Ff.wait_emptied(pe, f"o{t}")
                                for j in range(NB):
                                    last = pe.matmul(Ff.tile("wo")[:, t * D:(t + 1) * D], o_t[:, j, t * P:(t + 1) * P], l_wo[:, j, :],
                                                     start=(j == 0), stop=(j == NB - 1))
                            Ff.is_filled(last, "wo")
                            yield
                            Ff.wait_free(pe, "shift")
                            Ff.wait_emptied(pe, "wo")
                            late = l_x2[:, :, D // 2:D]
                            pe.matmul(Ff.tile("shift")[:, 0:D // 2], table["next_token"][:], late[:, 0, :], start=True, stop=True)
                            pe.matmul(Ff.tile("shift")[:, D // 2:D], table["next_token"][:], late[:, 1, :], start=True, stop=False)
                            Ff.is_filled(pe.matmul(Ff.tile("shift")[:, D // 2:D], table["next_tile"][:], late[:, 0, :], start=False, stop=True), "shift")
                            yield
                            Ff.wait_free(pe, "h2_t")
                            pe.wait_ge(SF["normed"], 1)
                            for t in range(NT):
                                last = pe.transpose(Ff.tile("h2_t")[:, t * P:(t + 1) * P], l_n[:, t, :], ident[:])
                            Ff.is_filled(last, "h2_t")
                            yield
                            Ff.wait_emptied(pe, "h2_t")
                            for n, (at, size) in enumerate(HBLK):
                                job = f"ff{n}"
                                Ff.wait_free(pe, job)
                                for a in range(2):
                                    last = pe.matmul(Ff.tile(job)[0:size, a * T:(a + 1) * T], l_w1[:, a * HID + at:a * HID + at + size], l_h2[:], start=True, stop=True)
                                Ff.is_filled(last, job)
                                yield
                            Ff.wait_free(pe, "w2")
                            for n in range(len(HBLK)):
                                Ff.wait_emptied(pe, f"ff{n}")
                            for t in range(NT):
                                for n, (at, size) in enumerate(HBLK):
                                    last = pe.matmul(Ff.tile("w2")[:, t * D:(t + 1) * D], l_ff[0:size, n, t * P:(t + 1) * P], l_w2[0:size, n, :],
                                                     start=(n == 0), stop=(n == len(HBLK) - 1))
                            Ff.is_filled(last, "w2")

                        run_stages(*streams(enc, scores, mix))

                    @block.scalar
                    def _(act):
                        def enc(i, b):
                            e = EB[i]
                            job = "h"
                            En[i].wait_filled(act, job)
                            En[i].is_emptied(act.activation(e["h"][:], En[i].tile(job)[:, 0:T], ACT.Identity, scale=ln_s[:, i, 0:1], bias=ln_b[:, i, 0:1]), job)
                            yield
                            job = "q"
                            act.wait_ge(SE[i]["q_min"], 1)
                            En[i].is_emptied(act.activation(e["q_pos"][:], En[i].tile(job)[:, 0:T], ACT.Relu, bias=bq[:, i:i + 1]), job)
                            act.activation(e["q_neg"][:], e["q_neg"][:], ACT.Exp).then_inc(SE[i]["q_exp"], 1)
                            act.wait_ge(SE[i]["k_min"], 1)
                            act.activation(e["k_neg"][:], e["k_neg"][:], ACT.Exp).then_inc(SE[i]["k_exp"], 1)
                            yield
                            yield
                            yield
                            yield
                            job = "h2"
                            En[i].wait_filled(act, job)
                            En[i].is_emptied(act.activation(e["h"][:], En[i].tile(job)[:, 0:T], ACT.Identity, scale=ln_s[:, i, 1:2], bias=ln_b[:, i, 1:2]), job)
                            yield
                            for a in range(2):
                                job = f"ff{a}"
                                En[i].wait_filled(act, job)
                                for n in range(2):
                                    blk = 2 * a + n
                                    last = act.activation(e["ff"][:, blk, :], En[i].tile(job)[:, n * T:(n + 1) * T], ACT.Relu, bias=b1[:, i, blk:blk + 1])
                                En[i].is_emptied(last, job)
                            yield
                            yield

                        def scores(b):
                            Lo.wait_filled(act, "x_t")
                            act.activation(l_h[0:D // 2, :], Lo.tile("x_t")[0:D // 2, 0:T], ACT.Copy)
                            Lo.is_emptied(act.activation(l_h[D // 2:D, 1:T], Lo.tile("x_t")[D // 2:D, 0:T - 1], ACT.Copy), "x_t")
                            yield
                            for t in range(NT):
                                for a, name in enumerate("qk"):
                                    job = f"{name}{t}"
                                    Lo.wait_filled(act, job)
                                    Lo.is_emptied(act.activation(qk[:, t, FH * a:FH * (a + 1), :].rearrange("p h d -> p (h d)"), Lo.tile(job)[:], ACT.Copy), job)
                                for name in "qk":
                                    Lo.wait_emptied(act, f"{name}{t}")
                                act.activation(sq[:, t], qk[:, t], ACT.Square).then_inc(SL[f"squared{t}"], 1)
                                if late is not None:
                                    Ff.wait_filled(act, f"o{t}")
                                job = f"v{t}"
                                Lo.wait_filled(act, job)
                                Lo.is_emptied(act.activation(v[:, t, :], Lo.tile(job)[:], ACT.Copy), job)
                                if t:
                                    Lo.wait_filled(act, "vp")
                                    Lo.is_emptied(act.activation(v_prev[:], Lo.tile("vp")[0:WIN, :], ACT.Copy), "vp")
                                yield
                            for t in range(NT):
                                for name, dst in (("qt", q_t), ("kt", k_t)):
                                    job = f"{name}{t}"
                                    Lo.wait_filled(act, job)
                                    Lo.is_emptied(act.activation(dst[:, :, t * P:(t + 1) * P], Lo.tile(job)[:].rearrange("p (j t) -> p j t", t=P), ACT.Copy), job)
                                yield
                            for t in range(NT):
                                act.wait_ge(SL[f"neg_max{t}"], 1)
                                for h in range(FH):
                                    act.activation(sim[t][:, h, :], sim[t][:, h, :], ACT.Exp, bias=neg_max[:, t, h:h + 1],
                                                   accum_out=sim_sum[:, t, h:h + 1]).then_inc(SL[f"exp{t}"], 1)
                                yield

                        def mix(b):
                            def keep(job, dst, rows):
                                Ff.wait_filled(act, job)
                                Ff.is_emptied(act.activation(dst, Ff.tile(job)[0:rows, :].rearrange("p (h t) -> p h t", t=P), ACT.Copy), job)

                            keep("own00", own_t[:, 0, 0:4, :], P)
                            yield
                            keep("o0", o_t[:, :, 0:P], P)
                            keep("own10", own_t[:, 1, 0:4, :], P)
                            yield
                            keep("prev0", prev_t[:, 0:4, :], WIN)
                            yield
                            keep("o1", o_t[:, :, P:T], P)
                            yield
                            yield
                            Ff.wait_filled(act, "shift")
                            Ff.is_emptied(act.activation(l_s[:, :, D // 2:D], Ff.tile("shift")[:, 0:D].rearrange("p (t d) -> p t d", t=NT), ACT.Copy), "shift")
                            yield
                            Ff.wait_filled(act, "h2_t")
                            Ff.is_emptied(act.activation(l_h2[:], Ff.tile("h2_t")[:, 0:T], ACT.Identity, scale=l_g, bias=l_bias), "h2_t")
                            yield
                            for n, (at, size) in enumerate(HBLK):
                                job = f"ff{n}"
                                Ff.wait_filled(act, job)
                                act.activation(gelu[0:size, n, :], Ff.tile(job)[0:size, T:2 * T], ACT.Gelu, bias=l_b1[0:size, 1, n:n + 1]).then_inc(SF["gelu"], 1)
                                yield

                        if early is not None:
                            act.activation(l_x[:], x_loc[:, bass.ds(early * NT, NT), :], ACT.Copy).then_inc(SL["x_copied"], 1)
                        if late is not None:
                            act.activation(EB[1]["x"][:], x_enc[:, bass.ds(late * NT, NT), :], ACT.Copy).then_inc(SE[1]["x_copied"], 1)
                        run_stages(*streams(enc, scores, mix))

                    @block.gpsimd
                    def _(pool):
                        def bias_first(dst, src, bias, done):
                            pool.tensor_tensor(dst[:], src[:], bias.unsqueeze(1).to_broadcast([P, NT, D]), ALU.add).then_inc(done, 1)

                        def enc(i, b):
                            e = EB[i]
                            pool.wait_ge(SE[i]["x_copied"], 1)
                            for n, (bias, jobs) in enumerate(((bo, "out"), (b2, "out2"))):
                                pool.wait_ge(SE[i]["var"], n + 1)
                                pool.tensor_tensor(e["rstd"][:], e["var"][:], half_pow[:, 0:NT], ALU.pow).then_inc(SE[i]["rstd"], 1)
                                bias_first(e["xb"], e["x"], bias[:, i, :], SE[i]["xb"])
                                for _ in range(4):
                                    yield

                        def scores(b):
                            yield
                            for t in range(NT):
                                for name in "qk":
                                    Lo.wait_emptied(pool, f"{name}{t}")
                                for half in range(2):
                                    to, src = slice(half * HALF, (half + 1) * HALF), slice((1 - half) * HALF, (2 - half) * HALF)
                                    for a in range(2):
                                        hs = slice(FH * a, FH * (a + 1))
                                        by = rot[:, t, 2 * a + 1, to].unsqueeze(1).to_broadcast([P, FH, HALF])
                                        pool.tensor_tensor(turned[:, t, hs, to], qk[:, t, hs, src], by, ALU.mult).then_inc(SL[f"turned{t}"], 1)
                                pool.wait_ge(SL[f"norm2_{t}"], 1)
                                pool.tensor_tensor(rnorm[:, t, :], norm2[:, t, :], half_pow[:, 0:2 * FH], ALU.pow).then_inc(SL[f"rnorm{t}"], 1)
                                yield

                        def mix(b):
                            for _ in range(4):
                                yield
                            Ff.wait_emptied(pool, "wo")
                            pool.tensor_copy(l_s[:, :, 0:D // 2], l_x2[:, :, 0:D // 2]).then_inc(SF["h_half"], 1)
                            yield
                            pool.wait_ge(SF["var"], 1)
                            pool.tensor_tensor(l_rstd[:], l_var[:], half_pow[:, 0:NT], ALU.pow).then_inc(SF["rstd"], 1)
                            bias_first(l_xb, l_x2, l_b2, SF["xb"])
                            yield

                        if late is not None:
                            pool.tensor_copy(l_x2[:], x_loc[:, bass.ds(late * NT, NT), :]).then_inc(SF["x_copied"], 1)
                        run_stages(*streams(enc, scores, mix))

                    @block.vector
                    def _(dve):
                        step = Chain(dve, dve_step)

                        def norm(x, stats, mom, var, rstd, out, S, n):
                            for t in range(NT):
                                last = dve.bn_stats(stats[:, t, :], x[:, t, :])
                            step(last)
                            for t in range(NT):
                                last = dve.bn_aggr(mom[:, t, :], stats[:, t, :])
                            step(last)
                            dve.tensor_scalar(var[:], mom[:, :, 1], EPS, None, ALU.add).then_inc(S["var"], 1)
                            dve.wait_ge(S["rstd"], n + 1)
                            for t in range(NT):
                                last = dve.tensor_scalar(out[:, t, :], x[:, t, :], mom[:, t, 0:1], rstd[:, t:t + 1], ALU.subtract, ALU.mult)
                            last.then_inc(S["normed"], 1)

                        def enc(i, b):
                            e = EB[i]
                            two = lambda a: a.rearrange("p (t d) -> p t d", t=NT)
                            dve.wait_ge(SE[i]["x_copied"], 1)
                            norm(e["x"], e["stats"], e["mom"], e["var"], e["rstd"], e["n"], SE[i], 0)
                            yield
                            job = "q"
                            En[i].wait_filled(dve, job)
                            dve.tensor_scalar(e["q_neg"][:], En[i].tile(job)[:, 0:T], bq[:, i:i + 1], 0.0, ALU.add, ALU.min).then_inc(SE[i]["q_min"], 1)
                            job = "kv"
                            En[i].wait_filled(dve, job)
                            En[i].is_emptied(dve.tensor_tensor(e["kv1"][:, :, 0:2 * D], En[i].tile(job)[:].rearrange("p (t n) -> p t n", t=NT),
                                                            bkv[:, i].rearrange("p a n -> p (a n)").unsqueeze(1).to_broadcast([P, NT, 2 * D]), ALU.add), job)
                            En[i].wait_emptied(dve, job)
                            dve.tensor_scalar(e["k_neg"][:], e["kv1"][:, :, 0:D], 0.0, None, ALU.min).then_inc(SE[i]["k_min"], 1)
                            dve.wait_ge(SE[i]["q_exp"], 1)
                            dve.tensor_tensor(e["q_pos"][:], e["q_pos"][:], e["q_neg"][:], ALU.add).then_inc(SE[i]["q_ready"], 1)
                            dve.wait_ge(SE[i]["k_exp"], 1)
                            dve.scalar_tensor_tensor(e["kv1"][:, :, 0:D], e["kv1"][:, :, 0:D], 0.0, e["k_neg"][:], ALU.max, ALU.add).then_inc(SE[i]["k_ready"], 1)
                            yield
                            job = "mat"
                            En[i].wait_filled(dve, job)
                            dve.tensor_tensor(e["kv_mat"][:], En[i].tile(job)[:, 0:D], table["head_block"][:], ALU.mult)
                            En[i].is_emptied(dve.tensor_scalar(e["k_mat"][:], table["head_block"][:], En[i].tile(job)[:, D:D + 1], None, ALU.mult), job)
                            yield
                            job = "read"
                            En[i].wait_filled(dve, job)
                            step(dve.tensor_scalar(e["rec"][:], En[i].tile(job)[:, T:2 * T], 1e-6, None, ALU.add))
                            step(dve.reciprocal(e["rec"][:], e["rec"][:]))
                            En[i].is_emptied(dve.tensor_tensor(e["attn"][:], En[i].tile(job)[:, 0:T], e["rec"][:], ALU.mult), job)
                            yield
                            job = "out"
                            En[i].wait_filled(dve, job)
                            dve.wait_ge(SE[i]["xb"], 1)
                            En[i].is_emptied(dve.tensor_tensor(e["x"][:], two(En[i].tile(job)[:, 0:T]), e["xb"][:], ALU.add), job)
                            En[i].wait_emptied(dve, job)
                            norm(e["x"], e["stats"], e["mom"], e["var"], e["rstd"], e["n"], SE[i], 1)
                            yield
                            yield
                            yield
                            job = "out2"
                            En[i].wait_filled(dve, job)
                            dve.wait_ge(SE[i]["xb"], 2)
                            En[i].is_emptied(dve.tensor_tensor(x_enc[:, bass.ds(b * NT, NT), :], two(En[i].tile(job)[:, 0:T]), e["xb"][:], ALU.add), job)
                            En[i].wait_emptied(dve, job)
                            yield

                        def scores(b):
                            yield
                            def rotate(t):
                                dve.wait_ge(SL[f"squared{t}"], 1)
                                step(dve.tensor_reduce(norm2[:, t, :], sq[:, t], AX_X, ALU.add))
                                dve.tensor_scalar(norm2[:, t, :], norm2[:, t, :], 1e-24, None, ALU.max).then_inc(SL[f"norm2_{t}"], 1)
                                for a in range(2):
                                    hs = slice(FH * a, FH * (a + 1))
                                    last = dve.tensor_tensor(sq[:, t, hs, :], qk[:, t, hs, :], rot[:, t, 2 * a, :].unsqueeze(1).to_broadcast([P, FH, FDH]), ALU.mult)
                                last.then_inc(SL[f"scaled{t}"], 1)

                            def finish(t):
                                dve.wait_ge(SL[f"scaled{t}"], 1)
                                dve.wait_ge(SL[f"turned{t}"], 4)
                                step(dve.tensor_tensor(sq[:, t], sq[:, t], turned[:, t], ALU.add))
                                dve.wait_ge(SL[f"rnorm{t}"], 1)
                                dve.tensor_tensor(qk[:, t], sq[:, t], rnorm[:, t, :].unsqueeze(2).to_broadcast([P, 2 * FH, FDH]), ALU.mult).then_inc(SL[f"rotated{t}"], 1)

                            rotate(0)
                            yield
                            rotate(1)
                            finish(0)
                            yield
                            finish(1)
                            yield
                            yield

                            def divide(t):
                                dve.wait_ge(SL[f"exp{t}"], FH)
                                step(dve.reciprocal(sim_rec[:, t, :], sim_sum[:, t, :]))
                                keys = P if t == 0 else KEYS
                                dve.tensor_tensor(sim[t][:], sim[t][:], sim_rec[:, t, :].unsqueeze(2).to_broadcast([P, FH, keys]), ALU.mult).then_inc(SL["divided"], 1)

                            for t in range(NT):
                                per = 4 if t == 0 else 2
                                keys = P if t == 0 else KEYS
                                mask = table["window"][:, t * KEYS + KEYS - keys:(t + 1) * KEYS].unsqueeze(1).to_broadcast([P, per, keys])
                                for n in range(FH // per):
                                    job = f"s{t}{n}"
                                    Lo.wait_filled(dve, job)
                                    h0 = n % 2 + 2 * (n // 2) * per
                                    Lo.is_emptied(dve.tensor_tensor(sim[t][:, h0:h0 + 2 * per - 1:2, :],
                                                                    Lo.tile(job)[:, 0:per * keys].rearrange("p (h k) -> p h k", k=keys), mask, ALU.add), job)
                                for n in range(FH // per):
                                    Lo.wait_emptied(dve, f"s{t}{n}")
                                dve.tensor_reduce(neg_max[:, t, :], sim[t][:], AX_X, ALU.max, negate=True).then_inc(SL[f"neg_max{t}"], 1)
                                if t:
                                    divide(0)
                                yield
                            divide(1)
                            dve.wait_ge(SL["divided"], NT)

                        def mix(b):
                            two = lambda a: a.rearrange("p (t d) -> p t d", t=NT)

                            def keep(job, dst, rows):
                                Ff.wait_filled(dve, job)
                                Ff.is_emptied(dve.tensor_copy(dst, Ff.tile(job)[0:rows, :].rearrange("p (h t) -> p h t", t=P)), job)

                            keep("own01", own_t[:, 0, 4:8, :], P)
                            yield
                            keep("own11", own_t[:, 1, 4:8, :], P)
                            yield
                            keep("prev1", prev_t[:, 4:8, :], WIN)
                            yield
                            yield
                            Ff.wait_filled(dve, "wo")
                            dve.wait_ge(SF["x_copied"], 1)
                            Ff.is_emptied(dve.tensor_tensor(l_x2[:], l_x2[:], two(Ff.tile("wo")[:, 0:T]), ALU.add), "wo")
                            yield
                            Ff.wait_emptied(dve, "shift")
                            dve.wait_ge(SF["h_half"], 1)
                            norm(l_s, l_stats, l_mom, l_var, l_rstd, l_n, SF, 0)
                            yield
                            yield
                            for n, (at, size) in enumerate(HBLK):
                                job = f"ff{n}"
                                dve.wait_ge(SF["gelu"], n + 1)
                                Ff.is_emptied(dve.scalar_tensor_tensor(l_ff[0:size, n, :], Ff.tile(job)[0:size, 0:T], l_b1[0:size, 0, n:n + 1],
                                                                       gelu[0:size, n, :], ALU.add, ALU.mult), job)
                                yield
                            Ff.wait_filled(dve, "w2")
                            dve.wait_ge(SF["xb"], 1)
                            Ff.is_emptied(dve.tensor_tensor(x_loc[:, bass.ds(b * NT, NT), :], two(Ff.tile("w2")[:, 0:T]), l_xb[:], ALU.add), "w2")
                            Ff.wait_emptied(dve, "w2")

                        if early is not None:
                            dve.tensor_copy(EB[0]["x"][:], x_enc[:, bass.ds(early * NT, NT), :]).then_inc(SE[0]["x_copied"], 1)
                        run_stages(*streams(enc, scores, mix))

                with nc.Block() as block:
                    @block.sync
                    def _(sync):
                        sync.sem_clear(per_batch)

            step_of(0, None)
            with nc.Fori(0, B - 1) as b:
                step_of(b + 1, b)
            step_of(None, B - 1)

            with nc.Block() as block:
                @block.sync
                def _(sync):
                    for s in (w_loaded, w_step):
                        sync.sem_clear(s)

        fin = ctx.enter_context(nc.semaphore("final_step"))
        root2, tanh_done, stored = sem("final_root"), sem("final_tanh"), sem("stored")
        silu = sq[:].rearrange("p t h d -> p (t h d)").rearrange("p (n d) -> p n d", d=D)
        with nc.Block() as block:
            @block.scalar
            def _(act):
                act.activation(silu, x_loc[:], ACT.Tanh, scale=0.5).then_inc(tanh_done, 1)

            @block.gpsimd
            def _(pool):
                pool.wait_ge(root2, 1)
                pool.tensor_tensor(rstd[:], var_eps[:], half_pow[:, 0:B * NT], ALU.pow).then_inc(root2, 1)

            @block.vector
            def _(dve):
                step = Chain(dve, fin)
                for n in range(B * NT):
                    last = dve.bn_stats(stats[:, n, :], x_enc[:, n, :])
                step(last)
                for n in range(B * NT):
                    last = dve.bn_aggr(moments[:, n, :], stats[:, n, :])
                step(last)
                dve.tensor_scalar(var_eps[:], moments[:, :, 1], EPS, None, ALU.add).then_inc(root2, 1)
                dve.wait_ge(root2, 2)
                for n in range(B * NT):
                    last = dve.tensor_scalar(x_enc[:, n, :], x_enc[:, n, :], moments[:, n, 0:1], rstd[:, n:n + 1], ALU.subtract, ALU.mult)
                step(last)
                wide = [P, B * NT, D]
                step(dve.tensor_tensor(x_enc[:], x_enc[:], lnf_s[:].unsqueeze(1).to_broadcast(wide), ALU.mult))
                step(dve.tensor_tensor(x_enc[:], x_enc[:], lnf_b[:].unsqueeze(1).to_broadcast(wide), ALU.add))
                dve.wait_ge(tanh_done, 1)
                step(dve.scalar_tensor_tensor(x_loc[:], silu, 1.0, x_loc[:], ALU.add, ALU.mult))
                step(dve.tensor_tensor(x_loc[:], x_loc[:], x_enc[:], ALU.mult))
                step(dve.scalar_tensor_tensor(x_in[:], x_loc[:], 0.5, x_in[:], ALU.mult, ALU.add))

            @block.sync
            def _(sync):
                sync.wait_ge(fin, 8)
                sync.dma_start(out.rearrange("b (t p) d -> p (b t) d", p=P), x_in[:]).then_inc(stored, 16)
                sync.wait_ge(stored, 16)


ENC_W, LOC_W = 4 * D + 2 * FF, 3 * INNER + NB * D + 2 * HID + len(HBLK) * D
ATTN0 = ("Wq", "Wk", "Wv", "Wf1", "Wf2", "Wg1", "Wg2", "Wo", "norm_w")
ATTN1 = ("Wq", "bq", "Wk", "bk", "Wv", "bv", "Wo", "bo", "W1", "b1", "W2", "b2", "ln1_s", "ln1_b", "ln2_s", "ln2_b", "lnf_s", "lnf_b")
FFN1 = ("wqkv", "q_scale", "k_scale", "wo", "ln_g", "ln_b", "w1", "b1", "w2", "b2")


def build(nc, x, w0, attn1, ffn1, tables0, tables1, x1, out):
    with ExitStack() as ctx:
        psum = [ctx.enter_context(nc.psum_tensor(f"bank{i}", [P, 512], F32)) for i in range(8)]
        layer0(nc, x, x1, w0, tables0, psum)
        layer1(nc, x1, out, attn1, ffn1, tables1, psum)


def lay_out_experts(a):
    gate = np.concatenate([a["L0_ffn_w_gate"], a["L0_ffn_shared_gate_w"][None]])
    up = np.concatenate([a["L0_ffn_w_up"], a["L0_ffn_shared_up_w"][None]])
    down = np.concatenate([a["L0_ffn_w_down"], a["L0_ffn_shared_down_w"][None]])
    return {"w_in": np.stack([gate, up], axis=1).transpose(3, 0, 1, 2),
            "w_down": down.transpose(2, 0, 1),
            "gate_w": a["L0_ffn_gate_w"].T, "expert_bias": a["L0_ffn_expert_bias"]}


def lay_out_layer1(a):
    e = {k: a[f"L1_attn_{k}"] for k in ATTN1}
    f = {k: a[f"L1_ffn_{k}"] for k in FFN1}
    step = LA // LF
    rows = lambda m: m.reshape(LA, -1, P, m.shape[-1]).transpose(0, 2, 1, 3).reshape(LA, P, -1)
    w = np.concatenate([e["Wq"], e["Wk"], e["Wv"], e["Wo"], e["W1"], rows(e["W2"])], axis=-1)
    col = np.concatenate([np.stack([e[k] for k in ("bq", "ln1_s", "ln2_s", "ln1_b", "ln2_b")], axis=-1),
                          e["b1"].reshape(LA, NB, P).transpose(0, 2, 1)], axis=-1)
    row = np.stack([e[k] for k in ("bk", "bv", "bo", "b2")], axis=1)
    enc = {"w": w.reshape(LF, step, P, -1).transpose(0, 2, 1, 3), "col": col.reshape(LF, step, P, -1).transpose(0, 2, 1, 3),
           "row": row.reshape(LF, step, 4, D), "lnf_s": e["lnf_s"], "lnf_b": e["lnf_b"]}
    pad = len(HBLK) * P - HID
    filled = lambda m, axis: np.concatenate([m, np.zeros([pad if n == axis else s for n, s in enumerate(m.shape)], m.dtype)], axis=axis)
    w = np.concatenate([f["wqkv"], f["wo"].reshape(LF, NB, P, D).transpose(0, 2, 1, 3).reshape(LF, P, -1), f["w1"],
                        filled(f["w2"], 1).reshape(LF, len(HBLK), P, D).transpose(0, 2, 1, 3).reshape(LF, P, -1)], axis=-1)
    b1 = filled(f["b1"].reshape(LF, 2, HID), 2).reshape(LF, 2 * len(HBLK), P).transpose(0, 2, 1)
    swap = lambda m: np.concatenate([m[:, FDH // 2:], m[:, :FDH // 2]], axis=-1)
    loc = {"w": w, "col": np.concatenate([f["ln_g"][..., None], f["ln_b"][..., None], b1], axis=-1),
           "row": np.concatenate([f["b2"], f["q_scale"], swap(f["q_scale"]), f["k_scale"], swap(f["k_scale"])], axis=-1)}
    return enc, loc


def kernel(**inputs):
    import concourse.bacc as bacc
    from concourse.bass_utils import run_bass_kernel_spmd
    nc = bacc.Bacc("TRN2", target_bir_lowering=False, num_devices=1)
    arrays = {}

    def dram(name, a):
        arrays[name] = np.ascontiguousarray(a)
        return nc.dram_tensor(name, arrays[name].shape, F32, kind="ExternalInput").ap()

    x = dram("L0_attn_x", inputs["L0_attn_x"])
    w0 = {k: dram(f"L0_attn_{k}", inputs[f"L0_attn_{k}"]) for k in ATTN0}
    w0.update({k: dram(f"L0_ffn_{k}", v) for k, v in lay_out_experts({k: np.asarray(v) for k, v in inputs.items()}).items()})
    enc, loc = lay_out_layer1({k: np.asarray(v) for k, v in inputs.items()})
    attn1 = {k: dram(f"L1_attn_{k}", v) for k, v in enc.items()}
    ffn1 = {k: dram(f"L1_ffn_{k}", v) for k, v in loc.items()}
    tables0 = {k: dram(f"table0_{k}", v) for k, v in shape_constants().items()}
    tables1 = {k: dram(f"table1_{k}", v) for k, v in layer1_constants().items()}
    x1 = nc.dram_tensor("x1", (B, T, D), F32, kind="Internal").ap()
    out = nc.dram_tensor("out", (B, T, D), F32, kind="ExternalOutput").ap()
    build(nc, x, w0, attn1, ffn1, tables0, tables1, x1, out)
    r = run_bass_kernel_spmd(nc, [arrays], core_ids=[0])
    return r.results[0]["out"]
```

```python
import numpy as np
import concourse.bass as bass
from concourse import mybir
from contextlib import ExitStack

F32 = mybir.dt.float32
ALU = mybir.AluOpType
ACT = mybir.ActivationFunctionType
AX_X = mybir.AxisListType.X

P = 128
D = 128
B = 8
T = 256
NT = T // P
EPS = 1e-5

GH, GDK, GM = 8, 16, 64
HM = GH * GM
CH = 8
CT = P // CH
NCH = T // CH
GRP = 64
GC = GRP // CH
NG = T // GRP
NB = HM // P
FLOOR = -19.0

E, TOPK = 16, 8
ROUTE_SCALE = 2.826

LA, LH, LDK = 4, 16, 8
FF = 4 * D

LF, FH, FDH, WIN = 2, 8, 64, 64
INNER = FH * FDH
KEYS = WIN + P
HID = int(D * 4 * 2 / 3)
HBLK = [(0, 128), (128, 128), (256, HID - 256)]
NEG = -1e30


def shape_constants():
    i = np.arange(P)
    pos, chunk = i % CH, i // CH
    c = {}
    c["ident"] = np.eye(P)
    same = chunk[:, None] == chunk[None, :]
    mid = CH // 2 - 1
    up = same & (pos[:, None] > mid) & (pos[:, None] <= pos[None, :])
    down = same & (pos[:, None] <= mid) & (pos[:, None] > pos[None, :])
    c["from_mid"] = -(up.astype(float) - down.astype(float))
    span = np.zeros((T, NCH))
    for n in range(NCH):
        span[n * CH + mid + 1:(n + 1) * CH + mid + 1, n] = -1.0
    span = span.reshape(GC, NT, 2, CH, NCH).transpose(1, 2, 0, 3, 4)
    c["mid_to_mid"] = span.reshape(NT, P, NCH).transpose(1, 0, 2).reshape(P, -1)
    c["chunk_causal"] = (same & (i[:, None] <= i[None, :])).astype(float)
    c["chunk_of_token"] = (2 * (chunk % GC) + chunk // GC == np.arange(CT)[:, None]).T.astype(float)
    kc = np.arange(GDK * GC)
    c["group_chunk"] = (kc[:, None] % GC == (np.arange(GRP) // CH)[None, :]).astype(float)
    c["sum_chunks"] = (kc[:, None] // GC == np.arange(2 * GDK)[None, :]).astype(float)
    rep = np.zeros((P, GH, P))
    for h in range(GH):
        for k in range(GDK):
            rep[h * GDK + k, h, k * GC:(k + 1) * GC] = 1.0
    c["spread_key"] = rep.reshape(P, -1)
    c["head_rows"] = (i[:, None] // GDK == np.arange(GH)[None, :]).astype(float)
    return {k: np.ascontiguousarray(v, dtype=np.float32) for k, v in c.items()}


def layer1_constants():
    i = np.arange(P)
    c = {}
    c["ident"] = np.eye(P)
    c["head_block"] = (i[:, None] // LDK == i[None, :] // LDK).astype(float)
    c["next_token"] = (i[:, None] + 1 == i[None, :]).astype(float)
    c["next_tile"] = ((i[:, None] == P - 1) & (i[None, :] == 0)).astype(float)
    half = D // 2
    f32 = np.float32
    freq = np.exp(np.arange(half, dtype=f32) * f32(-np.log(10000.0) / (half - 1))).astype(f32)
    ang = ((np.arange(T, dtype=f32) + f32(1.0))[:, None] * freq[None, :]).astype(f32)
    emb = np.concatenate([np.sin(ang), np.cos(ang)], axis=-1)
    c["pos_emb"] = emb.reshape(NT, P, D).transpose(1, 0, 2).reshape(P, -1)
    hi = np.arange(0, FDH, 2, dtype=f32)
    inv = (f32(1.0) / f32(10000.0) ** (hi / f32(FDH))).astype(f32)
    t = np.arange(T, dtype=f32)
    ang = (t[:, None] * inv[None, :]).astype(f32)
    base = ((hi + f32(0.4 * FDH)) / f32(1.4 * FDH)).astype(f32)
    power = ((t - T // 2) / f32(WIN // 2)).astype(f32)
    sc = (base[None, :] ** power[:, None]).astype(f32)
    cos, sin = np.cos(ang), np.sin(ang)
    dbl = lambda a, s=1.0: np.concatenate([s * a, a], axis=-1)
    rot = np.stack([dbl(cos * sc), dbl(sin * sc, -1.0), dbl(cos / sc), dbl(sin / sc, -1.0)], axis=1)
    c["rotary"] = rot.reshape(NT, P, 4 * FDH).transpose(1, 0, 2).reshape(P, -1)
    j = np.arange(KEYS) - WIN
    m = []
    for tt in range(NT):
        qi, kj = i[:, None] + tt * P, j[None, :] + tt * P
        seen = (kj >= 0) & (qi >= kj) & (qi <= kj + WIN) & (kj // WIN >= qi // WIN - 1)
        m.append(np.where(seen, 0.0, NEG))
    c["window"] = np.stack(m, axis=1).reshape(P, -1)
    return {k: np.ascontiguousarray(v, dtype=np.float32) for k, v in c.items()}


def packed(tables):
    return np.concatenate(list(tables.values()), axis=1), list(tables), [t.shape[1] for t in tables.values()]


def slices_of(tile, const):
    _, widths, names = const
    at, out = 0, {}
    for name, width in zip(names, widths):
        out[name] = tile[:, at:at + width]
        at += width
    return out


class Banks:

    def __init__(self, ctx, nc, name, banks, jobs):
        self.banks, self.jobs = banks, {job: n for n, job in enumerate(jobs)}
        assert len(self.jobs) == len(jobs)
        self.filled = [ctx.enter_context(nc.semaphore(f"{name}_filled{i}")) for i in range(len(banks))]
        self.emptied = [ctx.enter_context(nc.semaphore(f"{name}_emptied{i}")) for i in range(len(banks))]

    def at(self, job):
        n = self.jobs[job]
        return n % len(self.banks), n // len(self.banks)

    def tile(self, job):
        return self.banks[self.at(job)[0]]

    def wait_free(self, pe, job):
        b, use = self.at(job)
        if use:
            pe.wait_ge(self.emptied[b], use)

    def is_filled(self, ins, job):
        ins.then_inc(self.filled[self.at(job)[0]], 1)

    def wait_filled(self, eng, job):
        b, use = self.at(job)
        eng.wait_ge(self.filled[b], use + 1)

    def is_emptied(self, ins, job):
        ins.then_inc(self.emptied[self.at(job)[0]], 1)

    def wait_emptied(self, eng, job):
        b, use = self.at(job)
        eng.wait_ge(self.emptied[b], use + 1)

    def sems(self):
        return self.filled + self.emptied


class Chain:

    def __init__(self, eng, sem):
        self.eng, self.sem, self.count = eng, sem, 0

    def __call__(self, ins):
        ins.then_inc(self.sem, 1)
        self.count += 1
        self.eng.wait_ge(self.sem, self.count)


def run_stages(*streams):
    live = list(streams)
    while live:
        for s in list(live):
            if next(s, "end") == "end":
                live.remove(s)


def layer0(nc, x, x1, w, const, psum):
    ctx = ExitStack()
    with ctx:
        def sb(name, *shape):
            return ctx.enter_context(nc.sbuf_tensor(name, list(shape), F32))

        def sem(name):
            return ctx.enter_context(nc.semaphore(name))

        tables = sb("tables", P, sum(width for width in const[1]))
        table = slices_of(tables, const)
        ident = table["ident"]
        w_q, w_k, w_kv = sb("w_q", P, D), sb("w_k", P, D), sb("w_kv", P, 2 * D)
        w_fg = sb("w_fg", P, 2 * GDK)
        w_f2, w_g2 = sb("w_f2", GDK, HM), sb("w_g2", GDK, D)
        w_out, norm_w = sb("w_out", P, D), sb("norm_w", P, 1)
        gate_t = sb("gate_t", P, E)
        route_bias = sb("route_bias", P, E)
        w_in_t = sb("w_in_t", P, E + 1, 2, P)
        w_down_t = sb("w_down_t", P, E + 1, D)
        half_pow = sb("half_pow", P, 2 * GH)

        x_all = sb("x_all", P, B * NT, D)

        xin = sb("xin", P, NT, D)
        v_pad = sb("v_pad", P, NT, D + GDK)
        stats, moments = sb("stats", P, NT, 6), sb("moments", P, NT, 2)
        var_eps, rstd = sb("var_eps", P, NT), sb("rstd", P, NT)
        xn, xn_t = sb("xn", P, NT, D), sb("xn_t", P, T)
        tanh_qk, qk_t = sb("tanh_qk", P, 2, T), sb("qk_t", P, 2, T)
        tanh_k = sb("tanh_k", P, NT, D)
        kv = sb("kv", P, NT, 2, D)
        fg1 = sb("fg1", GDK, 2, T)
        sp = sb("softplus", P, NT, HM)
        slot_w = sb("slot_w", P, NT, HM)
        from_mid, to_mid = sb("from_mid", P, NT, HM), sb("to_mid", P, NT, HM)
        exp_gate = sb("exp_gate", P, NT, D)
        chunk_decay = sb("chunk_decay", P, NB, GDK, NCH)
        kv_chunks = sb("kv_chunks", P, NT, 2, D, CT)
        q_heads = sb("q_heads", P, GH, T)
        qk_near = sb("qk_near", P, NT, GH, P)
        q_spread = sb("q_spread", P, GH, T)
        state = sb("state", P, 2, NB, 1 + GDK * NCH)
        k_state_t = sb("k_state_t", P, NG, HM)
        slots = sb("slots", P, NT, HM)
        slot_max, slot_sum = sb("slot_max", P, NT, GH), sb("slot_sum", P, NT, GH)
        slot_q = sb("slot_q", P, NT, HM)
        slot_w_t = sb("slot_w_t", P, NT, NB, P)
        slot_q_t = sb("slot_q_t", P, NT, NB, 2, P)
        far = sb("far", P, NT, GH, P)
        near_w = qk_near
        read_t = sb("read_t", P, NT, GH // 4, P)
        den, og, og_sq = sb("den", P, NT, D), sb("og", P, NT, D), sb("og_sq", P, NT, D)
        og_ms, og_rms = sb("og_ms", P, NT * GH), sb("og_rms", P, NT * GH)
        og_t, attn = sb("og_t", P, T), sb("attn", P, NT, D)
        score, sel, sel_left = sb("score", P, NT, E), sb("sel", P, NT, E), sb("sel_left", P, NT, E)
        top8, mix_sum = sb("top8", P, NT, TOPK), sb("mix_sum", P, NT)
        mix = sb("mix", P, NT, E + 1)
        tanh_g, hid = sb("tanh_g", P, 2, T), sb("hid", P, 2, T)
        y, silu_y = sb("y", P, NT, D), sb("silu_y", P, NT, D)
        part = sb("part", P, 2, NT, D)

        loads, x_loads, expert_loads, scaled = sem("loads"), sem("x_loads"), sem("expert_loads"), sem("out_scaled")
        pairs = ([(tables[:], const[0])]
                 + [(w_q[:], w["Wq"]), (w_k[:], w["Wk"]), (w_kv[:, 0:D], w["Wk"]), (w_kv[:, D:2 * D], w["Wv"]),
                    (w_fg[:, 0:GDK], w["Wf1"]), (w_fg[:, GDK:2 * GDK], w["Wg1"]), (w_f2[:], w["Wf2"]),
                    (w_g2[:], w["Wg2"]), (w_out[:], w["Wo"]), (norm_w[:], w["norm_w"].rearrange("(p a) -> p a", a=1)),
                    (gate_t[:], w["gate_w"]), (route_bias[:], w["expert_bias"].partition_broadcast(P))])
        expert_pairs = [(dst[:, e:min(e + 4, E + 1)], src[:, e:min(e + 4, E + 1)]) for e in range(0, E + 1, 4)
                        for dst, src in ((w_in_t, w["w_in"]), (w_down_t, w["w_down"]))]

        with nc.Block() as block:
            @block.sync
            def _(sync):
                for dst, src in pairs:
                    sync.dma_start(dst, src).then_inc(loads, 16)
                for dst, src in expert_pairs:
                    sync.dma_start(dst, src).then_inc(expert_loads, 16)

            @block.scalar
            def _(act):
                act.dma_start(x_all[:], x).then_inc(x_loads, 16)

            @block.vector
            def _(dve):
                dve.wait_ge(loads, 16 * len(pairs))
                dve.wait_ge(x_loads, 16)
                dve.tensor_scalar(w_out[:], w_out[:], norm_w[:], None, ALU.mult).then_inc(scaled, 1)

            @block.gpsimd
            def _(pool):
                pool.memset(state[:, :, :, 0:1], 0.0)
                pool.memset(chunk_decay[:, :, :, NCH - 1:NCH], 0.0)
                pool.memset(mix[:, :, E:E + 1], 0.5)
                pool.memset(half_pow[:], -0.5)
                pool.memset(slot_q_t[:], 0.0)
                pool.memset(v_pad[:, :, D:D + GDK], 0.0)

        g_jobs = (["x_t", "fg1", "qk", "kv", "f0", "f1", "gate", "mid0", "mid1", "decay"]
                  + [f"near{t}{a}" for t in range(NT) for a in range(2)]
                  + [f"spread{a}" for a in range(4)]
                  + [f"state{j}{r}" for j in range(NB) for r in range(2)]
                  + [f"state_t{g}" for g in range(NG)]
                  + ["slots0", "slots1", "w_t0", "w_t1", "q_t0", "q_t1"])
        r_jobs = ([f"near_v{t}{a}" for t in range(NT) for a in range(2)] + [f"far{t}{a}" for t in range(NT) for a in range(2)]
                  + ["read", "back", "og_t", "attn"])
        m_jobs = ["route"]
        for e in range(E + 1):
            m_jobs += [f"in{e}"] + ([f"out{e - 1}"] if e else [])
        m_jobs += [f"out{E}"]
        pauses = (1, 2, 4, 6, 8, 11, 14)
        G = Banks(ctx, nc, "slots", psum[0:3], g_jobs)
        R = Banks(ctx, nc, "read", psum[3:5], r_jobs)
        M = Banks(ctx, nc, "moe", psum[5:8], m_jobs)
        names = ["var_ready", "rstd_ready", "xn_ready", "qk_tanh", "k_tanh", "qk_ready", "softplus_ready",
                 "exp_ready", "slot_w_ready", "chunks_ready", "kv_ready", "q_heads_ready", "sub0", "sub1", "slot_exp0", "slot_exp1",
                 "slot_q0", "slot_q1", "og_ms_ready", "og_rms_ready", "og_ready", "tanh_g_ready", "tanh_y_ready", "v_copied", "mix_ready", "x1_ready", "x1_stored", "y_added", "silu_y_ready"]
        S = {n: sem(f"a_{n}") for n in names}
        steps = {n: sem(f"a_{n}_step") for n in ("dve", "act")}
        per_batch = range(G.filled[0].num, steps["act"].num + 1)

        def step_of(early, late):
            def streams(slot_attention, read_out, moe):
                live = [early is not None and moe(), early is not None and slot_attention(), late is not None and read_out()]
                return [s for s in live if s]

            with nc.Block() as block:
                if late is not None:
                    @block.sync
                    def _(sync):
                        dst = x1[bass.ds(late, 1)].rearrange("a (c t g u) d -> (a t g) c u d", t=NT, g=2, u=CH)
                        sync.wait_ge(S["x1_ready"], 1)
                        for t in range(NT):
                            for g in range(2):
                                sync.dma_start(dst[2 * t + g], attn[g * GRP:(g + 1) * GRP, t, :]).then_inc(S["x1_stored"], 16)
                        sync.wait_ge(S["x1_stored"], 16 * NG)

                @block.tensor
                def _(pe):
                    def slot_attention():
                        G.wait_free(pe, "x_t")
                        pe.wait_ge(S["xn_ready"], 1)
                        for t in range(NT):
                            last = pe.transpose(G.tile("x_t")[:, t * P:(t + 1) * P], xn[:, t, :], ident[:])
                        G.is_filled(last, "x_t")
                        yield
                        G.wait_emptied(pe, "x_t")
                        G.wait_free(pe, "fg1")
                        pe.matmul(G.tile("fg1")[0:GDK, 0:T], w_fg[:, 0:GDK], xn_t[:], start=True, stop=True)
                        G.is_filled(pe.matmul(G.tile("fg1")[0:GDK, T:2 * T], w_fg[:, GDK:2 * GDK], xn_t[:], start=True, stop=True), "fg1")
                        G.wait_free(pe, "qk")
                        pe.matmul(G.tile("qk")[:, 0:T], w_q[:], xn_t[:], start=True, stop=True)
                        G.is_filled(pe.matmul(G.tile("qk")[:, T:2 * T], w_k[:], xn_t[:], start=True, stop=True), "qk")
                        G.wait_free(pe, "kv")
                        for t in range(NT):
                            last = pe.matmul(G.tile("kv")[:, t * 2 * D:(t + 1) * 2 * D], xn_t[:, t * P:(t + 1) * P], w_kv[:], start=True, stop=True)
                        G.is_filled(last, "kv")
                        yield
                        G.wait_emptied(pe, "fg1")
                        for t in range(NT):
                            G.wait_free(pe, f"f{t}")
                            G.is_filled(pe.matmul(G.tile(f"f{t}")[:], fg1[:, 0, t * P:(t + 1) * P], w_f2[:], start=True, stop=True), f"f{t}")
                        G.wait_free(pe, "gate")
                        for t in range(NT):
                            last = pe.matmul(G.tile("gate")[:, t * P:(t + 1) * P], fg1[:, 1, t * P:(t + 1) * P], w_g2[:], start=True, stop=True)
                        G.is_filled(last, "gate")
                        yield
                        pe.wait_ge(S["softplus_ready"], 1)
                        for t in range(NT):
                            G.wait_free(pe, f"mid{t}")
                            G.is_filled(pe.matmul(G.tile(f"mid{t}")[:], table["from_mid"][:], sp[:, t, :], start=True, stop=True), f"mid{t}")
                        G.wait_free(pe, "decay")
                        for j in range(NB):
                            for t in range(NT):
                                last = pe.matmul(G.tile("decay")[:, j * NCH:(j + 1) * NCH], sp[:, t, j * P:(j + 1) * P],
                                                 table["mid_to_mid"][:, t * NCH:(t + 1) * NCH], start=(t == 0), stop=(t == NT - 1))
                        G.is_filled(last, "decay")
                        yield
                        G.wait_emptied(pe, "qk")
                        pe.wait_ge(S["qk_ready"], 1)
                        pe.wait_ge(S["q_heads_ready"], GH)
                        for t in range(NT):
                            for a in range(2):
                                job = f"near{t}{a}"
                                G.wait_free(pe, job)
                                G.is_filled(pe.matmul(G.tile(job)[:], qk_t[:, 1, t * P:(t + 1) * P],
                                                      q_heads[:, 4 * a:4 * a + 4, t * P:(t + 1) * P], start=True, stop=True), job)
                        for a in range(4):
                            job = f"spread{a}"
                            G.wait_free(pe, job)
                            for i in range(2):
                                h = 2 * a + i
                                last = pe.matmul(G.tile(job)[:, i * T:(i + 1) * T], table["spread_key"][:, h * P:(h + 1) * P],
                                                 qk_t[:, 0, :], start=True, stop=True)
                            G.is_filled(last, job)
                        yield
                        pe.wait_ge(S["slot_w_ready"], 1)
                        pe.wait_ge(S["chunks_ready"], 2 * NT)
                        for j in range(NB):
                            for r in range(2):
                                job = f"state{j}{r}"
                                G.wait_free(pe, job)
                                out = G.tile(job)[:].rearrange("p (k g) -> p k g", g=NG)
                                for i in range(2):
                                    h = 2 * j + i
                                    for t in range(NT):
                                        last = pe.matmul(out[GM * i:GM * (i + 1), :, 2 * t:2 * t + 2],
                                                         to_mid[:, t, h * GM:(h + 1) * GM],
                                                         kv_chunks[:, t, r, h * GDK:(h + 1) * GDK, :], start=True, stop=True)
                                G.is_filled(last, job)
                        yield
                        for g in range(NG):
                            job = f"state_t{g}"
                            G.wait_free(pe, job)
                            if g == 0:
                                for j in range(NB):
                                    G.wait_emptied(pe, f"state{j}0")
                            for j in range(NB):
                                last = pe.transpose(G.tile(job)[:, j * P:(j + 1) * P], state[:, 0, j, g:GDK * NCH:NG], ident[:])
                            G.is_filled(last, job)
                        for t in range(NT):
                            job = f"slots{t}"
                            G.wait_free(pe, job)
                            for a in range(2):
                                G.wait_emptied(pe, f"near{t}{a}")
                            for a in range(4):
                                G.wait_emptied(pe, f"spread{a}")
                            for g in range(2):
                                G.wait_emptied(pe, f"state_t{2 * t + g}")
                            for h in range(GH):
                                cols = slice(h * GM, (h + 1) * GM)
                                for i in range(2):
                                    g = 2 * t + i
                                    pe.matmul(G.tile(job)[GRP * i:GRP * (i + 1), cols], q_spread[:, h, g * GRP:(g + 1) * GRP],
                                              k_state_t[:, g, cols], start=True, stop=False)
                                    last = pe.matmul(G.tile(job)[GRP * i:GRP * (i + 1), cols], qk_near[:, t, h, GRP * i:GRP * (i + 1)],
                                                     to_mid[:, t, cols], start=False, stop=True)
                            G.is_filled(last, job)
                        yield
                        for t in range(NT):
                            job = f"w_t{t}"
                            G.wait_free(pe, job)
                            for j in range(NB):
                                last = pe.transpose(G.tile(job)[:, j * P:(j + 1) * P], to_mid[:, t, j * P:(j + 1) * P], ident[:])
                            G.is_filled(last, job)
                        yield
                        for t in range(NT):
                            job = f"q_t{t}"
                            G.wait_free(pe, job)
                            pe.wait_ge(S[f"slot_q{t}"], 1)
                            for j in range(NB):
                                last = pe.transpose(G.tile(job)[:, j * P:(j + 1) * P], slot_q[:, t, j * P:(j + 1) * P], ident[:])
                            G.is_filled(last, job)

                    def near_values(t):
                        for a in range(2):
                            job = f"near_v{t}{a}"
                            R.wait_free(pe, job)
                            for i in range(2):
                                j = 2 * a + i
                                last = pe.matmul(R.tile(job)[:, 2 * i * P:2 * (i + 1) * P], slot_w_t[:, t, j, :], slot_q_t[:, t, j], start=True, stop=True)
                            R.is_filled(last, job)

                    def read_out():
                        near_values(1)
                        yield
                        yield
                        for t in range(NT):
                            for a in range(2):
                                job = f"far{t}{a}"
                                R.wait_free(pe, job)
                                out = R.tile(job)[:].rearrange("p (h t) -> p h t", t=P)
                                for j in range(2):
                                    for g in range(2):
                                        at = slice(g * GRP, (g + 1) * GRP)
                                        last = pe.matmul(out[:, 2 * j:2 * j + 2, at], state[:, 1, 2 * a + j, 2 * t + g:GDK * NCH:NG],
                                                         slot_q_t[:, t, 2 * a + j, :, at], start=True, stop=True)
                                R.is_filled(last, job)
                        yield
                        R.wait_free(pe, "read")
                        for t in range(NT):
                            for a in range(2):
                                R.wait_emptied(pe, f"far{t}{a}")
                                R.wait_emptied(pe, f"near_v{t}{a}")
                            for h in range(GH):
                                at = 2 * GDK * (h % 4)
                                dst = R.tile("read")[at:at + 2 * GDK, (2 * t + h // 4) * P:(2 * t + h // 4 + 1) * P]
                                pe.matmul(dst, v_pad[:, t, h * GDK:(h + 2) * GDK], near_w[:, t, h, :], start=True, stop=False)
                                last = pe.matmul(dst, table["sum_chunks"][:], far[:, t, h, :], start=False, stop=True)
                        R.is_filled(last, "read")
                        yield
                        R.wait_free(pe, "back")
                        R.wait_emptied(pe, "read")
                        for t in range(NT):
                            for a in range(GH // 4):
                                last = pe.transpose(R.tile("back")[:, (2 * t + a) * P:(2 * t + a + 1) * P], read_t[:, t, a, :], ident[:])
                        R.is_filled(last, "back")
                        yield
                        R.wait_free(pe, "og_t")
                        pe.wait_ge(S["og_ready"], 1)
                        for t in range(NT):
                            last = pe.transpose(R.tile("og_t")[:, t * P:(t + 1) * P], og[:, t, :], ident[:])
                        R.is_filled(last, "og_t")
                        yield
                        R.wait_free(pe, "attn")
                        R.wait_emptied(pe, "og_t")
                        for t in range(NT):
                            last = pe.matmul(R.tile("attn")[:, t * D:(t + 1) * D], og_t[:, t * P:(t + 1) * P], w_out[:], start=True, stop=True)
                        R.is_filled(last, "attn")

                    def experts_in(e):
                        job = f"in{e}"
                        M.wait_free(pe, job)
                        pe.matmul(M.tile(job)[:, 0:T], w_in_t[:, e, 0, :], xn_t[:], start=True, stop=True)
                        M.is_filled(pe.matmul(M.tile(job)[:, T:2 * T], w_in_t[:, e, 1, :], xn_t[:], start=True, stop=True), job)

                    def experts_out(e):
                        job = f"out{e}"
                        M.wait_free(pe, job)
                        M.wait_emptied(pe, f"in{e}")
                        for t in range(NT):
                            last = pe.matmul(M.tile(job)[:, t * D:(t + 1) * D], hid[:, e % 2, t * P:(t + 1) * P], w_down_t[:, e, :], start=True, stop=True)
                        M.is_filled(last, job)

                    def moe():
                        yield
                        G.wait_emptied(pe, "x_t")
                        M.wait_free(pe, "route")
                        pe.wait_ge(expert_loads, 16 * len(expert_pairs))
                        for t in range(NT):
                            last = pe.matmul(M.tile("route")[:, t * E:(t + 1) * E], xn_t[:, t * P:(t + 1) * P], gate_t[:], start=True, stop=True)
                        M.is_filled(last, "route")
                        experts_in(0)
                        yield
                        for e in range(1, E + 1):
                            experts_in(e)
                            experts_out(e - 1)
                            if e in pauses:
                                yield
                        experts_out(E)

                    if late is not None:
                        near_values(0)
                    run_stages(*streams(slot_attention, read_out, moe))

                @block.scalar
                def _(act):
                    step = Chain(act, steps["act"])

                    def slot_attention():
                        G.wait_filled(act, "x_t")
                        G.is_emptied(act.activation(xn_t[:], G.tile("x_t")[:, 0:T], ACT.Copy), "x_t")
                        yield
                        G.wait_filled(act, "fg1")
                        G.is_emptied(act.activation(fg1[:].rearrange("p r t -> p (r t)"), G.tile("fg1")[0:GDK, :], ACT.Copy), "fg1")
                        G.wait_filled(act, "qk")
                        act.activation(tanh_qk[:].rearrange("p r t -> p (r t)"), G.tile("qk")[:], ACT.Tanh, scale=0.5).then_inc(S["qk_tanh"], 1)
                        G.wait_filled(act, "kv")
                        tok = G.tile("kv")[:].rearrange("p (t r d) -> p t r d", t=NT, r=2)
                        act.activation(tanh_k[:], tok[:, :, 0, :], ACT.Tanh, scale=0.5).then_inc(S["k_tanh"], 1)
                        yield
                        for t in range(NT):
                            G.wait_emptied(act, f"f{t}")
                        step(act.activation(sp[:], sp[:], ACT.Exp, scale=-1.0))
                        G.wait_filled(act, "gate")
                        G.is_emptied(act.activation(exp_gate[:].rearrange("p t d -> p (t d)"), G.tile("gate")[:, 0:T], ACT.Exp, scale=-1.0), "gate")
                        act.activation(sp[:], sp[:], ACT.Ln, bias=1.0).then_inc(S["softplus_ready"], 1)
                        act.wait_ge(S["softplus_ready"], 1)
                        act.activation(slot_w[:], sp[:], ACT.Exp, scale=-1.0).then_inc(S["exp_ready"], 1)
                        yield
                        for t in range(NT):
                            G.wait_filled(act, f"mid{t}")
                            act.activation(from_mid[:, t, :], G.tile(f"mid{t}")[:], ACT.Exp)
                            G.is_emptied(act.activation(to_mid[:, t, :], G.tile(f"mid{t}")[:], ACT.Exp, scale=-1.0), f"mid{t}")
                        G.wait_filled(act, "decay")
                        for j in range(NB):
                            src = G.tile("decay")[:, j * NCH:j * NCH + NCH - 1].unsqueeze(1).to_broadcast([P, GDK, NCH - 1])
                            last = act.activation(chunk_decay[:, j, :, 0:NCH - 1], src, ACT.Exp)
                        G.is_emptied(last, "decay")
                        yield
                        yield
                        yield
                        for g in range(NG):
                            job = f"state_t{g}"
                            G.wait_filled(act, job)
                            G.is_emptied(act.activation(k_state_t[:, g, :], G.tile(job)[:], ACT.Copy), job)
                        yield
                        for t in range(NT):
                            act.wait_ge(S[f"sub{t}"], 1)
                            act.activation(slots[:, t, :], slots[:, t, :], ACT.Exp).then_inc(S[f"slot_exp{t}"], 1)
                        for t in range(NT):
                            job = f"w_t{t}"
                            if late is not None and t == 0:
                                R.wait_filled(act, "far11")
                            G.wait_filled(act, job)
                            G.is_emptied(act.activation(slot_w_t[:, t].rearrange("p j t -> p (j t)"), G.tile(job)[:], ACT.Copy), job)
                        yield
                        for t in range(NT):
                            job = f"q_t{t}"
                            G.wait_filled(act, job)
                            for i in range(2):
                                rows = slice(GM * i, GM * (i + 1))
                                last = act.activation(slot_q_t[rows, t, :, i, :], G.tile(job)[rows, :].rearrange("p (j t) -> p j t", t=P), ACT.Copy)
                            G.is_emptied(last, job)

                    def read_out():
                        yield
                        yield
                        yield
                        R.wait_filled(act, "read")
                        R.is_emptied(act.activation(read_t[:].rearrange("p t a n -> p (t a n)"), R.tile("read")[:], ACT.Copy), "read")
                        yield
                        yield
                        R.wait_filled(act, "og_t")
                        R.is_emptied(act.activation(og_t[:], R.tile("og_t")[:, 0:T], ACT.Copy), "og_t")
                        yield

                    def tanh(e):
                        job = f"in{e}"
                        M.wait_filled(act, job)
                        if e >= 2:
                            M.wait_emptied(act, f"in{e - 2}")
                        act.activation(tanh_g[:, e % 2, :], M.tile(job)[:, 0:T], ACT.Tanh, scale=0.5).then_inc(S["tanh_g_ready"], 1)

                    def weigh(e):
                        job = f"out{e}"
                        M.wait_filled(act, job)
                        if e >= 2:
                            act.wait_ge(S["y_added"], e - 1)
                        for t in range(NT):
                            last = act.activation(part[:, e % 2, t, :], M.tile(job)[:, t * D:(t + 1) * D], ACT.Copy, scale=mix[:, t, e:e + 1])
                        M.is_emptied(last, job)

                    def moe():
                        yield
                        M.wait_filled(act, "route")
                        M.is_emptied(act.activation(score[:].rearrange("p t e -> p (t e)"), M.tile("route")[:, 0:NT * E], ACT.Exp, scale=-1.0), "route")
                        tanh(0)
                        yield
                        act.wait_ge(S["mix_ready"], NT)
                        for e in range(1, E + 1):
                            tanh(e)
                            weigh(e - 1)
                            if e in pauses:
                                yield
                        weigh(E)

                    if late is not None:
                        act.activation(silu_y[:], y[:], ACT.Tanh, scale=0.5).then_inc(S["tanh_y_ready"], 1)
                    run_stages(*streams(slot_attention, read_out, moe))

                @block.gpsimd
                def _(pool):
                    def slot_attention():
                        pool.wait_ge(S["var_ready"], 1)
                        pool.tensor_tensor(rstd[:], var_eps[:], half_pow[:, 0:NT], ALU.pow).then_inc(S["rstd_ready"], 1)
                        yield
                        pool.wait_ge(S["qk_ready"], 1)
                        for h in range(GH):
                            pool.tensor_scalar(q_heads[:, h, :], qk_t[:, 0, :], table["head_rows"][:, h:h + 1], None, ALU.mult).then_inc(S["q_heads_ready"], 1)
                        yield
                        pool.wait_ge(S["kv_ready"], 1)
                        for t in range(NT):
                            for r in range(2):
                                mask = table["chunk_of_token"][:].unsqueeze(1).to_broadcast([P, D, CT])
                                pool.tensor_tensor(kv_chunks[:, t, r], kv[:, t, r, :].unsqueeze(2).to_broadcast([P, D, CT]), mask, ALU.mult).then_inc(S["chunks_ready"], 1)
                        yield
                        for _ in range(5):
                            yield
                        if late is not None:
                            R.wait_filled(pool, "read")
                        pool.tensor_copy(v_pad[:, :, 0:D], kv[:, :, 1, :]).then_inc(S["v_copied"], 1)
                        yield

                    def read_out():
                        for _ in range(4):
                            yield
                        pool.wait_ge(S["og_ms_ready"], 1)
                        pool.tensor_tensor(og_rms[:], og_ms[:], half_pow[:], ALU.pow).then_inc(S["og_rms_ready"], 1)
                        yield

                    def moe():
                        yield
                        yield
                        if late is not None:
                            pool.wait_ge(S["silu_y_ready"], 1)
                        for e in range(E + 1):
                            M.wait_emptied(pool, f"out{e}")
                            if e == 0:
                                ins = pool.tensor_copy(y[:], part[:, 0])
                            else:
                                pool.wait_ge(S["y_added"], e)
                                ins = pool.tensor_tensor(y[:], y[:], part[:, e % 2], ALU.add)
                            ins.then_inc(S["y_added"], 1)
                            if e + 1 in pauses:
                                yield
                        pool.wait_ge(S["y_added"], E + 1)

                    run_stages(*streams(slot_attention, read_out, moe))

                @block.vector
                def _(dve):
                    step = Chain(dve, steps["dve"])

                    def slot_attention():
                        yield
                        dve.wait_ge(S["qk_tanh"], 1)
                        qk_flat = qk_t[:].rearrange("p r t -> p (r t)")
                        G.is_emptied(dve.scalar_tensor_tensor(qk_flat, tanh_qk[:].rearrange("p r t -> p (r t)"), 1.0,
                                                              G.tile("qk")[:], ALU.add, ALU.mult), "qk")
                        G.wait_emptied(dve, "qk")
                        dve.tensor_scalar(qk_flat, qk_flat, 0.5, None, ALU.mult).then_inc(S["qk_ready"], 1)
                        dve.wait_ge(S["k_tanh"], 1)
                        tok = G.tile("kv")[:].rearrange("p (t r d) -> p t r d", t=NT, r=2)
                        dve.scalar_tensor_tensor(kv[:, :, 0, :], tanh_k[:], 1.0, tok[:, :, 0, :], ALU.add, ALU.mult)
                        G.is_emptied(dve.tensor_copy(kv[:, :, 1, :], tok[:, :, 1, :]), "kv")
                        G.wait_emptied(dve, "kv")
                        dve.tensor_scalar(kv[:, :, 0, :], kv[:, :, 0, :], 0.5, None, ALU.mult).then_inc(S["kv_ready"], 1)
                        yield
                        for t in range(NT):
                            G.wait_filled(dve, f"f{t}")
                            G.is_emptied(dve.tensor_scalar(sp[:, t, :], G.tile(f"f{t}")[:], FLOOR, None, ALU.max), f"f{t}")
                        yield
                        dve.wait_ge(S["exp_ready"], 1)
                        step(dve.tensor_scalar(slot_w[:], slot_w[:], -1.0, 1.0, ALU.mult, ALU.add))
                        for t in range(NT):
                            G.wait_emptied(dve, f"mid{t}")
                            last = dve.tensor_tensor(to_mid[:, t, :], to_mid[:, t, :], slot_w[:, t, :], ALU.mult)
                        last.then_inc(S["slot_w_ready"], 1)
                        yield
                        if late is not None:
                            R.wait_filled(dve, "read")
                        for t in range(NT):
                            for a in range(2):
                                job = f"near{t}{a}"
                                G.wait_filled(dve, job)
                                mask = table["chunk_causal"][:].unsqueeze(1).to_broadcast([P, 4, P])
                                G.is_emptied(dve.tensor_tensor(qk_near[:, t, 4 * a:4 * a + 4, :],
                                                               G.tile(job)[:].rearrange("p (h t) -> p h t", t=P), mask, ALU.mult), job)
                        for a in range(4):
                            job = f"spread{a}"
                            G.wait_filled(dve, job)
                            mask = table["group_chunk"][:].unsqueeze(1).to_broadcast([P, 2 * NG, GRP])
                            G.is_emptied(dve.tensor_tensor(q_spread[:, 2 * a:2 * a + 2, :].rearrange("p h (g t) -> p (h g) t", t=GRP),
                                                           G.tile(job)[:].rearrange("p (g t) -> p g t", t=GRP), mask, ALU.mult), job)
                        yield
                        G.wait_emptied(dve, "decay")
                        for j in range(NB):
                            for r in range(2):
                                job = f"state{j}{r}"
                                G.wait_filled(dve, job)
                                G.is_emptied(dve.tensor_tensor_scan(state[:, r, j, 1:1 + GDK * NCH], G.tile(job)[:],
                                                                    chunk_decay[:, j].rearrange("p k c -> p (k c)"), 0.0, ALU.add, ALU.mult), job)
                        yield
                        for t in range(NT):
                            job = f"slots{t}"
                            G.wait_filled(dve, job)
                            G.is_emptied(dve.tensor_tensor(slots[:, t, :], G.tile(job)[:], from_mid[:, t, :], ALU.mult), job)
                            G.wait_emptied(dve, job)
                            heads = slots[:, t, :].rearrange("p (h m) -> p h m", m=GM)
                            step(dve.tensor_reduce(slot_max[:, t, :], heads, AX_X, ALU.max))
                            dve.tensor_tensor(heads, heads, slot_max[:, t, :].unsqueeze(2).to_broadcast([P, GH, GM]), ALU.subtract).then_inc(S[f"sub{t}"], 1)
                        yield
                        for t in range(NT):
                            dve.wait_ge(S[f"slot_exp{t}"], 1)
                            dve.tensor_tensor(slot_q[:, t, :], slots[:, t, :], from_mid[:, t, :], ALU.mult).then_inc(S[f"slot_q{t}"], 1)
                            step(dve.tensor_reduce(slot_sum[:, t, :], slots[:, t, :].rearrange("p (h m) -> p h m", m=GM), AX_X, ALU.add))
                        yield
                        G.wait_emptied(dve, "gate")
                        step(dve.scalar_tensor_tensor(den[:].rearrange("p t (h v) -> p (t h) v", v=GDK), exp_gate[:].rearrange("p t (h v) -> p (t h) v", v=GDK), 1.0,
                                                      slot_sum[:].rearrange("p t h -> p (t h)").unsqueeze(2).to_broadcast([P, NT * GH, GDK]), ALU.add, ALU.mult))
                        step(dve.reciprocal(den[:], den[:]))

                    def read_out():
                        dve.wait_ge(S["tanh_y_ready"], 1)
                        dve.scalar_tensor_tensor(silu_y[:], silu_y[:], 1.0, y[:], ALU.add, ALU.mult).then_inc(S["silu_y_ready"], 1)
                        for t in range(NT):
                            for a in range(2):
                                job = f"near_v{t}{a}"
                                R.wait_filled(dve, job)
                                mask = table["chunk_causal"][:].unsqueeze(1).to_broadcast([P, 4, P])
                                R.is_emptied(dve.tensor_tensor(near_w[:, t, 4 * a:4 * a + 4, :],
                                                               R.tile(job)[:].rearrange("p (h t) -> p h t", t=P), mask, ALU.mult), job)
                        yield
                        yield
                        for t in range(NT):
                            for i in range(2):
                                job = f"far{t}{i}"
                                R.wait_filled(dve, job)
                                mask = table["group_chunk"][:].unsqueeze(1).to_broadcast([P, 2 * 4, GRP])
                                R.is_emptied(dve.tensor_tensor(far[:, t, 4 * i:4 * i + 4, :].rearrange("p h (g t) -> p (h g) t", t=GRP),
                                                               R.tile(job)[:].rearrange("p (n t) -> p n t", t=GRP), mask, ALU.mult), job)
                        yield
                        yield
                        R.wait_filled(dve, "back")
                        R.is_emptied(dve.tensor_tensor(og[:].rearrange("p t (h v) -> p (t h) v", v=GDK),
                                                       R.tile("back")[:].rearrange("p (h v) -> p h v", v=2 * GDK)[:, :, 0:GDK],
                                                       den[:].rearrange("p t (h v) -> p (t h) v", v=GDK), ALU.mult), "back")
                        R.wait_emptied(dve, "back")
                        heads = og[:].rearrange("p t (h v) -> p (t h) v", v=GDK)
                        step(dve.tensor_tensor(og_sq[:], og[:], og[:], ALU.mult))
                        step(dve.tensor_reduce(og_ms[:], og_sq[:].rearrange("p t (h v) -> p (t h) v", v=GDK), AX_X, ALU.add))
                        dve.tensor_scalar(og_ms[:], og_ms[:], 1.0 / GDK, EPS, ALU.mult, ALU.add).then_inc(S["og_ms_ready"], 1)
                        yield
                        dve.wait_ge(S["og_rms_ready"], 1)
                        dve.tensor_tensor(heads, heads, og_rms[:].unsqueeze(2).to_broadcast([P, NT * GH, GDK]), ALU.mult).then_inc(S["og_ready"], 1)
                        yield
                        R.wait_filled(dve, "attn")
                        dve.wait_ge(S["silu_y_ready"], 1)
                        R.is_emptied(dve.tensor_tensor(attn[:].rearrange("p t d -> p (t d)"), R.tile("attn")[:, 0:T], silu_y[:].rearrange("p t d -> p (t d)"), ALU.mult), "attn")
                        R.wait_emptied(dve, "attn")
                        rows = x_all[:, bass.ds(late * NT, NT), :]
                        dve.scalar_tensor_tensor(attn[:], attn[:], 0.5, rows, ALU.mult, ALU.add).then_inc(S["x1_ready"], 1)
                        yield

                    def hidden(e):
                        job = f"in{e}"
                        dve.wait_ge(S["tanh_g_ready"], e + 1)
                        step(dve.scalar_tensor_tensor(hid[:, e % 2, :], tanh_g[:, e % 2, :], 1.0, M.tile(job)[:, 0:T], ALU.add, ALU.mult))
                        M.is_emptied(dve.tensor_tensor(hid[:, e % 2, :], hid[:, e % 2, :], M.tile(job)[:, T:2 * T], ALU.mult), job)

                    def moe():
                        yield
                        M.wait_emptied(dve, "route")
                        step(dve.tensor_scalar(score[:], score[:], 1.0, None, ALU.add))
                        step(dve.reciprocal(score[:], score[:]))
                        step(dve.tensor_tensor(sel[:], score[:], route_bias[:].unsqueeze(1).to_broadcast([P, NT, E]), ALU.add))
                        for t in range(NT):
                            last = dve.max(top8[:, t, :], sel[:, t, :])
                        step(last)
                        for t in range(NT):
                            last = dve.match_replace(sel_left[:, t, :], top8[:, t, :], sel[:, t, :], -3e38)
                        step(last)
                        step(dve.tensor_tensor(sel_left[:], sel_left[:], sel[:], ALU.not_equal))
                        step(dve.tensor_tensor(sel_left[:], sel_left[:], score[:], ALU.mult))
                        step(dve.tensor_reduce(mix_sum[:], sel_left[:], AX_X, ALU.add))
                        step(dve.reciprocal(mix_sum[:], mix_sum[:]))
                        for t in range(NT):
                            dve.tensor_scalar(mix[:, t, 0:E], sel_left[:, t, :], mix_sum[:, t:t + 1], 0.5 * ROUTE_SCALE, ALU.mult, ALU.mult).then_inc(S["mix_ready"], 1)
                        hidden(0)
                        yield
                        for e in range(1, E + 1):
                            hidden(e)
                            if e in pauses:
                                yield

                    if early is not None:
                        step(dve.tensor_copy(xin[:], x_all[:, bass.ds(early * NT, NT), :]))
                        for t in range(NT):
                            last = dve.bn_stats(stats[:, t, :], xin[:, t, :])
                        step(last)
                        for t in range(NT):
                            last = dve.bn_aggr(moments[:, t, :], stats[:, t, :])
                        step(last)
                        dve.tensor_scalar(var_eps[:], moments[:, :, 1], EPS, None, ALU.add).then_inc(S["var_ready"], 1)
                        dve.wait_ge(S["rstd_ready"], 1)
                        for t in range(NT):
                            last = dve.tensor_scalar(xn[:, t, :], xin[:, t, :], moments[:, t, 0:1], rstd[:, t:t + 1], ALU.subtract, ALU.mult)
                        last.then_inc(S["xn_ready"], 1)
                    run_stages(*streams(slot_attention, read_out, moe))

            with nc.Block() as block:
                @block.sync
                def _(sync):
                    sync.sem_clear(per_batch)

        step_of(0, None)
        with nc.Fori(0, B - 1) as b:
            step_of(b + 1, b)
        step_of(None, B - 1)


def layer1(nc, x1, out, wa, wf, const, psum):
    LSTEP = LA // LF
    ctx = ExitStack()
    with ctx:
        def sb(name, *shape):
            return ctx.enter_context(nc.sbuf_tensor(name, list(shape), F32))

        def sem(name):
            return ctx.enter_context(nc.semaphore(name))

        tables = sb("layer1_tables", P, sum(width for width in const[1]))
        table = slices_of(tables, const)
        ident = table["ident"]
        x_enc, x_loc = sb("x_enc", P, B * NT, D), sb("x_loc", P, B * NT, D)
        x_in = sb("x_in", P, B * NT, D)
        half_pow = sb("half_pow1", P, 2 * B * NT)
        e_w, e_col, e_row = sb("e_w", P, LSTEP, ENC_W), sb("e_col", P, LSTEP, 5 + NB), sb("e_row", P, LSTEP, 4, D)
        l_w, l_col, l_row = sb("l_w", P, LOC_W), sb("l_col", P, 2 + 2 * len(HBLK)), sb("l_row", P, D + 4 * FDH)
        assert LF == 2
        e_next = [sb("e_w_next", P, LSTEP, ENC_W), sb("e_col_next", P, LSTEP, 5 + NB), sb("e_row_next", P, LSTEP, 4, D)]
        l_next = [sb("l_w_next", P, LOC_W), sb("l_col_next", P, 2 + 2 * len(HBLK)), sb("l_row_next", P, D + 4 * FDH)]

        def weight_loads(n, enc, loc):
            w_pairs = [(enc[0][:], wa["w"][n]), (loc[0][:], wf["w"][n]), (enc[1][:], wa["col"][n]), (loc[1][:], wf["col"][n]),
                       (enc[2][:], wa["row"][n].partition_broadcast(P)), (loc[2][:], wf["row"][n].partition_broadcast(P))]
            return w_pairs

        first_weights = weight_loads(0, [e_w, e_col, e_row], [l_w, l_col, l_row])
        last_weights = weight_loads(1, e_next, l_next)
        w_loaded, w_next_loaded, w_step = sem("w_loaded"), sem("w_next_loaded"), sem("w_step")
        wq, wkv, wo = e_w[:, :, 0:D], e_w[:, :, D:3 * D], e_w[:, :, 3 * D:4 * D]
        w1, w2 = e_w[:, :, 4 * D:4 * D + FF], e_w[:, :, 4 * D + FF:ENC_W].rearrange("p l (a n) -> p l a n", n=D)
        bq, ln_s, ln_b = e_col[:, :, 0], e_col[:, :, 1:3], e_col[:, :, 3:5]
        b1 = e_col[:, :, 5:5 + NB]
        bkv, bo, b2 = e_row[:, :, 0:2, :], e_row[:, :, 2, :], e_row[:, :, 3, :]
        at_wo, at_w1 = 3 * INNER, 3 * INNER + NB * D
        at_w2 = at_w1 + 2 * HID
        l_wqkv, l_wo = l_w[:, 0:at_wo], l_w[:, at_wo:at_w1].rearrange("p (a n) -> p a n", n=D)
        l_w1, l_w2 = l_w[:, at_w1:at_w2], l_w[:, at_w2:LOC_W].rearrange("p (a n) -> p a n", n=D)
        l_g, l_bias = l_col[:, 0:1], l_col[:, 1:2]
        l_b1 = l_col[:, 2:2 + 2 * len(HBLK)].rearrange("p (a n) -> p a n", a=2)
        l_b2, qk_scale = l_row[:, 0:D], l_row[:, D:D + 4 * FDH]
        rot = sb("l_rot", P, NT, 4, FDH)
        lnf_s, lnf_b = sb("lnf_s", P, D), sb("lnf_b", P, D)

        stats, moments = sb("stats1", P, B * NT, 6), sb("moments1", P, B * NT, 2)
        var_eps, rstd = sb("var_eps1", P, B * NT), sb("rstd1", P, B * NT)
        loads, first, root = sem("b_loads"), sem("b_first_step"), sem("b_root")
        pairs = [
            (x_in[:], x1.rearrange("b (t p) d -> p (b t) d", p=P)), (tables[:], const[0]),
            (lnf_s[:], wa["lnf_s"].partition_broadcast(P)), (lnf_b[:], wa["lnf_b"].partition_broadcast(P))]
        with nc.Block() as block:
            @block.sync
            def _(sync):
                for dst, src in pairs:
                    sync.dma_start(dst, src).then_inc(loads, 16)
                for dst, src in first_weights:
                    sync.dma_start(dst, src).then_inc(w_loaded, 16)
                for dst, src in last_weights:
                    sync.dma_start(dst, src).then_inc(w_next_loaded, 16)

            @block.gpsimd
            def _(pool):
                pool.memset(half_pow[:], -0.5).then_inc(root, 1)
                pool.wait_ge(root, 2)
                pool.tensor_tensor(rstd[:], var_eps[:], half_pow[:, 0:B * NT], ALU.pow).then_inc(root, 1)

            @block.vector
            def _(dve):
                step = Chain(dve, first)
                dve.wait_ge(loads, 16 * len(pairs))
                for n in range(B * NT):
                    last = dve.bn_stats(stats[:, n, :], x_in[:, n, :])
                step(last)
                for n in range(B * NT):
                    last = dve.bn_aggr(moments[:, n, :], stats[:, n, :])
                step(last)
                dve.tensor_scalar(var_eps[:], moments[:, :, 1], EPS, None, ALU.add).then_inc(root, 1)
                dve.wait_ge(root, 3)
                for n in range(B * NT):
                    last = dve.tensor_scalar(x_loc[:, n, :], x_in[:, n, :], moments[:, n, 0:1], rstd[:, n:n + 1], ALU.subtract, ALU.mult)
                step(last)
                pos = table["pos_emb"][:]
                for n in range(B):
                    dve.scalar_tensor_tensor(x_enc[:, NT * n:NT * (n + 1), :].rearrange("p t d -> p (t d)"),
                                             x_loc[:, NT * n:NT * (n + 1), :].rearrange("p t d -> p (t d)"), float(np.sqrt(D)), pos, ALU.mult, ALU.add)

        def encoder_buffers(i):
            n = lambda name, *shape: sb(f"e{i}_{name}", *shape)
            return dict(
                x=n("x", P, NT, D), xb=n("xb", P, NT, D), stats=n("stats", P, NT, 6), mom=n("mom", P, NT, 2),
                var=n("var", P, NT), rstd=n("rstd", P, NT), n=n("n", P, NT, D), h=n("h", P, T),
                q_neg=n("q_neg", P, T), q_pos=n("q_pos", P, T),
                kv1=n("kv1", P, NT, 2 * D + 1),
                k_neg=n("k_neg", P, NT, D), kv_mat=n("kv_mat", P, D), k_mat=n("k_mat", P, D),
                rec=n("rec", P, T), attn=n("attn", P, T), ff=n("ff", P, NB, T))

        EB = [encoder_buffers(i) for i in range(LSTEP)]

        l_x, l_x2, l_xb = sb("l_x", P, NT, D), sb("l_x2", P, NT, D), sb("l_xb", P, NT, D)
        l_h = sb("l_h", P, T)
        qk, sq, turned = sb("l_qk", P, NT, 2 * FH, FDH), sb("l_sq", P, NT, 2 * FH, FDH), sb("l_turned", P, NT, 2 * FH, FDH)
        norm2, rnorm = sb("norm2", P, NT, 2 * FH), sb("rnorm", P, NT, 2 * FH)
        v, v_prev = sb("l_v", P, NT, INNER), sb("v_prev", WIN, INNER)
        q_t, k_t = sb("l_q_t", P, NB, T), sb("l_k_t", P, NB, T)
        sim = [sb("sim0", P, FH, P), sb("sim1", P, FH, KEYS)]
        neg_max, sim_sum, sim_rec = sb("neg_max", P, NT, FH), sb("sim_sum", P, NT, FH), sb("sim_rec", P, NT, FH)
        own_t, prev_t = sb("own_t", P, NT, FH, P), sb("prev_t", WIN, FH, P)
        o_t = sb("l_o_t", P, NB, T)
        l_s, l_n, l_h2 = sb("l_s", P, NT, D), sb("l_n", P, NT, D), sb("l_h2", P, T)
        l_stats, l_mom = sb("l_stats", P, NT, 6), sb("l_mom", P, NT, 2)
        l_var, l_rstd = sb("l_var", P, NT), sb("l_rstd", P, NT)
        gelu, l_ff = sb("l_gelu", P, len(HBLK), T), sb("l_ff", P, len(HBLK), T)

        e_jobs = ["h", "q", "kv", "mat", "read", "out", "h2", "ff0", "ff1", "out2"]
        a_jobs = ["x_t", "q0", "k0", "v0", "q1", "k1", "v1", "vp", "qt0", "kt0", "qt1", "kt1", "s00", "s01", "s10", "s11", "s12", "s13"]
        f_jobs = ["own00", "own01", "o0", "own10", "own11", "prev0", "prev1", "o1", "wo", "shift", "h2_t", "ff0", "ff1", "ff2", "w2"]
        En = [Banks(ctx, nc, f"enc{i}", psum[2 * i:2 * i + 2], e_jobs) for i in range(LSTEP)]
        Lo = Banks(ctx, nc, "scores", psum[4:6], a_jobs)
        Ff = Banks(ctx, nc, "mix", psum[6:8], f_jobs)
        e_names = ["x_copied", "var", "rstd", "normed", "q_min", "q_exp", "q_ready", "k_min", "k_exp", "k_ready", "xb"]
        l_names = ["x_copied", "squared0", "squared1", "norm2_0", "norm2_1", "rnorm0", "rnorm1", "scaled0", "scaled1", "turned0", "turned1",
                   "rotated0", "rotated1", "neg_max0", "neg_max1", "exp0", "exp1", "divided"]
        f_names = ["x_copied", "xb", "h_half", "var", "rstd", "normed", "gelu"]
        SE = [{n: sem(f"e{i}_{n}") for n in e_names} for i in range(LSTEP)]
        SL = {n: sem(f"l_{n}") for n in l_names}
        SF = {n: sem(f"f_{n}") for n in f_names}
        dve_step = sem("b_dve_step")
        per_batch = range(En[0].filled[0].num, dve_step.num + 1)

        HALF = FDH // 2

        with nc.Block() as block:
            @block.gpsimd
            def _(pool):
                for e in EB:
                    pool.memset(e["kv1"][:, :, 2 * D:2 * D + 1], 1.0)

            @block.vector
            def _(dve):
                dve.memset(l_h[D // 2:D, 0:1], 0.0)

        with nc.Fori(0, LF):
            with nc.Block() as block:
                @block.vector
                def _(dve):
                    dve.wait_ge(w_loaded, 16 * len(first_weights))
                    src = table["rotary"][:].rearrange("p (t a) -> p t a", t=NT)
                    sc = qk_scale
                    dst = rot[:].rearrange("p t a d -> p t (a d)")
                    for n, by in ((0, 8.0), (1, 1.0)):
                        cols = slice(n * 2 * FDH, (n + 1) * 2 * FDH)
                        for t in range(NT):
                            dve.scalar_tensor_tensor(dst[:, t, cols], src[:, t, cols], by, sc[:, cols], ALU.mult, ALU.mult).then_inc(w_step, 1)
                    dve.wait_ge(w_step, 2 * NT)

            def step_of(early, late):
                def streams(enc, scores, mix):
                    live = [late is not None and enc(1, late), early is not None and enc(0, early),
                            late is not None and mix(late), early is not None and scores(early)]
                    return [s for s in live if s]

                with nc.Block() as block:
                    @block.tensor
                    def _(pe):
                        def enc(i, b):
                            e = EB[i]

                            def turn(job, src):
                                En[i].wait_free(pe, job)
                                for t in range(NT):
                                    last = pe.transpose(En[i].tile(job)[:, t * P:(t + 1) * P], src[:, t, :], ident[:])
                                En[i].is_filled(last, job)

                            pe.wait_ge(SE[i]["normed"], 1)
                            turn("h", e["n"])
                            yield
                            En[i].wait_emptied(pe, "h")
                            job = "q"
                            En[i].wait_free(pe, job)
                            En[i].is_filled(pe.matmul(En[i].tile(job)[:, 0:T], wq[:, i, :], e["h"][:], start=True, stop=True), job)
                            job = "kv"
                            En[i].wait_free(pe, job)
                            for t in range(NT):
                                last = pe.matmul(En[i].tile(job)[:, t * 2 * D:(t + 1) * 2 * D], e["h"][:, t * P:(t + 1) * P],
                                                 wkv[:, i, :], start=True, stop=True)
                            En[i].is_filled(last, job)
                            yield
                            job = "mat"
                            En[i].wait_free(pe, job)
                            pe.wait_ge(SE[i]["k_ready"], 1)
                            for t in range(NT):
                                last = pe.matmul(En[i].tile(job)[:, 0:D + 1], e["kv1"][:, t, 0:D], e["kv1"][:, t, D:2 * D + 1], start=(t == 0), stop=(t == NT - 1))
                            En[i].is_filled(last, job)
                            yield
                            job = "read"
                            En[i].wait_free(pe, job)
                            En[i].wait_emptied(pe, "mat")
                            pe.wait_ge(SE[i]["q_ready"], 1)
                            pe.matmul(En[i].tile(job)[:, 0:T], e["kv_mat"][:], e["q_pos"][:], start=True, stop=True)
                            En[i].is_filled(pe.matmul(En[i].tile(job)[:, T:2 * T], e["k_mat"][:], e["q_pos"][:], start=True, stop=True), job)
                            yield
                            job = "out"
                            En[i].wait_free(pe, job)
                            En[i].wait_emptied(pe, "read")
                            for t in range(NT):
                                last = pe.matmul(En[i].tile(job)[:, t * D:(t + 1) * D], e["attn"][:, t * P:(t + 1) * P], wo[:, i, :], start=True, stop=True)
                            En[i].is_filled(last, job)
                            yield
                            pe.wait_ge(SE[i]["normed"], 2)
                            turn("h2", e["n"])
                            yield
                            En[i].wait_emptied(pe, "h2")
                            for a in range(2):
                                job = f"ff{a}"
                                En[i].wait_free(pe, job)
                                for n in range(2):
                                    blk = 2 * a + n
                                    last = pe.matmul(En[i].tile(job)[:, n * T:(n + 1) * T], w1[:, i, blk * P:(blk + 1) * P], e["h"][:], start=True, stop=True)
                                En[i].is_filled(last, job)
                            yield
                            job = "out2"
                            En[i].wait_free(pe, job)
                            for a in range(2):
                                En[i].wait_emptied(pe, f"ff{a}")
                            for t in range(NT):
                                for n in range(NB):
                                    last = pe.matmul(En[i].tile(job)[:, t * D:(t + 1) * D], e["ff"][:, n, t * P:(t + 1) * P], w2[:, i, n, :],
                                                     start=(n == 0), stop=(n == NB - 1))
                            En[i].is_filled(last, job)
                            yield

                        def scores(b):
                            yield
                            Lo.wait_emptied(pe, "x_t")
                            for t in range(NT):
                                for n, name in enumerate("qkv"):
                                    job = f"{name}{t}"
                                    Lo.wait_free(pe, job)
                                    Lo.is_filled(pe.matmul(Lo.tile(job)[:], l_h[:, t * P:(t + 1) * P], l_wqkv[:, n * INNER:(n + 1) * INNER],
                                                           start=True, stop=True), job)
                                if t:
                                    Lo.wait_free(pe, "vp")
                                    Lo.is_filled(pe.matmul(Lo.tile("vp")[0:WIN, :], l_h[:, WIN:P], l_wqkv[:, 2 * INNER:3 * INNER], start=True, stop=True), "vp")
                                yield
                            for t in range(NT):
                                pe.wait_ge(SL[f"rotated{t}"], 1)
                                for a, name in enumerate(("qt", "kt")):
                                    job = f"{name}{t}"
                                    Lo.wait_free(pe, job)
                                    for j in range(NB):
                                        src = qk[:, t, FH * a + 2 * j:FH * a + 2 * j + 2, :].rearrange("p h d -> p (h d)")
                                        last = pe.transpose(Lo.tile(job)[:, j * P:(j + 1) * P], src, ident[:])
                                    Lo.is_filled(last, job)
                                yield
                            for t in range(NT):
                                Lo.wait_emptied(pe, f"qt{t}")
                                Lo.wait_emptied(pe, f"kt{t}")
                                per = 4 if t == 0 else 2
                                keys = P if t == 0 else KEYS
                                for n in range(FH // per):
                                    job = f"s{t}{n}"
                                    Lo.wait_free(pe, job)
                                    rows = slice(FDH * (n % 2), FDH * (n % 2) + FDH)
                                    for i in range(per):
                                        j = (n // 2) * per + i
                                        last = pe.matmul(Lo.tile(job)[:, i * keys:(i + 1) * keys], q_t[rows, j, t * P:(t + 1) * P],
                                                         k_t[rows, j, (t + 1) * P - keys:(t + 1) * P], start=True, stop=True)
                                    Lo.is_filled(last, job)
                                yield

                        def turn_scores(job, t, a, rows, keys):
                            Ff.wait_free(pe, job)
                            for n in range(4):
                                last = pe.transpose(Ff.tile(job)[0:rows, n * P:(n + 1) * P], sim[t][:, 4 * a + n, keys], ident[:])
                            Ff.is_filled(last, job)

                        def mix(b):
                            def attend(t):
                                job = f"o{t}"
                                Ff.wait_free(pe, job)
                                for h in range(FH):
                                    if h % 4 == 0:
                                        Ff.wait_emptied(pe, f"own{t}{h // 4}")
                                        if t:
                                            Ff.wait_emptied(pe, f"prev{h // 4}")
                                    cols, at = slice(h * FDH, (h + 1) * FDH), FDH * (h % 2)
                                    dst = Ff.tile(job)[at:at + FDH, (h // 2) * P:(h // 2 + 1) * P]
                                    last = pe.matmul(dst, v[:, t, cols], own_t[:, t, h, :], start=True, stop=(t == 0))
                                    if t:
                                        last = pe.matmul(dst, v_prev[:, cols], prev_t[:, h, :], start=False, stop=True)
                                Ff.is_filled(last, job)

                            yield
                            attend(0)
                            turn_scores("own10", 1, 0, P, slice(WIN, WIN + P))
                            turn_scores("own11", 1, 1, P, slice(WIN, WIN + P))
                            yield
                            turn_scores("prev0", 1, 0, WIN, slice(0, WIN))
                            turn_scores("prev1", 1, 1, WIN, slice(0, WIN))
                            yield
                            attend(1)
                            yield
                            Ff.wait_free(pe, "wo")
                            for t in range(NT):
                                Ff.wait_emptied(pe, f"o{t}")
                                for j in range(NB):
                                    last = pe.matmul(Ff.tile("wo")[:, t * D:(t + 1) * D], o_t[:, j, t * P:(t + 1) * P], l_wo[:, j, :],
                                                     start=(j == 0), stop=(j == NB - 1))
                            Ff.is_filled(last, "wo")
                            yield
                            Ff.wait_free(pe, "shift")
                            Ff.wait_emptied(pe, "wo")
                            late = l_x2[:, :, D // 2:D]
                            pe.matmul(Ff.tile("shift")[:, 0:D // 2], table["next_token"][:], late[:, 0, :], start=True, stop=True)
                            pe.matmul(Ff.tile("shift")[:, D // 2:D], table["next_token"][:], late[:, 1, :], start=True, stop=False)
                            Ff.is_filled(pe.matmul(Ff.tile("shift")[:, D // 2:D], table["next_tile"][:], late[:, 0, :], start=False, stop=True), "shift")
                            yield
                            Ff.wait_free(pe, "h2_t")
                            pe.wait_ge(SF["normed"], 1)
                            for t in range(NT):
                                last = pe.transpose(Ff.tile("h2_t")[:, t * P:(t + 1) * P], l_n[:, t, :], ident[:])
                            Ff.is_filled(last, "h2_t")
                            yield
                            Ff.wait_emptied(pe, "h2_t")
                            for n, (at, size) in enumerate(HBLK):
                                job = f"ff{n}"
                                Ff.wait_free(pe, job)
                                for a in range(2):
                                    last = pe.matmul(Ff.tile(job)[0:size, a * T:(a + 1) * T], l_w1[:, a * HID + at:a * HID + at + size], l_h2[:], start=True, stop=True)
                                Ff.is_filled(last, job)
                                if n:
                                    yield
                            Ff.wait_free(pe, "w2")
                            for n in range(len(HBLK)):
                                Ff.wait_emptied(pe, f"ff{n}")
                            for t in range(NT):
                                for n, (at, size) in enumerate(HBLK):
                                    last = pe.matmul(Ff.tile("w2")[:, t * D:(t + 1) * D], l_ff[0:size, n, t * P:(t + 1) * P], l_w2[0:size, n, :],
                                                     start=(n == 0), stop=(n == len(HBLK) - 1))
                            Ff.is_filled(last, "w2")

                        if late is not None:
                            turn_scores("own00", 0, 0, P, slice(0, P))
                            turn_scores("own01", 0, 1, P, slice(0, P))
                        if early is not None:
                            pe.wait_ge(SL["x_copied"], 1)
                            for t in range(NT):
                                last = pe.transpose(Lo.tile("x_t")[:, t * P:(t + 1) * P], l_x[:, t, :], ident[:])
                            Lo.is_filled(last, "x_t")
                        run_stages(*streams(enc, scores, mix))

                    @block.scalar
                    def _(act):
                        def enc(i, b):
                            e = EB[i]
                            job = "h"
                            En[i].wait_filled(act, job)
                            En[i].is_emptied(act.activation(e["h"][:], En[i].tile(job)[:, 0:T], ACT.Identity, scale=ln_s[:, i, 0:1], bias=ln_b[:, i, 0:1]), job)
                            yield
                            job = "q"
                            act.wait_ge(SE[i]["q_min"], 1)
                            En[i].is_emptied(act.activation(e["q_pos"][:], En[i].tile(job)[:, 0:T], ACT.Relu, bias=bq[:, i:i + 1]), job)
                            act.activation(e["q_neg"][:], e["q_neg"][:], ACT.Exp).then_inc(SE[i]["q_exp"], 1)
                            act.wait_ge(SE[i]["k_min"], 1)
                            act.activation(e["k_neg"][:], e["k_neg"][:], ACT.Exp).then_inc(SE[i]["k_exp"], 1)
                            yield
                            yield
                            yield
                            yield
                            job = "h2"
                            En[i].wait_filled(act, job)
                            En[i].is_emptied(act.activation(e["h"][:], En[i].tile(job)[:, 0:T], ACT.Identity, scale=ln_s[:, i, 1:2], bias=ln_b[:, i, 1:2]), job)
                            yield
                            for a in range(2):
                                job = f"ff{a}"
                                En[i].wait_filled(act, job)
                                for n in range(2):
                                    blk = 2 * a + n
                                    last = act.activation(e["ff"][:, blk, :], En[i].tile(job)[:, n * T:(n + 1) * T], ACT.Relu, bias=b1[:, i, blk:blk + 1])
                                En[i].is_emptied(last, job)
                            yield
                            yield

                        def scores(b):
                            Lo.wait_filled(act, "x_t")
                            act.activation(l_h[0:D // 2, :], Lo.tile("x_t")[0:D // 2, 0:T], ACT.Copy)
                            Lo.is_emptied(act.activation(l_h[D // 2:D, 1:T], Lo.tile("x_t")[D // 2:D, 0:T - 1], ACT.Copy), "x_t")
                            yield
                            for t in range(NT):
                                for a, name in enumerate("qk"):
                                    job = f"{name}{t}"
                                    Lo.wait_filled(act, job)
                                    Lo.is_emptied(act.activation(qk[:, t, FH * a:FH * (a + 1), :].rearrange("p h d -> p (h d)"), Lo.tile(job)[:], ACT.Copy), job)
                                for name in "qk":
                                    Lo.wait_emptied(act, f"{name}{t}")
                                act.activation(sq[:, t], qk[:, t], ACT.Square).then_inc(SL[f"squared{t}"], 1)
                                if late is not None:
                                    Ff.wait_filled(act, f"o{t}")
                                job = f"v{t}"
                                Lo.wait_filled(act, job)
                                Lo.is_emptied(act.activation(v[:, t, :], Lo.tile(job)[:], ACT.Copy), job)
                                if t:
                                    Lo.wait_filled(act, "vp")
                                    Lo.is_emptied(act.activation(v_prev[:], Lo.tile("vp")[0:WIN, :], ACT.Copy), "vp")
                                yield
                            for t in range(NT):
                                for name, dst in (("qt", q_t), ("kt", k_t)):
                                    job = f"{name}{t}"
                                    Lo.wait_filled(act, job)
                                    Lo.is_emptied(act.activation(dst[:, :, t * P:(t + 1) * P], Lo.tile(job)[:].rearrange("p (j t) -> p j t", t=P), ACT.Copy), job)
                                yield
                            for t in range(NT):
                                act.wait_ge(SL[f"neg_max{t}"], 1)
                                for h in range(FH):
                                    act.activation(sim[t][:, h, :], sim[t][:, h, :], ACT.Exp, bias=neg_max[:, t, h:h + 1],
                                                   accum_out=sim_sum[:, t, h:h + 1]).then_inc(SL[f"exp{t}"], 1)
                                yield

                        def mix(b):
                            def keep(job, dst, rows):
                                Ff.wait_filled(act, job)
                                Ff.is_emptied(act.activation(dst, Ff.tile(job)[0:rows, :].rearrange("p (h t) -> p h t", t=P), ACT.Copy), job)

                            keep("own00", own_t[:, 0, 0:4, :], P)
                            yield
                            keep("o0", o_t[:, :, 0:P], P)
                            keep("own10", own_t[:, 1, 0:4, :], P)
                            yield
                            keep("prev0", prev_t[:, 0:4, :], WIN)
                            yield
                            keep("o1", o_t[:, :, P:T], P)
                            yield
                            yield
                            Ff.wait_filled(act, "shift")
                            Ff.is_emptied(act.activation(l_s[:, :, D // 2:D], Ff.tile("shift")[:, 0:D].rearrange("p (t d) -> p t d", t=NT), ACT.Copy), "shift")
                            yield
                            Ff.wait_filled(act, "h2_t")
                            Ff.is_emptied(act.activation(l_h2[:], Ff.tile("h2_t")[:, 0:T], ACT.Identity, scale=l_g, bias=l_bias), "h2_t")
                            yield
                            for n, (at, size) in enumerate(HBLK):
                                job = f"ff{n}"
                                Ff.wait_filled(act, job)
                                act.activation(gelu[0:size, n, :], Ff.tile(job)[0:size, T:2 * T], ACT.Gelu, bias=l_b1[0:size, 1, n:n + 1]).then_inc(SF["gelu"], 1)
                                if n:
                                    yield

                        if early is not None:
                            act.activation(l_x[:], x_loc[:, bass.ds(early * NT, NT), :], ACT.Copy).then_inc(SL["x_copied"], 1)
                        run_stages(*streams(enc, scores, mix))

                    @block.gpsimd
                    def _(pool):
                        def bias_first(dst, src, bias, done):
                            pool.tensor_tensor(dst[:], src[:], bias.unsqueeze(1).to_broadcast([P, NT, D]), ALU.add).then_inc(done, 1)

                        def enc(i, b):
                            e = EB[i]
                            pool.wait_ge(SE[i]["x_copied"], 1)
                            for n, (bias, jobs) in enumerate(((bo, "out"), (b2, "out2"))):
                                pool.wait_ge(SE[i]["var"], n + 1)
                                pool.tensor_tensor(e["rstd"][:], e["var"][:], half_pow[:, 0:NT], ALU.pow).then_inc(SE[i]["rstd"], 1)
                                bias_first(e["xb"], e["x"], bias[:, i, :], SE[i]["xb"])
                                for _ in range(4):
                                    yield

                        def scores(b):
                            yield
                            for t in range(NT):
                                for name in "qk":
                                    Lo.wait_emptied(pool, f"{name}{t}")
                                for half in range(2):
                                    to, src = slice(half * HALF, (half + 1) * HALF), slice((1 - half) * HALF, (2 - half) * HALF)
                                    for a in range(2):
                                        hs = slice(FH * a, FH * (a + 1))
                                        by = rot[:, t, 2 * a + 1, to].unsqueeze(1).to_broadcast([P, FH, HALF])
                                        pool.tensor_tensor(turned[:, t, hs, to], qk[:, t, hs, src], by, ALU.mult).then_inc(SL[f"turned{t}"], 1)
                                pool.wait_ge(SL[f"norm2_{t}"], 1)
                                pool.tensor_tensor(rnorm[:, t, :], norm2[:, t, :], half_pow[:, 0:2 * FH], ALU.pow).then_inc(SL[f"rnorm{t}"], 1)
                                yield

                        def mix(b):
                            for _ in range(4):
                                yield
                            Ff.wait_emptied(pool, "wo")
                            pool.tensor_copy(l_s[:, :, 0:D // 2], l_x2[:, :, 0:D // 2]).then_inc(SF["h_half"], 1)
                            yield
                            pool.wait_ge(SF["var"], 1)
                            pool.tensor_tensor(l_rstd[:], l_var[:], half_pow[:, 0:NT], ALU.pow).then_inc(SF["rstd"], 1)
                            bias_first(l_xb, l_x2, l_b2, SF["xb"])
                            yield

                        if late is not None:
                            pool.tensor_copy(l_x2[:], x_loc[:, bass.ds(late * NT, NT), :]).then_inc(SF["x_copied"], 1)
                        run_stages(*streams(enc, scores, mix))

                    @block.vector
                    def _(dve):
                        step = Chain(dve, dve_step)

                        def moments_of(x, stats, mom, var, S):
                            for t in range(NT):
                                last = dve.bn_stats(stats[:, t, :], x[:, t, :])
                            step(last)
                            for t in range(NT):
                                last = dve.bn_aggr(mom[:, t, :], stats[:, t, :])
                            step(last)
                            dve.tensor_scalar(var[:], mom[:, :, 1], EPS, None, ALU.add).then_inc(S["var"], 1)

                        def normalise(x, mom, rstd, out, S, n):
                            dve.wait_ge(S["rstd"], n)
                            for t in range(NT):
                                last = dve.tensor_scalar(out[:, t, :], x[:, t, :], mom[:, t, 0:1], rstd[:, t:t + 1], ALU.subtract, ALU.mult)
                            last.then_inc(S["normed"], 1)

                        def enc(i, b):
                            e = EB[i]
                            two = lambda a: a.rearrange("p (t d) -> p t d", t=NT)
                            normalise(e["x"], e["mom"], e["rstd"], e["n"], SE[i], 1)
                            yield
                            job = "q"
                            En[i].wait_filled(dve, job)
                            dve.tensor_scalar(e["q_neg"][:], En[i].tile(job)[:, 0:T], bq[:, i:i + 1], 0.0, ALU.add, ALU.min).then_inc(SE[i]["q_min"], 1)
                            job = "kv"
                            En[i].wait_filled(dve, job)
                            En[i].is_emptied(dve.tensor_tensor(e["kv1"][:, :, 0:2 * D], En[i].tile(job)[:].rearrange("p (t n) -> p t n", t=NT),
                                                            bkv[:, i].rearrange("p a n -> p (a n)").unsqueeze(1).to_broadcast([P, NT, 2 * D]), ALU.add), job)
                            En[i].wait_emptied(dve, job)
                            dve.tensor_scalar(e["k_neg"][:], e["kv1"][:, :, 0:D], 0.0, None, ALU.min).then_inc(SE[i]["k_min"], 1)
                            dve.wait_ge(SE[i]["q_exp"], 1)
                            dve.tensor_tensor(e["q_pos"][:], e["q_pos"][:], e["q_neg"][:], ALU.add).then_inc(SE[i]["q_ready"], 1)
                            dve.wait_ge(SE[i]["k_exp"], 1)
                            dve.scalar_tensor_tensor(e["kv1"][:, :, 0:D], e["kv1"][:, :, 0:D], 0.0, e["k_neg"][:], ALU.max, ALU.add).then_inc(SE[i]["k_ready"], 1)
                            yield
                            job = "mat"
                            En[i].wait_filled(dve, job)
                            dve.tensor_tensor(e["kv_mat"][:], En[i].tile(job)[:, 0:D], table["head_block"][:], ALU.mult)
                            En[i].is_emptied(dve.tensor_scalar(e["k_mat"][:], table["head_block"][:], En[i].tile(job)[:, D:D + 1], None, ALU.mult), job)
                            yield
                            job = "read"
                            En[i].wait_filled(dve, job)
                            step(dve.tensor_scalar(e["rec"][:], En[i].tile(job)[:, T:2 * T], 1e-6, None, ALU.add))
                            step(dve.reciprocal(e["rec"][:], e["rec"][:]))
                            En[i].is_emptied(dve.tensor_tensor(e["attn"][:], En[i].tile(job)[:, 0:T], e["rec"][:], ALU.mult), job)
                            yield
                            job = "out"
                            En[i].wait_filled(dve, job)
                            dve.wait_ge(SE[i]["xb"], 1)
                            En[i].is_emptied(dve.tensor_tensor(e["x"][:], two(En[i].tile(job)[:, 0:T]), e["xb"][:], ALU.add), job)
                            En[i].wait_emptied(dve, job)
                            moments_of(e["x"], e["stats"], e["mom"], e["var"], SE[i])
                            yield
                            normalise(e["x"], e["mom"], e["rstd"], e["n"], SE[i], 2)
                            yield
                            yield
                            job = "out2"
                            En[i].wait_filled(dve, job)
                            dve.wait_ge(SE[i]["xb"], 2)
                            En[i].is_emptied(dve.tensor_tensor(x_enc[:, bass.ds(b * NT, NT), :], two(En[i].tile(job)[:, 0:T]), e["xb"][:], ALU.add), job)
                            En[i].wait_emptied(dve, job)
                            yield

                        def scores(b):
                            yield
                            def rotate(t):
                                dve.wait_ge(SL[f"squared{t}"], 1)
                                step(dve.tensor_reduce(norm2[:, t, :], sq[:, t], AX_X, ALU.add))
                                dve.tensor_scalar(norm2[:, t, :], norm2[:, t, :], 1e-24, None, ALU.max).then_inc(SL[f"norm2_{t}"], 1)
                                for a in range(2):
                                    hs = slice(FH * a, FH * (a + 1))
                                    last = dve.tensor_tensor(sq[:, t, hs, :], qk[:, t, hs, :], rot[:, t, 2 * a, :].unsqueeze(1).to_broadcast([P, FH, FDH]), ALU.mult)
                                last.then_inc(SL[f"scaled{t}"], 1)

                            def finish(t):
                                dve.wait_ge(SL[f"scaled{t}"], 1)
                                dve.wait_ge(SL[f"turned{t}"], 4)
                                step(dve.tensor_tensor(sq[:, t], sq[:, t], turned[:, t], ALU.add))
                                dve.wait_ge(SL[f"rnorm{t}"], 1)
                                dve.tensor_tensor(qk[:, t], sq[:, t], rnorm[:, t, :].unsqueeze(2).to_broadcast([P, 2 * FH, FDH]), ALU.mult).then_inc(SL[f"rotated{t}"], 1)

                            rotate(0)
                            yield
                            rotate(1)
                            finish(0)
                            yield
                            finish(1)
                            yield
                            yield

                            def divide(t):
                                dve.wait_ge(SL[f"exp{t}"], FH)
                                step(dve.reciprocal(sim_rec[:, t, :], sim_sum[:, t, :]))
                                keys = P if t == 0 else KEYS
                                dve.tensor_tensor(sim[t][:], sim[t][:], sim_rec[:, t, :].unsqueeze(2).to_broadcast([P, FH, keys]), ALU.mult).then_inc(SL["divided"], 1)

                            for t in range(NT):
                                per = 4 if t == 0 else 2
                                keys = P if t == 0 else KEYS
                                mask = table["window"][:, t * KEYS + KEYS - keys:(t + 1) * KEYS].unsqueeze(1).to_broadcast([P, per, keys])
                                for n in range(FH // per):
                                    job = f"s{t}{n}"
                                    Lo.wait_filled(dve, job)
                                    h0 = n % 2 + 2 * (n // 2) * per
                                    Lo.is_emptied(dve.tensor_tensor(sim[t][:, h0:h0 + 2 * per - 1:2, :],
                                                                    Lo.tile(job)[:, 0:per * keys].rearrange("p (h k) -> p h k", k=keys), mask, ALU.add), job)
                                for n in range(FH // per):
                                    Lo.wait_emptied(dve, f"s{t}{n}")
                                dve.tensor_reduce(neg_max[:, t, :], sim[t][:], AX_X, ALU.max, negate=True).then_inc(SL[f"neg_max{t}"], 1)
                                if t:
                                    divide(0)
                                yield
                            divide(1)
                            dve.wait_ge(SL["divided"], NT)

                        def mix(b):
                            two = lambda a: a.rearrange("p (t d) -> p t d", t=NT)

                            def keep(job, dst, rows):
                                Ff.wait_filled(dve, job)
                                Ff.is_emptied(dve.tensor_copy(dst, Ff.tile(job)[0:rows, :].rearrange("p (h t) -> p h t", t=P)), job)

                            keep("own01", own_t[:, 0, 4:8, :], P)
                            yield
                            keep("own11", own_t[:, 1, 4:8, :], P)
                            yield
                            keep("prev1", prev_t[:, 4:8, :], WIN)
                            yield
                            yield
                            Ff.wait_filled(dve, "wo")
                            dve.wait_ge(SF["x_copied"], 1)
                            Ff.is_emptied(dve.tensor_tensor(l_x2[:], l_x2[:], two(Ff.tile("wo")[:, 0:T]), ALU.add), "wo")
                            yield
                            Ff.wait_emptied(dve, "shift")
                            dve.wait_ge(SF["h_half"], 1)
                            moments_of(l_s, l_stats, l_mom, l_var, SF)
                            normalise(l_s, l_mom, l_rstd, l_n, SF, 1)
                            yield
                            yield
                            for n, (at, size) in enumerate(HBLK):
                                job = f"ff{n}"
                                dve.wait_ge(SF["gelu"], n + 1)
                                Ff.is_emptied(dve.scalar_tensor_tensor(l_ff[0:size, n, :], Ff.tile(job)[0:size, 0:T], l_b1[0:size, 0, n:n + 1],
                                                                       gelu[0:size, n, :], ALU.add, ALU.mult), job)
                                if n:
                                    yield
                            Ff.wait_filled(dve, "w2")
                            dve.wait_ge(SF["xb"], 1)
                            Ff.is_emptied(dve.tensor_tensor(x_loc[:, bass.ds(b * NT, NT), :], two(Ff.tile("w2")[:, 0:T]), l_xb[:], ALU.add), "w2")
                            Ff.wait_emptied(dve, "w2")

                        for i, batch in ((1, late), (0, early)):
                            if batch is not None:
                                dve.tensor_copy(EB[i]["x"][:], x_enc[:, bass.ds(batch * NT, NT), :]).then_inc(SE[i]["x_copied"], 1)
                        for i, batch in ((1, late), (0, early)):
                            if batch is not None:
                                dve.wait_ge(SE[i]["x_copied"], 1)
                                moments_of(EB[i]["x"], EB[i]["stats"], EB[i]["mom"], EB[i]["var"], SE[i])
                        run_stages(*streams(enc, scores, mix))

                with nc.Block() as block:
                    @block.sync
                    def _(sync):
                        sync.sem_clear(per_batch)

            step_of(0, None)
            with nc.Fori(0, B - 1) as b:
                step_of(b + 1, b)
            step_of(None, B - 1)

            with nc.Block() as block:
                @block.sync
                def _(sync):
                    sync.sem_clear(w_step)

                @block.scalar
                def _(act):
                    act.wait_ge(w_next_loaded, 16 * len(last_weights))
                    for dst, src in zip((e_w, e_col, e_row), e_next):
                        act.activation(dst[:], src[:], ACT.Copy)

                @block.gpsimd
                def _(pool):
                    pool.wait_ge(w_next_loaded, 16 * len(last_weights))
                    pool.tensor_copy(l_w[:, 0:at_wo], l_next[0][:, 0:at_wo])

                @block.vector
                def _(dve):
                    dve.wait_ge(w_next_loaded, 16 * len(last_weights))
                    dve.tensor_copy(l_w[:, at_wo:LOC_W], l_next[0][:, at_wo:LOC_W])
                    dve.tensor_copy(l_col[:], l_next[1][:])
                    dve.tensor_copy(l_row[:], l_next[2][:])

        fin = ctx.enter_context(nc.semaphore("final_step"))
        root2, tanh_done, stored = sem("final_root"), sem("final_tanh"), sem("stored")
        silu = sq[:].rearrange("p t h d -> p (t h d)").rearrange("p (n d) -> p n d", d=D)
        with nc.Block() as block:
            @block.scalar
            def _(act):
                act.activation(silu, x_loc[:], ACT.Tanh, scale=0.5).then_inc(tanh_done, 1)

            @block.gpsimd
            def _(pool):
                pool.wait_ge(root2, 1)
                pool.tensor_tensor(rstd[:], var_eps[:], half_pow[:, 0:B * NT], ALU.pow).then_inc(root2, 1)

            @block.vector
            def _(dve):
                step = Chain(dve, fin)
                for n in range(B * NT):
                    last = dve.bn_stats(stats[:, n, :], x_enc[:, n, :])
                step(last)
                for n in range(B * NT):
                    last = dve.bn_aggr(moments[:, n, :], stats[:, n, :])
                step(last)
                dve.tensor_scalar(var_eps[:], moments[:, :, 1], EPS, None, ALU.add).then_inc(root2, 1)
                dve.wait_ge(root2, 2)
                for n in range(B * NT):
                    last = dve.tensor_scalar(x_enc[:, n, :], x_enc[:, n, :], moments[:, n, 0:1], rstd[:, n:n + 1], ALU.subtract, ALU.mult)
                step(last)
                wide = [P, B * NT, D]
                step(dve.tensor_tensor(x_enc[:], x_enc[:], lnf_s[:].unsqueeze(1).to_broadcast(wide), ALU.mult))
                step(dve.tensor_tensor(x_enc[:], x_enc[:], lnf_b[:].unsqueeze(1).to_broadcast(wide), ALU.add))
                dve.wait_ge(tanh_done, 1)
                step(dve.scalar_tensor_tensor(x_loc[:], silu, 1.0, x_loc[:], ALU.add, ALU.mult))
                step(dve.tensor_tensor(x_loc[:], x_loc[:], x_enc[:], ALU.mult))
                step(dve.scalar_tensor_tensor(x_in[:], x_loc[:], 0.5, x_in[:], ALU.mult, ALU.add))

            @block.sync
            def _(sync):
                sync.wait_ge(fin, 8)
                sync.dma_start(out.rearrange("b (t p) d -> p (b t) d", p=P), x_in[:]).then_inc(stored, 16)
                sync.wait_ge(stored, 16)


ENC_W, LOC_W = 4 * D + 2 * FF, 3 * INNER + NB * D + 2 * HID + len(HBLK) * D
ATTN0 = ("Wq", "Wk", "Wv", "Wf1", "Wf2", "Wg1", "Wg2", "Wo", "norm_w")
ATTN1 = ("Wq", "bq", "Wk", "bk", "Wv", "bv", "Wo", "bo", "W1", "b1", "W2", "b2", "ln1_s", "ln1_b", "ln2_s", "ln2_b", "lnf_s", "lnf_b")
FFN1 = ("wqkv", "q_scale", "k_scale", "wo", "ln_g", "ln_b", "w1", "b1", "w2", "b2")


def build(nc, x, w0, attn1, ffn1, tables0, tables1, x1, out):
    with ExitStack() as ctx:
        psum = [ctx.enter_context(nc.psum_tensor(f"bank{i}", [P, 512], F32)) for i in range(8)]
        layer0(nc, x, x1, w0, tables0, psum)
        layer1(nc, x1, out, attn1, ffn1, tables1, psum)


def lay_out_experts(a):
    gate = np.concatenate([a["L0_ffn_w_gate"], a["L0_ffn_shared_gate_w"][None]])
    up = np.concatenate([a["L0_ffn_w_up"], a["L0_ffn_shared_up_w"][None]])
    down = np.concatenate([a["L0_ffn_w_down"], a["L0_ffn_shared_down_w"][None]])
    return {"w_in": np.stack([gate, up], axis=1).transpose(3, 0, 1, 2),
            "w_down": down.transpose(2, 0, 1),
            "gate_w": a["L0_ffn_gate_w"].T, "expert_bias": a["L0_ffn_expert_bias"]}


def lay_out_layer1(a):
    e = {k: a[f"L1_attn_{k}"] for k in ATTN1}
    f = {k: a[f"L1_ffn_{k}"] for k in FFN1}
    step = LA // LF
    rows = lambda m: m.reshape(LA, -1, P, m.shape[-1]).transpose(0, 2, 1, 3).reshape(LA, P, -1)
    w = np.concatenate([e["Wq"], e["Wk"], e["Wv"], e["Wo"], e["W1"], rows(e["W2"])], axis=-1)
    col = np.concatenate([np.stack([e[k] for k in ("bq", "ln1_s", "ln2_s", "ln1_b", "ln2_b")], axis=-1),
                          e["b1"].reshape(LA, NB, P).transpose(0, 2, 1)], axis=-1)
    row = np.stack([e[k] for k in ("bk", "bv", "bo", "b2")], axis=1)
    enc = {"w": w.reshape(LF, step, P, -1).transpose(0, 2, 1, 3), "col": col.reshape(LF, step, P, -1).transpose(0, 2, 1, 3),
           "row": row.reshape(LF, step, 4, D), "lnf_s": e["lnf_s"], "lnf_b": e["lnf_b"]}
    pad = len(HBLK) * P - HID
    filled = lambda m, axis: np.concatenate([m, np.zeros([pad if n == axis else s for n, s in enumerate(m.shape)], m.dtype)], axis=axis)
    w = np.concatenate([f["wqkv"], f["wo"].reshape(LF, NB, P, D).transpose(0, 2, 1, 3).reshape(LF, P, -1), f["w1"],
                        filled(f["w2"], 1).reshape(LF, len(HBLK), P, D).transpose(0, 2, 1, 3).reshape(LF, P, -1)], axis=-1)
    b1 = filled(f["b1"].reshape(LF, 2, HID), 2).reshape(LF, 2 * len(HBLK), P).transpose(0, 2, 1)
    swap = lambda m: np.concatenate([m[:, FDH // 2:], m[:, :FDH // 2]], axis=-1)
    loc = {"w": w, "col": np.concatenate([f["ln_g"][..., None], f["ln_b"][..., None], b1], axis=-1),
           "row": np.concatenate([f["b2"], f["q_scale"], swap(f["q_scale"]), f["k_scale"], swap(f["k_scale"])], axis=-1)}
    return enc, loc


def kernel(**inputs):
    import concourse.bacc as bacc
    from concourse.bass_utils import run_bass_kernel_spmd
    nc = bacc.Bacc("TRN2", target_bir_lowering=False, num_devices=1)
    arrays = {}

    def dram(name, a):
        arrays[name] = np.ascontiguousarray(a)
        return nc.dram_tensor(name, arrays[name].shape, F32, kind="ExternalInput").ap()

    x = np.asarray(inputs["L0_attn_x"]).reshape(B, GC, NT, 2, CH, D).transpose(3, 1, 4, 0, 2, 5).reshape(P, B * NT, D)
    x = dram("L0_attn_x", x)
    w0 = {k: dram(f"L0_attn_{k}", inputs[f"L0_attn_{k}"]) for k in ATTN0}
    w0.update({k: dram(f"L0_ffn_{k}", v) for k, v in lay_out_experts({k: np.asarray(v) for k, v in inputs.items()}).items()})
    enc, loc = lay_out_layer1({k: np.asarray(v) for k, v in inputs.items()})
    attn1 = {k: dram(f"L1_attn_{k}", v) for k, v in enc.items()}
    ffn1 = {k: dram(f"L1_ffn_{k}", v) for k, v in loc.items()}
    tables = []
    for name, constants in (("tables0", shape_constants()), ("tables1", layer1_constants())):
        side_by_side, names, widths = packed(constants)
        tables.append((dram(name, side_by_side), widths, names))
    x1 = nc.dram_tensor("x1", (B, T, D), F32, kind="Internal").ap()
    out = nc.dram_tensor("out", (B, T, D), F32, kind="ExternalOutput").ap()
    build(nc, x, w0, attn1, ffn1, tables[0], tables[1], x1, out)
    r = run_bass_kernel_spmd(nc, [arrays], core_ids=[0])
    return r.results[0]["out"]
```
